# Optimizing a Trainium2 kernel written in Bass

```python
import numpy as np
import jax
import jax.numpy as jnp

def _softmax(x, axis=-1):
    return jax.nn.softmax(x, axis=axis)

def _gelu(x):
    return jax.nn.gelu(x, approximate=True)

def _silu(x):
    return jax.nn.silu(x)

def _sigmoid(x):
    return jax.nn.sigmoid(x)

def _layernorm(x, axis=-1, eps=1e-05):
    m = jnp.mean(x, axis=axis, keepdims=True)
    v = jnp.var(x, axis=axis, keepdims=True)
    return (x - m) / jnp.sqrt(v + eps)

def _scatter_add(tgt, idx, src, axis=0):
    return tgt.at[idx].add(src)

def _segment_sum(src, seg, n):
    return jax.ops.segment_sum(src, seg, n)
kernel_name = 'mk_decoder_postln_d1_seqx_r4_f066ce'

def setup_inputs(seed: int=0):
    np.random.seed(seed)
    _w = jnp.asarray

    def _rec_inputs():
        import jax
        import jax.numpy as jnp
        _rk = jax.random.key(seed)
        x = -0.0002928 + 1 * jax.random.normal(jax.random.fold_in(_rk, 1), (8, 512, 256), jnp.float32)
        _lenS = 512 - jax.random.randint(jax.random.fold_in(_rk, 7), (8,), 0, max(1, 512 // 4) + 1, jnp.int32)
        _lenS2 = 512 - jax.random.randint(jax.random.fold_in(_rk, 8), (8,), 0, max(1, 512 // 4) + 1, jnp.int32)
        _ctx_1024P = jax.random.normal(jax.random.fold_in(_rk, 11), (8, 16, 256), jnp.float32)
        _ctx_1024c = jax.random.dirichlet(jax.random.fold_in(_rk, 511), 0.3 * jnp.ones((16,), jnp.float32), (8, 512))
        _ctx_1024t = jnp.einsum('bsk,bkd->bsd', _ctx_1024c, _ctx_1024P)
        _ctx_1024t = _ctx_1024t * jax.lax.rsqrt(jnp.mean(jnp.square(_ctx_1024t)) + 1e-12) * 0.953939
        ctx_1024 = -1.39393e-06 + 0.999914 * (_ctx_1024t + 0.3 * jax.random.normal(jax.random.fold_in(_rk, 611), (8, 512, 256), jnp.float32))
        return (x, ctx_1024)
    x, ctx_1024 = _rec_inputs()

    def _L0_attn_setup():
        import jax, jax.numpy as jnp
        import numpy as np
        DIM = 256
        HEADS = 16
        HEAD_DIM = DIM // HEADS
        B, N = (4, 1024)
        key = jax.random.key(seed)
        ks = jax.random.split(key, 9)
        s = 1.0 / np.sqrt(DIM)
        return {'x': jax.random.normal(ks[0], (B, N, DIM), dtype=jnp.float32), 'Wq': jax.random.uniform(ks[1], (DIM, DIM), jnp.float32, -s, s), 'bq': jax.random.uniform(ks[2], (DIM,), jnp.float32, -s, s), 'Wk': jax.random.uniform(ks[3], (DIM, DIM), jnp.float32, -s, s), 'bk': jax.random.uniform(ks[4], (DIM,), jnp.float32, -s, s), 'Wv': jax.random.uniform(ks[5], (DIM, DIM), jnp.float32, -s, s), 'bv': jax.random.uniform(ks[6], (DIM,), jnp.float32, -s, s), 'Wp': jax.random.uniform(ks[7], (DIM, DIM), jnp.float32, -s, s), 'bp': jax.random.uniform(ks[8], (DIM,), jnp.float32, -s, s)}
    _L0_attn_all = _L0_attn_setup()
    _L0_attn_in = {k: v for k, v in _L0_attn_all.items() if k in ('Wq', 'bq', 'Wk', 'bk', 'Wv', 'bv', 'Wp', 'bp')}
    del _L0_attn_all

    def _L0_xattn_setup():
        import jax, jax.numpy as jnp
        import numpy as np
        B, S, M, H, D = (2, 512, 256, 16, 64)
        IGNORE = -1000.0

        def fp8_round(x):
            return x.astype(jnp.float8_e4m3fn).astype(jnp.float32)
        key = jax.random.key(seed)
        ks = jax.random.split(key, 7)
        w_scale = jnp.float32(0.02)
        return {'query_input': jax.random.normal(ks[0], (B, S, M), jnp.float32), 'key_input': jax.random.normal(ks[1], (B, S, M), jnp.float32), 'value_input': jax.random.normal(ks[2], (B, S, M), jnp.float32), 'W_Q': jax.random.normal(ks[3], (H, M, D), jnp.float32) * w_scale, 'W_K': jax.random.normal(ks[4], (H, M, D), jnp.float32) * w_scale, 'W_V': jax.random.normal(ks[5], (H, M, D), jnp.float32) * w_scale, 'W_O': jax.random.normal(ks[6], (H, D, M), jnp.float32) * w_scale, 'b_Q': jnp.zeros((H, D), jnp.float32), 'b_K': jnp.zeros((H, D), jnp.float32), 'b_V': jnp.zeros((H, D), jnp.float32), 'b_O': jnp.zeros((M,), jnp.float32)}
    _L0_xattn_all = _L0_xattn_setup()
    _L0_xattn_in = {k: v for k, v in _L0_xattn_all.items() if k in ('W_Q', 'W_K', 'W_V', 'W_O', 'b_Q', 'b_K', 'b_V', 'b_O')}
    del _L0_xattn_all

    def _L0_ffn_setup():
        import jax, jax.numpy as jnp
        import numpy as np
        B, S, H, DFF, E, K = (2, 512, 256, 512, 8, 2)

        def _moe(x, Wg, W1, b1, W2, b2, W3, b3):
            Bm, Sm, Hm = x.shape
            xt = x.reshape(-1, Hm)
            gout = xt @ Wg.T
            topv, topi = jax.lax.top_k(gout, K)
            w = jax.nn.softmax(topv, axis=-1)
            comb = jnp.einsum('tke,tk->te', jax.nn.one_hot(topi, E, dtype=x.dtype), w)
            g = jnp.einsum('th,efh->etf', xt, W1) + b1[:, None, :]
            v = jnp.einsum('th,efh->etf', xt, W2) + b2[:, None, :]
            h = jax.nn.silu(g) * v
            eo = jnp.einsum('etf,ehf->eth', h, W3) + b3[:, None, :]
            out = jnp.einsum('eth,te->th', eo, comb)
            return out.reshape(Bm, Sm, Hm)
        key = jax.random.key(seed)
        ks = jax.random.split(key, 8)
        sc_h = 1.0 / np.sqrt(H)
        sc_f = 1.0 / np.sqrt(DFF)
        x = jax.random.normal(ks[0], (B, S, H), dtype=jnp.float32)
        Wg = jax.random.uniform(ks[1], (E, H), jnp.float32, -sc_h, sc_h)
        W1 = jax.random.uniform(ks[2], (E, DFF, H), jnp.float32, -sc_h, sc_h)
        b1 = jax.random.uniform(ks[3], (E, DFF), jnp.float32, -sc_h, sc_h)
        W2 = jax.random.uniform(ks[4], (E, DFF, H), jnp.float32, -sc_h, sc_h)
        b2 = jax.random.uniform(ks[5], (E, DFF), jnp.float32, -sc_h, sc_h)
        W3 = jax.random.uniform(ks[6], (E, H, DFF), jnp.float32, -sc_f, sc_f)
        b3 = jax.random.uniform(ks[7], (E, H), jnp.float32, -sc_f, sc_f)
        return {'x': x, 'Wg': Wg, 'W1': W1, 'b1': b1, 'W2': W2, 'b2': b2, 'W3': W3, 'b3': b3}
    _L0_ffn_all = _L0_ffn_setup()
    _L0_ffn_in = {k: v for k, v in _L0_ffn_all.items() if k in ('Wg', 'W1', 'b1', 'W2', 'b2', 'W3', 'b3')}
    del _L0_ffn_all
    return {'x': x, 'ctx_1024': ctx_1024, 'L0_attn_Wq': _L0_attn_in['Wq'], 'L0_attn_bq': _L0_attn_in['bq'], 'L0_attn_Wk': _L0_attn_in['Wk'], 'L0_attn_bk': _L0_attn_in['bk'], 'L0_attn_Wv': _L0_attn_in['Wv'], 'L0_attn_bv': _L0_attn_in['bv'], 'L0_attn_Wp': _L0_attn_in['Wp'], 'L0_attn_bp': _L0_attn_in['bp'], 'L0_xattn_W_Q': _L0_xattn_in['W_Q'], 'L0_xattn_W_K': _L0_xattn_in['W_K'], 'L0_xattn_W_V': _L0_xattn_in['W_V'], 'L0_xattn_W_O': _L0_xattn_in['W_O'], 'L0_xattn_b_Q': _L0_xattn_in['b_Q'], 'L0_xattn_b_K': _L0_xattn_in['b_K'], 'L0_xattn_b_V': _L0_xattn_in['b_V'], 'L0_xattn_b_O': _L0_xattn_in['b_O'], 'L0_ffn_Wg': _L0_ffn_in['Wg'], 'L0_ffn_W1': _L0_ffn_in['W1'], 'L0_ffn_b1': _L0_ffn_in['b1'], 'L0_ffn_W2': _L0_ffn_in['W2'], 'L0_ffn_b2': _L0_ffn_in['b2'], 'L0_ffn_W3': _L0_ffn_in['W3'], 'L0_ffn_b3': _L0_ffn_in['b3']}

def reference(x, ctx_1024, L0_attn_Wq, L0_attn_bq, L0_attn_Wk, L0_attn_bk, L0_attn_Wv, L0_attn_bv, L0_attn_Wp, L0_attn_bp, L0_xattn_W_Q, L0_xattn_W_K, L0_xattn_W_V, L0_xattn_W_O, L0_xattn_b_Q, L0_xattn_b_K, L0_xattn_b_V, L0_xattn_b_O, L0_ffn_Wg, L0_ffn_W1, L0_ffn_b1, L0_ffn_W2, L0_ffn_b2, L0_ffn_W3, L0_ffn_b3):
    import jax
    import jax.numpy as jnp

    def _L0_attn_ref(x, Wq, bq, Wk, bk, Wv, bv, Wp, bp):
        import jax, jax.numpy as jnp
        import numpy as np
        DIM = 256
        HEADS = 16
        HEAD_DIM = DIM // HEADS
        B, N = (4, 1024)
        b, n, d = x.shape
        q = x @ Wq + bq
        k = x @ Wk + bk
        v = x @ Wv + bv
        split = lambda t: t.reshape(b, n, HEADS, HEAD_DIM).transpose(0, 2, 1, 3)
        q, k, v = (split(q), split(k), split(v))
        q = jax.nn.elu(q) + 1.0
        k = jax.nn.elu(k) + 1.0
        kv = jnp.einsum('bhnd,bhnf->bhdf', k, v)
        out = jnp.einsum('bhnd,bhdf->bhnf', q, kv)
        out = out.transpose(0, 2, 1, 3).reshape(b, n, d)
        return out @ Wp + bp

    def _L0_xattn_ref(query_input, key_input, value_input, W_Q, W_K, W_V, W_O, b_Q, b_K, b_V, b_O):
        import jax, jax.numpy as jnp
        import numpy as np
        B, S, M, H, D = (2, 512, 256, 16, 64)
        IGNORE = -1000.0

        def fp8_round(x):
            return x.astype(jnp.float8_e4m3fn).astype(jnp.float32)
        q = jnp.einsum('bpm,hmd->bphd', fp8_round(query_input), fp8_round(W_Q)) + b_Q
        k = jnp.einsum('bpm,hmd->bphd', fp8_round(key_input), fp8_round(W_K)) + b_K
        v = jnp.einsum('bpm,hmd->bphd', fp8_round(value_input), fp8_round(W_V)) + b_V
        attn_scale = jnp.float32(np.sqrt(D))
        scores = jnp.einsum('bqhd,bkhd->bhqk', q, k) / attn_scale
        causal = jnp.tril(jnp.ones((S, S), dtype=bool))
        scores = jnp.where(causal[None, None], scores, jnp.float32(IGNORE))
        pattern = jax.nn.softmax(scores, axis=-1)
        z = jnp.einsum('bkhd,bhqk->bqhd', v, pattern)
        out = jnp.einsum('bqhd,hdm->bqm', z, W_O) + b_O
        return out

    def _L0_ffn_ref(x, Wg, W1, b1, W2, b2, W3, b3):
        import jax, jax.numpy as jnp
        import numpy as np
        B, S, H, DFF, E, K = (2, 512, 256, 512, 8, 2)

        def _moe(x, Wg, W1, b1, W2, b2, W3, b3):
            Bm, Sm, Hm = x.shape
            xt = x.reshape(-1, Hm)
            gout = xt @ Wg.T
            topv, topi = jax.lax.top_k(gout, K)
            w = jax.nn.softmax(topv, axis=-1)
            comb = jnp.einsum('tke,tk->te', jax.nn.one_hot(topi, E, dtype=x.dtype), w)
            g = jnp.einsum('th,efh->etf', xt, W1) + b1[:, None, :]
            v = jnp.einsum('th,efh->etf', xt, W2) + b2[:, None, :]
            h = jax.nn.silu(g) * v
            eo = jnp.einsum('etf,ehf->eth', h, W3) + b3[:, None, :]
            out = jnp.einsum('eth,te->th', eo, comb)
            return out.reshape(Bm, Sm, Hm)
        return _moe(x, Wg, W1, b1, W2, b2, W3, b3)
    x = _layernorm(x + _L0_attn_ref(x, L0_attn_Wq, L0_attn_bq, L0_attn_Wk, L0_attn_bk, L0_attn_Wv, L0_attn_bv, L0_attn_Wp, L0_attn_bp), axis=-1)
    x = _layernorm(x + _L0_xattn_ref(x, ctx_1024, ctx_1024, L0_xattn_W_Q, L0_xattn_W_K, L0_xattn_W_V, L0_xattn_W_O, L0_xattn_b_Q, L0_xattn_b_K, L0_xattn_b_V, L0_xattn_b_O), axis=-1)
    x = _layernorm(x + _L0_ffn_ref(x, L0_ffn_Wg, L0_ffn_W1, L0_ffn_b1, L0_ffn_W2, L0_ffn_b2, L0_ffn_W3, L0_ffn_b3), axis=-1)
    return x

_drawn_inputs = setup_inputs


def setup_inputs(seed=0):
    import zlib

    import numpy as np

    out = dict(_drawn_inputs(seed))
    spreads = {'L0_xattn_b_Q': (0.0, 0.8),
     'L0_xattn_b_K': (0.0, 2.0),
     'L0_xattn_b_V': (0.0, 0.1),
     'L0_xattn_b_O': (0.0, 0.1)}
    factors = {'L0_attn_bq': 7.536,
     'L0_attn_bk': 8.0,
     'L0_attn_bp': 200.0,
     'L0_xattn_W_Q': 8.0,
     'L0_xattn_W_K': 8.0,
     'L0_ffn_b1': 8.0,
     'L0_ffn_b2': 8.0,
     'L0_ffn_b3': 3.123}
    for name, (base, spread) in spreads.items():
        noise = np.random.default_rng([zlib.crc32(name.encode()), seed]).standard_normal(out[name].shape)
        drawn = base * np.exp(spread * noise) if base else spread * noise
        out[name] = jnp.asarray(drawn.astype(out[name].dtype))
    for name, factor in factors.items():
        out[name] = (out[name] * factor).astype(out[name].dtype)
    return out
```

```python
from contextlib import ExitStack

import numpy as np

import concourse.bass as bass
from concourse import mybir

F32 = mybir.dt.float32
BF16 = mybir.dt.bfloat16
FP8 = mybir.dt.float8e4
U32 = mybir.dt.uint32
I32 = mybir.dt.int32
ALU = mybir.AluOpType
ACT = mybir.ActivationFunctionType
AX_X = mybir.AxisListType.X

P = 128
NB, SEQ, DIM = 8, 512, 256
TOK = NB * SEQ
TT = SEQ // P
DC = DIM // P
LIN_D = 16
HEADS, HD = 16, 64
PAIRS = HEADS // 2
INNER = HEADS * HD
STEPS = PAIRS * TT
NE, FF, TOPK = 8, 512, 2
FC = FF // P
ROWTILES = TOK // P
MOE_TILES = TOK * TOPK // P + NE - 1
LIST_COLS = MOE_TILES + 2
DUMP = TOK * TOPK
EPS = 1e-5
FAR = 1e30

C_IDENT, C_CAUSAL, C_TRI, C_BLOCK, C_IOTA, C_LANE = 0, P, 2 * P, 3 * P, 4 * P, 5 * P
C_COLS = 5 * P + 8


def constants():
    r, c = np.arange(P)[:, None], np.arange(P)[None, :]
    t = np.zeros((P, C_COLS), np.float32)
    t[:, C_IDENT:C_IDENT + P] = r == c
    t[:, C_CAUSAL:C_CAUSAL + P] = np.where(c > r, FAR, 0.0)
    t[:, C_TRI:C_TRI + P] = r < c
    t[:, C_BLOCK:C_BLOCK + P] = r // LIN_D == c // LIN_D
    t[:, C_IOTA:C_IOTA + P] = c
    t[:, C_LANE] = np.arange(P)
    t[:, C_LANE + 1] = DUMP + 1 + np.arange(P)
    t[:, C_LANE + 2] = 2 * np.arange(P) + 1
    t[:, C_LANE + 3] = 2 * np.arange(P) + 2
    t[:, C_LANE + 4] = -0.5
    t[:, C_LANE + 5] = -0.5
    t[:, C_LANE + 6] = -0.5
    t[:, C_LANE + 7] = -0.5
    return t


def at(i, per, k):
    return i * per + k


def decoder_kernel(nc, x, xT, cT, Wq, Wk, Wv, Wp, bq, bk, bv, bp, WQ, WK, WV, WO, bQ, bK, bV, bO,
                   WgT, W1T, b1, W2T, b2, W3T, b3, consts, out):
    x2_d = nc.dram_tensor("x2_rows", (TOK, DIM), F32, kind="Internal").ap()
    y_d = nc.dram_tensor("expert_rows", (DUMP + P, DIM), F32, kind="Internal").ap()

    with ExitStack() as ctx:
        def sb(name, shape, dt=F32):
            return ctx.enter_context(nc.sbuf_tensor(name, shape, dt))

        def sem(name):
            return ctx.enter_context(nc.semaphore(name))

        PS = ctx.enter_context(nc.psum_tensor("PS", [P, 8, 512], F32))

        cst = sb("cst", [P, C_COLS])
        ident = cst[:, C_IDENT:C_IDENT + P]
        ident_b = sb("ident_b", [P, P], BF16)
        causal_b = sb("causal_b", [P, P], BF16)
        tri_b = sb("tri_b", [P, P], BF16)
        ones_b = sb("ones_b", [P, P], BF16)
        logits = sb("logits", [P, ROWTILES, NE])
        gates = sb("gates", [P, TOPK, ROWTILES])
        w1_sb = sb("w1_sb", [P, NE * DC * FF])
        ARENA = 40 * 1024
        arena = sb("arena", [P, ARENA])
        used = [0, 0]

        def view(stage, *shape, dt=F32):
            n = int(np.prod(shape)) * (4 if dt in (F32, U32, I32) else 2 if dt == BF16 else 1) // 4
            a = used[stage]
            used[stage] += n
            assert used[stage] <= ARENA, used
            v = arena[:, a:a + n]
            if dt != F32:
                v = v.bitcast(dt)
            if len(shape) > 1:
                names = "abc"[:len(shape)]
                v = v.rearrange(f"p ({' '.join(names)}) -> p {' '.join(names)}",
                                **dict(zip(names[1:], shape[1:])))
            return v

        wq, wk, wv, wp = (view(0, DC, DIM) for _ in range(4))
        wQ, wK, wV = (view(0, DC, INNER, dt=BF16) for _ in range(3))
        wO = view(0, PAIRS, DIM)
        wg = view(0, DC, NE)
        bq_c = view(0, DC)
        bQ_c, bK_c, nbQ = view(0, PAIRS), view(0, PAIRS), view(0, PAIRS)
        bkv_b = view(0, 2 * DIM)
        bp_b, bO_b = view(0, DIM), view(0, DIM)
        bV_b = view(0, INNER)
        xT_s, cT_s = view(0, DC, SEQ), view(0, DC, SEQ)
        xr_s = view(0, TT, DIM)
        k_s, q_s = view(0, TT, DIM), view(0, DC, SEQ)
        bd_s, m_s = view(0, DC, P), view(0, DC, DIM)
        cq_s = view(0, DC, SEQ, dt=BF16)
        res_s, pre_s, x1_s = view(0, TT, DIM), view(0, TT, DIM), view(0, TT, DIM)
        x2_s = view(0, TT, DIM)
        x1q_s = view(0, TT, DIM, dt=FP8)
        x1qT_s = view(0, DC, SEQ, dt=BF16)
        stats, mv, rstd = view(0, TT, 8), view(0, TT, 2), view(0, TT)
        QT, KT = view(0, 2, SEQ), view(0, 2, SEQ)
        V_s = view(0, 2, TT, P)
        ZT = view(0, PAIRS, SEQ)
        prob, pnorm = view(0, 2, 2, SEQ), view(0, 2, 2, SEQ)
        smin, ssum, sinv = view(0, 2, 2), view(0, 2, 2), view(0, 2, 2)
        PT = [view(0, TT, SEQ) for _ in range(4)]
        used[0] -= 4 * TT * SEQ
        kv_s = view(0, TT, 2 * DIM)
        ek_s, rk_s = view(0, TT, DIM), view(0, TT, DIM)
        eq_s, rq_s = view(0, DC, SEQ), view(0, DC, SEQ)
        qe_s, qm_s = view(0, DC, SEQ), view(0, DC, SEQ)
        x2T_s = rk_s.rearrange("p a b -> p (a b)").rearrange("p (a b) -> p a b", a=DC)
        stage_w = [prob.rearrange("p a b c -> p (a b c)"), pnorm.rearrange("p a b c -> p (a b c)")]

        w2_sb = view(1, NE * DC * FF)
        w3_sb = view(1, NE * FC * DIM)
        b1_b, b2_b, b3_b = view(1, NE * FF), view(1, NE * FF), view(1, NE * DIM)
        mark = used[1]
        top = view(1, ROWTILES, NE)
        topi = view(1, ROWTILES, NE, dt=U32)
        choice = view(1, TOPK, ROWTILES)
        onehot = view(1, TOPK, ROWTILES * NE)
        both_b = view(1, ROWTILES * NE, dt=BF16)
        run_a, run_b = view(1, ROWTILES, NE), view(1, ROWTILES, NE)
        before = view(1, ROWTILES, NE)
        etiles, etiles_i = view(1, NE), view(1, NE, dt=I32)
        cum_a, cum_b = view(1, NE), view(1, NE)
        slot = view(1, TOPK, ROWTILES)
        slot_i, tile_i, lane_i = (view(1, TOPK * ROWTILES, dt=I32) for _ in range(3))
        tile_f, lane_f = view(1, TOPK * ROWTILES), view(1, TOPK * ROWTILES)
        lane_hot = view(1, 2, P, dt=BF16)
        code_hot = view(1, 2, 2 * LIST_COLS, dt=BF16)
        hi_s, code, empty = view(1, LIST_COLS), view(1, LIST_COLS), view(1, LIST_COLS)
        past = view(1, LIST_COLS, NE)
        expert_f = view(1, LIST_COLS)
        expert = sb("expert", [P, LIST_COLS], I32)
        gather_l = sb("gather_l", [P, LIST_COLS], U32)
        scatter_l = sb("scatter_l", [P, LIST_COLS], U32)
        code_i = view(1, LIST_COLS, dt=I32)
        used[1] = mark
        xg = sb("xg", [P, 2, DIM])
        g_idx, s_idx = sb("g_idx", [P, 2], U32), sb("s_idx", [P, 2], U32)
        xgT = sb("xgT", [P, 2, DIM])
        g_s, v_s = view(1, 2, FF), view(1, 2, FF)
        silu_s, h_s = view(1, 2, FF), view(1, 2, FF)
        hT_s = view(1, FF)
        yo = view(1, 2, DIM)
        used[1] = 0
        yy = view(1, 2, TT, TOPK * DIM)
        xx, zz, oo = view(1, 2, TT, DIM), view(1, 2, TT, DIM), view(1, 2, TT, DIM)
        stats4, mv4, rstd4 = view(1, TT, 8), view(1, TT, 2), view(1, TT)

        s_const, s_wlin, s_wo = sem("const_in"), sem("lin_weights_in"), sem("wo_in")
        s_wraw = [sem(f"raw_weights_in{q}") for q in range(4)]
        s_w1, s_w23 = sem("w1_in"), sem("w23_in")
        s_cb, s_wexp, s_wmag, s_wadd, s_wcvt = sem("consts_bf16"), sem("w_exponents"), sem("w_magic"), sem("w_added"), sem("w_rounded")
        s_xT, s_xr, s_cT, s_x2out = sem("xT_in"), sem("x_rows_in"), sem("ctx_in"), sem("x2_out")
        p_q, p_kv, p_bd, p_m, p_y1 = sem("q_mm"), sem("kv_mm"), sem("kTv_mm"), sem("kTvW_mm"), sem("lin_out_mm")
        p_xt, p_proj, p_s, p_t, p_z = sem("x1qT_mm"), sem("proj_mm"), sem("score_mm"), sem("probT_mm"), sem("z_mm")
        p_y2, p_x2t, p_lg = sem("attn_out_mm"), sem("x2T_mm"), sem("logit_mm")
        a_q, a_k, a_m, a_xt, a_kq = sem("q_exp_relu"), sem("k_exp_relu"), sem("kTvW_sb"), sem("x1qT_sb"), sem("KQ_sb")
        a_e, a_t, a_x2t = sem("exp_done"), sem("probT0_sb"), sem("x2T_sb")
        d_kv, d_kf, d_bd, d_qf = sem("kv_bias"), sem("k_feat"), sem("kTv_sb"), sem("q_feat")
        d_ce, d_cm = sem("ctx_exponents"), sem("ctx_magic")
        d_pre, d_st, d_mv, d_x1, d_xq = sem("pre_ln"), sem("ln_stats"), sem("ln_mean_var"), sem("x1_rows"), sem("x1q_rows")
        d_min, d_inv, d_t, d_v, d_z, d_x2, d_lg = sem("row_min"), sem("row_inv"), sem("probT1_sb"), sem("V_sb"), sem("Z_sb"), sem("x2_rows_sb"), sem("logits_sb")
        g_ca, g_cq, g_res, g_ve, g_rs, g_n, g_res2 = sem("ctx_added"), sem("ctx_rounded"), sem("x_plus_bias"), sem("var_eps"), sem("rstd"), sem("prob_normed"), sem("x1_plus_bias")
        r_d, r_e, r_pre, r_hot, r_list, r_tab = sem("route_dve"), sem("route_exp"), sem("prefix_mm"), sem("hot_ready"), sem("list_mm"), sem("tables_ready")
        m_gi, m_si = sem("gather_idx"), sem("scatter_idx")
        m_in, m_out = [sem(f"tokens_in{h}") for h in range(2)], [sem(f"rows_out{h}") for h in range(2)]
        c_in, s_out = [sem(f"mix_in{h}") for h in range(2)], [sem(f"out_stored{h}") for h in range(2)]
        m_xt, m_xs, m_g, m_v, m_ht, m_o = sem("xgT_mm"), sem("xgT_sb"), sem("g_mm"), sem("v_mm"), sem("hT_mm"), sem("o_mm")
        m_gb, m_vb, m_si_, m_h, m_hs, m_yo = sem("g_bias"), sem("v_bias"), sem("silu"), sem("h_sb"), sem("hT_sb"), sem("yo_sb")
        c_mix, c_pre, c_st, c_mv, c_ve, c_rs, c_o = sem("mix_half"), sem("mix_pre"), sem("mix_stats"), sem("mix_mv"), sem("mix_ve"), sem("mix_rstd"), sem("mix_out")

        s_passed = sem("waits_passed")

        def wait_alone(eng, semaphore, value):
            eng.wait_ge(semaphore, value)
            eng.sem_inc(s_passed, 1)

        def tile(u, k):
            return u * 2 + k, u + k // 2, k % 2

        block = ctx.enter_context(nc.Block())
        ds = bass.ds
        N_WRAW = 12
        raw_w = [(w, wt, k, n) for w, wt in ((WQ, wQ), (WK, wK), (WV, wV)) for k in range(DC) for n in range(2)]

        @block.sync
        def _(sp):
            sp.dma_start(cst[:, :], consts).then_inc(s_const, 16)

            def load_batch(i):
                sp.dma_start(xT_s, xT[:, ds(i * SEQ, SEQ)].rearrange("(c p) t -> p c t", p=P)).then_inc(s_xT, 16)
                sp.dma_start(cT_s, cT[:, ds(i * SEQ, SEQ)].rearrange("(c p) t -> p c t", p=P)).then_inc(s_cT, 16)
                sp.dma_start(xr_s, x[ds(i * SEQ, SEQ), :].rearrange("(a p) d -> p a d", p=P)).then_inc(s_xr, 16)

            for w, dst in ((Wq, wq), (Wk, wk), (Wv, wv), (Wp, wp)):
                sp.dma_start(dst, w.rearrange("(c p) n -> p c n", p=P)).then_inc(s_wlin, 16)
            sp.dma_start(bq_c, bq.rearrange("(c p) -> p c", p=P), allow_slow_non_contiguous=True).then_inc(s_wlin, 16)
            sp.dma_start(bkv_b[:, 0:DIM], bk.partition_broadcast(P)).then_inc(s_wlin, 16)
            sp.dma_start(bkv_b[:, DIM:2 * DIM], bv.partition_broadcast(P)).then_inc(s_wlin, 16)
            sp.dma_start(bp_b, bp.partition_broadcast(P)).then_inc(s_wlin, 16)
            load_batch(0)
            for n, (w, _, k, c) in enumerate(raw_w):
                if n >= 4:
                    sp.wait_ge(s_wcvt, n - 3)
                sp.dma_start(stage_w[0][:, (n % 4) * 512:(n % 4) * 512 + 512],
                             w[k * P:(k + 1) * P, c * 512:(c + 1) * 512]).then_inc(s_wraw[n % 4], 16)
            sp.dma_start(wO, WO.rearrange("(c p) n -> p c n", p=P)).then_inc(s_wo, 16)
            sp.dma_start(wg, WgT.rearrange("(c p) n -> p c n", p=P)).then_inc(s_wo, 16)
            sp.dma_start(bQ_c, bQ.rearrange("(c p) -> p c", p=P), allow_slow_non_contiguous=True).then_inc(s_wo, 16)
            sp.dma_start(bK_c, bK.rearrange("(c p) -> p c", p=P), allow_slow_non_contiguous=True).then_inc(s_wo, 16)
            sp.dma_start(bV_b, bV.partition_broadcast(P)).then_inc(s_wo, 16)
            sp.dma_start(bO_b, bO.partition_broadcast(P)).then_inc(s_wo, 16)
            sp.dma_start(w1_sb[:, :].rearrange("p (e c f) -> p e c f", e=NE, c=DC),
                         W1T.rearrange("e (c p) f -> p e c f", p=P)).then_inc(s_w1, 16)

            def store_x2(i):
                sp.wait_ge(d_x2, at(i, TT, TT))
                sp.dma_start(x2_d[ds(i * SEQ, SEQ), :].rearrange("(a p) d -> p a d", p=P), x2_s).then_inc(s_x2out, 16)

            sp.nop().then_inc(s_x2out, 16)
            with sp.Fori(1, NB) as i:
                sp.wait_ge(s_const, 16)
                sp.wait_ge(p_bd, i)
                sp.wait_ge(g_res, i)
                sp.wait_ge(g_ca, i)
                load_batch(i)
                store_x2(i - 1)
            store_x2(NB - 1)

            sp.wait_ge(d_lg, NB)
            sp.wait_ge(s_x2out, 16 * (NB + 1))
            sp.dma_start(w2_sb.rearrange("p (e c f) -> p e c f", e=NE, c=DC),
                         W2T.rearrange("e (c p) f -> p e c f", p=P)).then_inc(s_w23, 16)
            sp.dma_start(b1_b, b1.partition_broadcast(P)).then_inc(s_w23, 16)
            sp.dma_start(b2_b, b2.partition_broadcast(P)).then_inc(s_w23, 16)
            sp.dma_start(w3_sb.rearrange("p (e c f) -> p e c f", e=NE, c=FC),
                         W3T.rearrange("e (c p) f -> p e c f", p=P)).then_inc(s_w23, 16)
            sp.dma_start(b3_b, b3.partition_broadcast(P)).then_inc(s_w23, 16)

            sp.wait_ge(m_out[0], 16 * ((MOE_TILES + 1) // 2))
            sp.wait_ge(m_out[1], 16 * (MOE_TILES // 2))

            def load_mix(i, h):
                sp.dma_start(yy[:, h], y_d[ds(i * SEQ * TOPK, SEQ * TOPK), :]
                             .rearrange("(a p j) d -> p a (j d)", p=P, j=TOPK)).then_inc(c_in[h], 16)
                sp.dma_start(xx[:, h], x2_d[ds(i * SEQ, SEQ), :].rearrange("(a p) d -> p a d", p=P)).then_inc(c_in[h], 16)

            load_mix(0, 0)
            load_mix(1, 1)
            for i in range(NB):
                sp.wait_ge(c_o, TT * (i + 1))
                sp.dma_start(out[i * SEQ:(i + 1) * SEQ, :].rearrange("(a p) d -> p a d", p=P), oo[:, i % 2]).then_inc(s_out[i % 2], 16)
                if i + 2 < NB:
                    load_mix(i + 2, i % 2)
            sp.wait_ge(s_out[0], 16 * NB // 2)
            sp.wait_ge(s_out[1], 16 * NB // 2)

        @block.tensor
        def _(pe):
            mm = nc.tensor.matmul

            def linear_attention(i):
                pe.wait_ge(s_xT, at(i, 16, 16))
                for m in range(DC):
                    for k in range(DC):
                        last = mm(PS[:, m, :], wq[:, k, m * P:(m + 1) * P], xT_s[:, k, :], start=k == 0, stop=k == DC - 1)
                    last.then_inc(p_q, 1)
                for t in range(TT):
                    for n, w in enumerate((wk, wv)):
                        for k in range(DC):
                            last = mm(PS[:, 2 + t, n * DIM:(n + 1) * DIM], xT_s[:, k, t * P:(t + 1) * P], w[:, k, :],
                                      start=k == 0, stop=k == DC - 1)
                    last.then_inc(p_kv, 1)
                pe.wait_ge(d_kf, at(i, TT, TT))
                for g in range(DC):
                    for t in range(TT):
                        last = mm(PS[:, 6, g * P:(g + 1) * P], kv_s[:, t, DIM + g * P:DIM + (g + 1) * P],
                                  k_s[:, t, g * P:(g + 1) * P], start=t == 0, stop=t == TT - 1)
                last.then_inc(p_bd, 1)
                pe.wait_ge(d_bd, at(i, 1, 1))
                for g in range(DC):
                    last = mm(PS[:, 7, g * DIM:(g + 1) * DIM], bd_s[:, g, :], wp[:, g, :], start=True, stop=True)
                last.then_inc(p_m, 1)
                pe.wait_ge(a_m, at(i, 1, 1))
                pe.wait_ge(d_qf, at(i, 1, 1))
                for t in range(TT):
                    for g in range(DC):
                        last = mm(PS[:, t // 2, (t % 2) * DIM:(t % 2 + 1) * DIM], q_s[:, g, t * P:(t + 1) * P],
                                  m_s[:, g, :], start=g == 0, stop=g == DC - 1)
                    last.then_inc(p_y1, 1)
                wait_alone(pe, d_xq, at(i, TT, TT))
                for k in range(DC):
                    for t in range(TT):
                        last = mm(PS[:, 2 + k, t * P:(t + 1) * P], x1q_s[:, t, k * P:(k + 1) * P], ident_b[:, :],
                                  start=True, stop=True)
                last.then_inc(p_xt, 1)

            def proj_k(i, p):
                if p == 0:
                    pe.wait_ge(g_cq, at(i, 1, 1))
                else:
                    pe.wait_ge(d_v, at(i, PAIRS, p))
                for k in range(DC):
                    last = mm(PS[:, 7, :], wK[:, k, p * P:(p + 1) * P], cq_s[:, k, :], start=k == 0, stop=k == DC - 1)
                last.then_inc(p_proj, 1)

            def proj_q(i, p):
                pe.wait_ge(a_kq, at(i, 2 * PAIRS, 2 * p + 1))
                if p == 0:
                    pe.wait_ge(a_xt, at(i, 1, 1))
                for k in range(DC):
                    last = mm(PS[:, 7, :], wQ[:, k, p * P:(p + 1) * P], x1qT_s[:, k, :], start=k == 0, stop=k == DC - 1)
                last.then_inc(p_proj, 1)

            def proj_v(i, p):
                pe.wait_ge(a_kq, at(i, 2 * PAIRS, 2 * p + 2))
                for t in range(TT):
                    for k in range(DC):
                        last = mm(PS[:, 7, t * P:(t + 1) * P], cq_s[:, k, t * P:(t + 1) * P], wV[:, k, p * P:(p + 1) * P],
                                  start=k == 0, stop=k == DC - 1)
                last.then_inc(p_proj, 1)

            def scores(i, s):
                p, t = divmod(s, TT)
                n = (t + 1) * P
                if t == 0:
                    pe.wait_ge(a_kq, at(i, 2 * PAIRS, 2 * p + 2))
                if s >= 2:
                    pe.wait_ge(a_e, at(i, 2 * STEPS, 2 * (s - 1)))
                for e in range(2):
                    bank = 2 * (s % 2) + e
                    mm(PS[:, bank, 0:n], QT[e * HD:(e + 1) * HD, p % 2, t * P:(t + 1) * P], KT[e * HD:(e + 1) * HD, p % 2, 0:n],
                       start=True, stop=False)
                    last = mm(PS[:, bank, n - P:n], ident_b[:, :], causal_b[:, :], start=False, stop=True)
                last.then_inc(p_s, 1)

            def transposes(i, s):
                p, t = divmod(s, TT)
                pe.wait_ge(g_n, at(i, STEPS, s + 1))
                if s >= 1:
                    pe.wait_ge(a_t, at(i, STEPS, s))
                    pe.wait_ge(d_t, at(i, STEPS, s))
                for e in range(2):
                    for j in range(t + 1):
                        last = nc.tensor.transpose(PS[:, 4 + e, j * P:(j + 1) * P], pnorm[:, s % 2, e, j * P:(j + 1) * P], ident)
                last.then_inc(p_t, 1)

            def weighted(i, p):
                pe.wait_ge(a_t, at(i, STEPS, TT * (p + 1)))
                pe.wait_ge(d_t, at(i, STEPS, TT * (p + 1)))
                pe.wait_ge(d_v, at(i, PAIRS, p + 1))
                if p >= 1:
                    pe.wait_ge(d_z, at(i, PAIRS, p))
                for j in range(TT):
                    for e in range(2):
                        last = mm(PS[e * HD:(e + 1) * HD, 6, j * P:SEQ], V_s[:, p % 2, j, e * HD:(e + 1) * HD],
                                  PT[2 * (p % 2) + e][:, j, j * P:SEQ], start=j == 0, stop=j == TT - 1)
                last.then_inc(p_z, 1)

            def attention(i):
                proj_k(i, 0)
                proj_q(i, 0)
                proj_v(i, 0)
                scores(i, 0)
                scores(i, 1)
                for s in range(STEPS):
                    p, t = divmod(s, TT)
                    if s + 2 < STEPS:
                        scores(i, s + 2)
                    transposes(i, s)
                    if p + 1 < PAIRS and t < 3:
                        (proj_k, proj_q, proj_v)[t](i, p + 1)
                    if t == 0 and p >= 1:
                        weighted(i, p - 1)
                weighted(i, PAIRS - 1)

            def attention_output(i):
                pe.wait_ge(d_z, at(i, PAIRS, PAIRS))
                for t in range(TT):
                    for p in range(PAIRS):
                        last = mm(PS[:, t // 2, (t % 2) * DIM:(t % 2 + 1) * DIM], ZT[:, p, t * P:(t + 1) * P], wO[:, p, :],
                                  start=p == 0, stop=p == PAIRS - 1)
                    last.then_inc(p_y2, 1)
                pe.wait_ge(d_x2, at(i, TT, TT))
                for k in range(DC):
                    for t in range(TT):
                        last = nc.tensor.transpose(PS[:, 2 + k, t * P:(t + 1) * P], x2_s[:, t, k * P:(k + 1) * P], ident)
                last.then_inc(p_x2t, 1)
                pe.wait_ge(a_x2t, at(i, 1, 1))
                for t in range(TT):
                    for k in range(DC):
                        last = mm(PS[:, 4, t * NE:(t + 1) * NE], x2T_s[:, k, t * P:(t + 1) * P], wg[:, k, :],
                                  start=k == 0, stop=k == DC - 1)
                last.then_inc(p_lg, 1)
                pe.wait_ge(d_lg, at(i, 1, 1))

            pe.wait_ge(s_wlin, 16 * 8)
            pe.wait_ge(s_wo, 16 * 6)
            pe.wait_ge(s_const, 16)
            pe.wait_ge(s_cb, 4)
            pe.wait_ge(s_wcvt, N_WRAW)
            with pe.Fori(0, NB) as i:
                linear_attention(i)
                attention(i)
                attention_output(i)

            pe.wait_ge(r_hot, 1)
            mm(PS[:, 0, 0:ROWTILES * NE], tri_b[:, :], both_b, start=True, stop=True)
            mm(PS[:, 1, 0:ROWTILES * NE], ones_b[:, :], both_b, start=True, stop=True).then_inc(r_pre, 1)
            for n in range(ROWTILES * TOPK):
                pe.wait_ge(r_hot, n + 2)
                mm(PS[:, 2, 0:2 * LIST_COLS], lane_hot[:, n % 2, :], code_hot[:, n % 2, :],
                   start=n == 0, stop=n == ROWTILES * TOPK - 1).then_inc(r_list, 1)

            def expert_of(s):
                return pe.value_load(expert[0:1, ds(s, 1)], min_val=0, max_val=NE - 1)

            def tokensT(s, nth, h):
                pe.wait_ge(m_in[h], at(nth, 16, 16))
                for k in range(DC):
                    last = nc.tensor.transpose(PS[:, 0, k * P:(k + 1) * P], xg[:, h, k * P:(k + 1) * P], ident)
                last.then_inc(m_xt, 1)

            def up(s, nth, h):
                e = expert_of(s)
                pe.wait_ge(m_xs, at(s, 1, 1))
                for bank, w, done in ((1 + h, w1_sb, m_g), (3 + h, w2_sb, m_v)):
                    for k in range(DC):
                        last = mm(PS[:, bank, :], xgT[:, h, k * P:(k + 1) * P], w[:, ds(e * (DC * FF) + k * FF, FF)],
                                  start=k == 0, stop=k == DC - 1)
                    last.then_inc(done, 1)

            def down(s, nth, h):
                e = expert_of(s)
                pe.wait_ge(m_h, at(s, 1, 1))
                for f in range(FC):
                    last = nc.tensor.transpose(PS[:, 5, f * P:(f + 1) * P], h_s[:, h, f * P:(f + 1) * P], ident)
                last.then_inc(m_ht, 1)
                pe.wait_ge(m_hs, at(s, 1, 1))
                for f in range(FC):
                    last = mm(PS[:, 6, 0:DIM], hT_s[:, f * P:(f + 1) * P], w3_sb[:, ds(e * (FC * DIM) + f * DIM, DIM)],
                              start=f == 0, stop=f == FC - 1)
                last.then_inc(m_o, 1)

            pe.wait_ge(r_tab, 1)
            pe.wait_ge(s_w1, 16)
            pe.wait_ge(s_w23, 16 * 5)
            tokensT(*tile(0, 0))
            up(*tile(0, 0))
            tokensT(*tile(0, 1))
            with pe.Fori(0, (MOE_TILES - 1) // 2) as u:
                for k in (1, 2):
                    up(*tile(u, k))
                    down(*tile(u, k - 1))
                    tokensT(*tile(u, k + 1))
            pe.wait_ge(m_yo, MOE_TILES - 1)
            down(*tile(0, MOE_TILES - 1))

        @block.scalar
        def _(act):
            A = nc.scalar.activation

            def linear_attention(i):
                for m in range(DC):
                    act.wait_ge(p_q, at(i, DC, m + 1))
                    A(eq_s[:, m, :], PS[:, m, :], ACT.Exp, bias=bq_c[:, m:m + 1])
                    A(rq_s[:, m, :], PS[:, m, :], ACT.Relu, bias=bq_c[:, m:m + 1]).then_inc(a_q, 1)
                for t in range(TT):
                    act.wait_ge(d_kv, at(i, TT, t + 1))
                    A(ek_s[:, t, :], kv_s[:, t, 0:DIM], ACT.Exp)
                    A(rk_s[:, t, :], kv_s[:, t, 0:DIM], ACT.Relu).then_inc(a_k, 1)
                act.wait_ge(p_m, at(i, 1, 1))
                A(m_s.rearrange("p a b -> p (a b)"), PS[:, 7, :], ACT.Copy).then_inc(a_m, 1)

            def proj(i, p, which):
                act.wait_ge(p_proj, at(i, 3 * PAIRS, 3 * p + which + 1))
                if which == 0:
                    A(KT[:, p % 2, :], PS[:, 7, :], ACT.Identity, bias=bK_c[:, p:p + 1]).then_inc(a_kq, 1)
                else:
                    A(QT[:, p % 2, :], PS[:, 7, :], ACT.Identity, bias=nbQ[:, p:p + 1], scale=-1.0 / HD ** 0.5).then_inc(a_kq, 1)

            def exps(i, s):
                n = (s % TT + 1) * P
                act.wait_ge(d_min, at(i, STEPS, s + 1))
                for e in range(2):
                    A(prob[:, s % 2, e, 0:n], PS[:, 2 * (s % 2) + e, 0:n], ACT.Exp, bias=smin[:, s % 2, e:e + 1], scale=-1.0,
                      accum_out=ssum[:, s % 2, e:e + 1]).then_inc(a_e, 1)

            def attention(i):
                proj(i, 0, 0)
                act.wait_ge(p_xt, at(i, 1, 1))
                A(x1qT_s, PS[:, 2:4, :], ACT.Copy).then_inc(a_xt, 1)
                proj(i, 0, 1)
                exps(i, 0)
                exps(i, 1)
                for s in range(STEPS):
                    p, t = divmod(s, TT)
                    act.wait_ge(p_t, at(i, STEPS, s + 1))
                    A(PT[2 * (p % 2)][:, 0:t + 1, t * P:(t + 1) * P],
                      PS[:, 4, 0:(t + 1) * P].rearrange("p (a b) -> p a b", b=P), ACT.Copy).then_inc(a_t, 1)
                    if s + 2 < STEPS:
                        exps(i, s + 2)
                    if p + 1 < PAIRS and t < 2:
                        proj(i, p + 1, t)
                act.wait_ge(p_x2t, at(i, 1, 1))
                A(x2T_s, PS[:, 2:4, :], ACT.Copy).then_inc(a_x2t, 1)

            act.wait_ge(s_wlin, 16 * 8)
            act.wait_ge(s_wo, 16 * 6)
            A(nbQ, bQ_c, ACT.Copy, scale=-1.0 / HD ** 0.5).then_inc(s_cb, 1)
            act.wait_ge(s_cb, 4)
            with act.Fori(0, NB) as i:
                linear_attention(i)
                attention(i)

            act.wait_ge(r_d, 3)
            A(gates[:, 1, :], choice[:, 0, :], ACT.Exp).then_inc(r_e, 1)

            def silu(s, nth, h):
                act.wait_ge(m_gb, at(s, 1, 1))
                A(silu_s[:, h, :], g_s[:, h, :], ACT.Silu).then_inc(m_si_, 1)

            def hidden(s, nth, h):
                act.wait_ge(m_ht, at(s, 1, 1))
                A(hT_s, PS[:, 5, :], ACT.Copy).then_inc(m_hs, 1)

            silu(*tile(0, 0))
            with act.Fori(0, (MOE_TILES - 1) // 2) as u:
                for k in (1, 2):
                    silu(*tile(u, k))
                    hidden(*tile(u, k - 1))
            hidden(*tile(0, MOE_TILES - 1))

        @block.vector
        def _(ve):
            V = nc.vector

            def layer_stats(n0, pre, st, mvt, done_pre, done_st, done_mv):
                for t in range(TT):
                    ve.wait_ge(done_pre, n0 + t + 1)
                    V.bn_stats(st[:, t, 0:6], pre[:, t, :]).then_inc(done_st, 1)
                for t in range(TT):
                    wait_alone(ve, done_st, n0 + t + 1)
                    V.bn_aggr(mvt[:, t, :], st[:, t, 0:6]).then_inc(done_mv, 1)

            def linear_attention(i):
                for t in range(TT):
                    ve.wait_ge(p_kv, at(i, TT, t + 1))
                    V.tensor_tensor(kv_s[:, t, :], PS[:, 2 + t, :], bkv_b, ALU.add).then_inc(d_kv, 1)
                for t in range(TT):
                    ve.wait_ge(a_k, at(i, TT, t + 1))
                    V.scalar_tensor_tensor(k_s[:, t, :], ek_s[:, t, :], 1.0, rk_s[:, t, :], ALU.min, ALU.add).then_inc(d_kf, 1)
                ve.wait_ge(a_q, at(i, DC, DC))
                V.scalar_tensor_tensor(q_s, eq_s, 1.0, rq_s, ALU.min, ALU.add).then_inc(d_qf, 1)
                ve.wait_ge(p_bd, at(i, 1, 1))
                V.tensor_tensor(bd_s, PS[:, 6, 0:DIM].rearrange("p (a b) -> p a b", b=P),
                                cst[:, C_BLOCK:C_BLOCK + P].unsqueeze(1).to_broadcast([P, DC, P]), ALU.mult).then_inc(d_bd, 1)
                ve.wait_ge(s_cT, at(i, 16, 16))
                V.tensor_scalar(qe_s.bitcast(U32), cT_s.bitcast(U32), 0x7F800000, None, ALU.bitwise_and).then_inc(d_ce, 1)
                ve.wait_ge(d_ce, at(i, 1, 1))
                V.tensor_scalar(qm_s, qe_s, 2.0 ** -6, 1.5 * 2.0 ** 20, ALU.max, ALU.mult).then_inc(d_cm, 1)
                ve.wait_ge(g_res, at(i, 1, 1))
                for t in range(TT):
                    ve.wait_ge(p_y1, at(i, TT, t // 2 * 2 + 2))
                    V.tensor_tensor(pre_s[:, t, :], PS[:, t // 2, (t % 2) * DIM:(t % 2 + 1) * DIM], res_s[:, t, :],
                                    ALU.add).then_inc(d_pre, 1)
                layer_stats(at(i, 2 * TT, 0), pre_s, stats, mv, d_pre, d_st, d_mv)
                wait_alone(ve, g_rs, at(i, 2, 1))
                for t in range(TT):
                    V.tensor_scalar(x1q_s[:, t, :], pre_s[:, t, :], mv[:, t, 0:1], rstd[:, t:t + 1], ALU.subtract, ALU.mult,
                                    saturate=False).then_inc(d_xq, 1)
                for t in range(TT):
                    V.tensor_scalar(x1_s[:, t, :], pre_s[:, t, :], mv[:, t, 0:1], rstd[:, t:t + 1], ALU.subtract, ALU.mult)\
                     .then_inc(d_x1, 1)

            def proj_v(i, p):
                ve.wait_ge(p_proj, at(i, 3 * PAIRS, 3 * p + 3))
                V.tensor_tensor(V_s[:, p % 2], PS[:, 7, :].rearrange("p (a b) -> p a b", b=P),
                                bV_b[:, p * P:(p + 1) * P].unsqueeze(1).to_broadcast([P, TT, P]), ALU.add).then_inc(d_v, 1)

            def row_min(i, s):
                n = (s % TT + 1) * P
                ve.wait_ge(p_s, at(i, STEPS, s + 1))
                V.tensor_reduce(smin[:, s % 2, :], PS[:, 2 * (s % 2):2 * (s % 2) + 2, 0:n], AX_X, ALU.min).then_inc(d_min, 1)

            def row_inv(i, s):
                ve.wait_ge(a_e, at(i, 2 * STEPS, 2 * s + 2))
                V.reciprocal(sinv[:, s % 2, :], ssum[:, s % 2, :]).then_inc(d_inv, 1)

            def z_rows(i, p):
                ve.wait_ge(p_z, at(i, PAIRS, p + 1))
                V.tensor_copy(ZT[:, p, :], PS[:, 6, :]).then_inc(d_z, 1)

            def attention(i):
                proj_v(i, 0)
                row_min(i, 0)
                row_min(i, 1)
                row_inv(i, 0)
                for s in range(STEPS):
                    p, t = divmod(s, TT)
                    if s + 1 < STEPS:
                        row_inv(i, s + 1)
                    if s + 2 < STEPS:
                        row_min(i, s + 2)
                    ve.wait_ge(p_t, at(i, STEPS, s + 1))
                    V.tensor_copy(PT[2 * (p % 2) + 1][:, 0:t + 1, t * P:(t + 1) * P],
                                  PS[:, 5, 0:(t + 1) * P].rearrange("p (a b) -> p a b", b=P)).then_inc(d_t, 1)
                    if p + 1 < PAIRS and t == 2:
                        proj_v(i, p + 1)
                    if t == 0 and p >= 1:
                        z_rows(i, p - 1)
                z_rows(i, PAIRS - 1)

            def attention_output(i):
                ve.wait_ge(g_res2, at(i, 1, 1))
                for t in range(TT):
                    ve.wait_ge(p_y2, at(i, TT, t // 2 * 2 + 2))
                    V.tensor_tensor(x1_s[:, t, :], PS[:, t // 2, (t % 2) * DIM:(t % 2 + 1) * DIM], res_s[:, t, :],
                                    ALU.add).then_inc(d_pre, 1)
                layer_stats(at(i, 2 * TT, TT), x1_s, stats, mv, d_pre, d_st, d_mv)
                ve.wait_ge(g_rs, at(i, 2, 2))
                wait_alone(ve, s_x2out, at(i, 16, 16))
                for t in range(TT):
                    V.tensor_scalar(x2_s[:, t, :], x1_s[:, t, :], mv[:, t, 0:1], rstd[:, t:t + 1], ALU.subtract, ALU.mult)\
                     .then_inc(d_x2, 1)
                ve.wait_ge(p_lg, at(i, 1, 1))
                V.tensor_copy(logits[:, ds(i * TT, TT), :], PS[:, 4, 0:TT * NE].rearrange("p (a b) -> p a b", b=NE))\
                 .then_inc(d_lg, 1)

            ve.wait_ge(s_const, 16)
            V.tensor_copy(ident_b[:, :], ident)
            V.tensor_copy(causal_b[:, :], cst[:, C_CAUSAL:C_CAUSAL + P]).then_inc(s_cb, 1)
            V.memset(ones_b[:, :], 1.0).then_inc(s_cb, 1)
            V.tensor_copy(tri_b[:, :], cst[:, C_TRI:C_TRI + P]).then_inc(s_cb, 1)
            raw_bits, magic = stage_w[0], stage_w[1]
            for n, (_, wt, k, c) in enumerate(raw_w):
                q = (n % 4) * 512
                m = (n % 2) * 1024
                ve.wait_ge(s_wraw[n % 4], 16 * (n // 4 + 1))
                V.tensor_scalar(magic[:, m:m + 512].bitcast(U32), raw_bits[:, q:q + 512].bitcast(U32), 0x7F800000, None,
                                ALU.bitwise_and).then_inc(s_wexp, 1)
                ve.wait_ge(s_wexp, n + 1)
                V.tensor_scalar(magic[:, m + 512:m + 1024], magic[:, m:m + 512], 2.0 ** -6, 1.5 * 2.0 ** 20, ALU.max, ALU.mult)\
                 .then_inc(s_wmag, 1)
                ve.wait_ge(s_wmag, n + 1)
                V.tensor_tensor(magic[:, m:m + 512], raw_bits[:, q:q + 512], magic[:, m + 512:m + 1024], ALU.add).then_inc(s_wadd, 1)
                ve.wait_ge(s_wadd, n + 1)
                V.tensor_tensor(wt[:, k, c * 512:(c + 1) * 512], magic[:, m:m + 512], magic[:, m + 512:m + 1024], ALU.subtract)\
                 .then_inc(s_wcvt, 1)
            ve.wait_ge(s_wlin, 16 * 8)
            ve.wait_ge(s_wo, 16 * 6)
            ve.wait_ge(s_wcvt, N_WRAW)
            with ve.Fori(0, NB) as i:
                linear_attention(i)
                attention(i)
                attention_output(i)

            step = [0]

            def done(ins):
                ins.then_inc(r_d, 1)
                step[0] += 1
                ve.wait_ge(r_d, step[0])

            ve.wait_ge(d_lg, NB)
            for t in range(ROWTILES):
                last = V.max(top[:, t, :], logits[:, t, :])
            done(last)
            for t in range(ROWTILES):
                last = V.max_index(topi[:, t, :], top[:, t, :], logits[:, t, :])
            done(last)
            done(V.tensor_tensor(choice[:, 0, :], top[:, :, 1], top[:, :, 0], ALU.subtract))
            ve.wait_ge(r_e, 1)
            done(V.tensor_scalar(gates[:, 0, :], gates[:, 1, :], 1.0, None, ALU.add))
            done(V.reciprocal(slot[:, 0, :], gates[:, 0, :]))
            done(V.tensor_copy(gates[:, 0, :], slot[:, 0, :]))
            done(V.tensor_tensor(slot[:, 1, :], gates[:, 1, :], slot[:, 0, :], ALU.mult))
            done(V.tensor_copy(gates[:, 1, :], slot[:, 1, :]))
            done(V.tensor_copy(choice, topi[:, :, 0:TOPK].rearrange("p t j -> p j t")))
            iota_e = cst[:, C_IOTA:C_IOTA + NE].unsqueeze(1).to_broadcast([P, ROWTILES, NE])
            hot = [onehot[:, j, :].rearrange("p (t e) -> p t e", e=NE) for j in range(TOPK)]
            for j in range(TOPK):
                done(V.tensor_tensor(hot[j], iota_e, choice[:, j, :].unsqueeze(2).to_broadcast([P, ROWTILES, NE]), ALU.is_equal))
            V.tensor_tensor(both_b, onehot[:, 0, :], onehot[:, 1, :], ALU.add).then_inc(r_hot, 1)
            ve.wait_ge(r_pre, 1)
            done(V.tensor_copy(run_a, PS[:, 1, 0:ROWTILES * NE].rearrange("p (t e) -> p t e", e=NE)))
            a, b = run_a, run_b
            d = 1
            while d < ROWTILES:
                V.tensor_copy(b[:, 0:d, :], a[:, 0:d, :])
                done(V.tensor_tensor(b[:, d:, :], a[:, d:, :], a[:, 0:ROWTILES - d, :], ALU.add))
                a, b = b, a
                d *= 2
            done(V.tensor_scalar(etiles, a[:, ROWTILES - 1, :], float(P - 1), None, ALU.add))
            done(V.tensor_copy(etiles_i, etiles))
            done(V.tensor_scalar(etiles_i, etiles_i, 7, None, ALU.logical_shift_right))
            done(V.tensor_copy(etiles, etiles_i))
            done(V.tensor_copy(cum_a, etiles))
            ca, cb = cum_a, cum_b
            d = 1
            while d < NE:
                V.tensor_copy(cb[:, 0:d], ca[:, 0:d])
                done(V.tensor_tensor(cb[:, d:], ca[:, d:], ca[:, 0:NE - d], ALU.add))
                ca, cb = cb, ca
                d *= 2
            done(V.tensor_tensor(past, cst[:, C_IOTA:C_IOTA + LIST_COLS].unsqueeze(2).to_broadcast([P, LIST_COLS, NE]),
                                 ca.unsqueeze(1).to_broadcast([P, LIST_COLS, NE]), ALU.is_ge))
            done(V.tensor_reduce(expert_f, past, AX_X, ALU.add))
            done(V.tensor_scalar(expert_f, expert_f, float(NE - 1), None, ALU.min))
            done(V.tensor_copy(expert[:, :], expert_f))
            done(V.tensor_tensor(cb, ca, etiles, ALU.subtract))
            done(V.tensor_scalar(cb, cb, float(P), None, ALU.mult))
            done(V.tensor_tensor(before, a, PS[:, 1, 0:ROWTILES * NE].rearrange("p (t e) -> p t e", e=NE), ALU.subtract))
            done(V.tensor_tensor(before, before, PS[:, 0, 0:ROWTILES * NE].rearrange("p (t e) -> p t e", e=NE), ALU.add))
            done(V.tensor_tensor(before, before, cb.unsqueeze(1).to_broadcast([P, ROWTILES, NE]), ALU.add))
            for j in range(TOPK):
                done(V.tensor_tensor(hot[j], hot[j], before, ALU.mult))
                done(V.tensor_reduce(slot[:, j, :], hot[j], AX_X, ALU.add))
            flat = slot.rearrange("p j t -> p (j t)")
            done(V.tensor_copy(slot_i, flat))
            done(V.tensor_scalar(tile_i, slot_i, 7, None, ALU.logical_shift_right))
            done(V.tensor_scalar(lane_i, slot_i, P - 1, None, ALU.bitwise_and))
            done(V.tensor_copy(tile_f, tile_i))
            done(V.tensor_copy(lane_f, lane_i))
            for n in range(ROWTILES * TOPK):
                t, j = divmod(n, TOPK)
                col = j * ROWTILES + t
                if n >= 2:
                    ve.wait_ge(r_list, n - 1)
                V.tensor_scalar(lane_hot[:, n % 2, :], cst[:, C_IOTA:C_IOTA + P], lane_f[:, col:col + 1], None, ALU.is_equal)
                V.tensor_scalar(code_hot[:, n % 2, 0:LIST_COLS], cst[:, C_IOTA:C_IOTA + LIST_COLS], tile_f[:, col:col + 1],
                                cst[:, C_LANE + 2 + j:C_LANE + 3 + j], ALU.is_equal, ALU.mult)
                V.tensor_scalar(code_hot[:, n % 2, LIST_COLS:], cst[:, C_IOTA:C_IOTA + LIST_COLS], tile_f[:, col:col + 1],
                                float(t), ALU.is_equal, ALU.mult).then_inc(r_hot, 1)
            ve.wait_ge(r_list, ROWTILES * TOPK)
            done(V.tensor_copy(hi_s, PS[:, 2, LIST_COLS:2 * LIST_COLS]))
            done(V.scalar_tensor_tensor(code, hi_s, float(TOPK * P), PS[:, 2, 0:LIST_COLS], ALU.mult, ALU.add))
            done(V.tensor_scalar(empty, code, 0.0, cst[:, C_LANE + 1:C_LANE + 2], ALU.is_equal, ALU.mult))
            done(V.tensor_scalar(hi_s, code, -1.0, 0.0, ALU.add, ALU.max))
            done(V.tensor_tensor(empty, empty, code, ALU.add))
            done(V.tensor_scalar(empty, empty, -1.0, None, ALU.add))
            done(V.tensor_copy(scatter_l[:, :], empty))
            done(V.tensor_copy(code_i, hi_s))
            done(V.tensor_scalar(gather_l[:, :].bitcast(I32), code_i, 1, None, ALU.logical_shift_right))
            V.tensor_copy(hi_s, expert_f).then_inc(r_tab, 1)

            def expert_of(s):
                return ve.value_load(expert[0:1, ds(s, 1)], min_val=0, max_val=NE - 1)

            def tokensT(s, nth, h):
                ve.wait_ge(m_xt, at(s, 1, 1))
                V.tensor_copy(xgT[:, h, :], PS[:, 0, 0:DIM]).then_inc(m_xs, 1)

            def gated(s, nth, h):
                e = expert_of(s)
                ve.wait_ge(m_g, at(s, 1, 1))
                V.tensor_tensor(g_s[:, h, :], PS[:, 1 + h, :], b1_b[:, ds(e * FF, FF)], ALU.add).then_inc(m_gb, 1)
                ve.wait_ge(m_v, at(s, 1, 1))
                V.tensor_tensor(v_s[:, h, :], PS[:, 3 + h, :], b2_b[:, ds(e * FF, FF)], ALU.add).then_inc(m_vb, 1)
                ve.wait_ge(m_si_, at(s, 1, 1))
                ve.wait_ge(m_vb, at(s, 1, 1))
                V.tensor_tensor(h_s[:, h, :], silu_s[:, h, :], v_s[:, h, :], ALU.mult).then_inc(m_h, 1)

            def rows_out(s, nth, h, wait=True):
                e = expert_of(s)
                ve.wait_ge(m_o, at(s, 1, 1))
                if wait:
                    ve.wait_ge(m_out[h], nth * 16)
                V.tensor_tensor(yo[:, h, :], PS[:, 6, 0:DIM], b3_b[:, ds(e * DIM, DIM)], ALU.add).then_inc(m_yo, 1)

            ve.wait_ge(s_w23, 16 * 5)
            tokensT(*tile(0, 0))
            gated(*tile(0, 0))
            tokensT(*tile(0, 1))
            for k in (1, 2):
                gated(*tile(0, k))
                rows_out(*tile(0, k - 1), wait=False)
                tokensT(*tile(0, k + 1))
            with ve.Fori(1, (MOE_TILES - 1) // 2) as u:
                for k in (1, 2):
                    gated(*tile(u, k))
                    rows_out(*tile(u, k - 1))
                    tokensT(*tile(u, k + 1))
            rows_out(*tile(0, MOE_TILES - 1))

            for i in range(NB):
                h = i % 2
                ve.wait_ge(c_in[h], 32 * (i // 2 + 1))
                for t in range(TT):
                    V.scalar_tensor_tensor(zz[:, h, t, :], yy[:, h, t, 0:DIM], gates[:, 0, i * TT + t:i * TT + t + 1], xx[:, h, t, :],
                                           ALU.mult, ALU.add).then_inc(c_mix, 1)
                for t in range(TT):
                    ve.wait_ge(c_mix, i * TT + t + 1)
                    V.scalar_tensor_tensor(xx[:, h, t, :], yy[:, h, t, DIM:2 * DIM], gates[:, 1, i * TT + t:i * TT + t + 1],
                                           zz[:, h, t, :], ALU.mult, ALU.add).then_inc(c_pre, 1)
                layer_stats(i * TT, xx[:, h], stats4, mv4, c_pre, c_st, c_mv)
                ve.wait_ge(c_rs, i + 1)
                if i >= 2:
                    ve.wait_ge(s_out[h], 16 * (i // 2))
                for t in range(TT):
                    V.tensor_scalar(oo[:, h, t, :], xx[:, h, t, :], mv4[:, t, 0:1], rstd4[:, t:t + 1], ALU.subtract, ALU.mult)\
                     .then_inc(c_o, 1)

        @block.gpsimd
        def _(po):
            G = nc.gpsimd
            half = cst[:, C_LANE + 4:C_LANE + 8]

            def rsqrt(out_, mvt, ve_sem, n, done):
                G.tensor_scalar(out_, mvt[:, :, 1], EPS, 1.0, ALU.add, ALU.mult).then_inc(ve_sem, 1)
                wait_alone(po, ve_sem, n)
                G.tensor_tensor(out_, out_, half, ALU.pow).then_inc(done, 1)

            po.wait_ge(s_const, 16)
            po.wait_ge(s_wlin, 16 * 8)
            po.wait_ge(s_wo, 16 * 6)
            with po.Fori(0, NB) as i:
                po.wait_ge(s_xr, at(i, 16, 16))
                G.tensor_tensor(res_s, xr_s, bp_b.unsqueeze(1).to_broadcast([P, TT, DIM]), ALU.add).then_inc(g_res, 1)
                po.wait_ge(d_cm, at(i, 1, 1))
                G.tensor_tensor(qe_s, cT_s, qm_s, ALU.add).then_inc(g_ca, 1)
                po.wait_ge(g_ca, at(i, 1, 1))
                G.tensor_tensor(cq_s, qe_s, qm_s, ALU.subtract).then_inc(g_cq, 1)
                wait_alone(po, d_mv, at(i, 2 * TT, TT))
                rsqrt(rstd, mv, g_ve, at(i, 2, 1), g_rs)
                for s in range(STEPS):
                    n = (s % TT + 1) * P
                    wait_alone(po, d_inv, at(i, STEPS, s + 1))
                    for e in range(2):
                        last = G.tensor_scalar(pnorm[:, s % 2, e, 0:n], prob[:, s % 2, e, 0:n], sinv[:, s % 2, e:e + 1], 1.0,
                                               ALU.mult, ALU.mult)
                    last.then_inc(g_n, 1)
                    if s == 1:
                        po.wait_ge(d_x1, at(i, TT, TT))
                        G.tensor_tensor(res_s, x1_s, bO_b.unsqueeze(1).to_broadcast([P, TT, DIM]), ALU.add).then_inc(g_res2, 1)
                wait_alone(po, d_mv, at(i, 2 * TT, 2 * TT))
                rsqrt(rstd, mv, g_ve, at(i, 2, 2), g_rs)

            def gather(s, nth, h):
                G.tensor_copy(g_idx[:, h:h + 1], gather_l[:, ds(s, 1)]).then_inc(m_gi, 1)
                wait_alone(po, m_gi, at(s, 1, 1))
                G.indirect_dma_start(out=xg[:, h, :], out_offset=None, in_=x2_d,
                                     in_offset=bass.IndirectOffsetOnAxis(ap=g_idx[:, h:h + 1], axis=0)).then_inc(m_in[h], 16)

            def scatter(s, nth, h, first=False, second=False):
                if not (first or second):
                    po.wait_ge(m_out[h], nth * 16)
                G.tensor_copy(s_idx[:, h:h + 1], scatter_l[:, ds(s, 1)]).then_inc(m_si, 1)
                po.wait_ge(m_si, at(s, 1, 1))
                if not first:
                    po.wait_ge(m_out[1 - h], (nth + h) * 16)
                wait_alone(po, m_yo, at(s, 1, 1))
                G.indirect_dma_start(out=y_d, out_offset=bass.IndirectOffsetOnAxis(ap=s_idx[:, h:h + 1], axis=0),
                                     in_=yo[:, h, :], in_offset=None).then_inc(m_out[h], 16)

            def transposed(s, nth, h):
                po.wait_ge(m_xt, at(s, 1, 1))

            po.wait_ge(r_tab, 1)
            po.wait_ge(s_x2out, 16 * (NB + 1))
            gather(*tile(0, 0))
            gather(*tile(0, 1))
            transposed(*tile(0, 0))
            gather(*tile(0, 2))
            for k in (1, 2):
                transposed(*tile(0, k))
                gather(*tile(0, k + 2))
                scatter(*tile(0, k - 1), first=k == 1, second=k == 2)
            with po.Fori(1, (MOE_TILES - 1) // 2) as u:
                for k in (1, 2):
                    transposed(*tile(u, k))
                    gather(*tile(u, k + 2))
                    scatter(*tile(u, k - 1))
            scatter(*tile(0, MOE_TILES - 1))
            po.wait_ge(m_in[0], 16 * ((LIST_COLS + 1) // 2))
            po.wait_ge(m_in[1], 16 * (LIST_COLS // 2))

            for i in range(NB):
                po.wait_ge(c_mv, TT * (i + 1))
                rsqrt(rstd4, mv4, c_ve, i + 1, c_rs)


_IN = ["x", "xT", "cT", "Wq", "Wk", "Wv", "Wp", "bq", "bk", "bv", "bp", "WQ", "WK", "WV", "WO", "bQ", "bK", "bV", "bO",
       "WgT", "W1T", "b1", "W2T", "b2", "W3T", "b3", "consts"]


def kernel(x, ctx_1024, L0_attn_Wq, L0_attn_bq, L0_attn_Wk, L0_attn_bk, L0_attn_Wv, L0_attn_bv, L0_attn_Wp, L0_attn_bp,
           L0_xattn_W_Q, L0_xattn_W_K, L0_xattn_W_V, L0_xattn_W_O, L0_xattn_b_Q, L0_xattn_b_K, L0_xattn_b_V, L0_xattn_b_O,
           L0_ffn_Wg, L0_ffn_W1, L0_ffn_b1, L0_ffn_W2, L0_ffn_b2, L0_ffn_W3, L0_ffn_b3):
    import concourse.bacc as bacc
    from concourse.bass_utils import run_bass_kernel_spmd

    x = np.asarray(x)
    ctx_1024 = np.asarray(ctx_1024)

    def cols(w):
        return np.asarray(w).transpose(1, 0, 2).reshape(DIM, INNER)

    arrays = dict(
        x=x.reshape(TOK, DIM), xT=x.reshape(TOK, DIM).T, cT=ctx_1024.reshape(TOK, DIM).T,
        Wq=L0_attn_Wq, Wk=L0_attn_Wk, Wv=L0_attn_Wv, Wp=L0_attn_Wp, bq=L0_attn_bq, bk=L0_attn_bk, bv=L0_attn_bv, bp=L0_attn_bp,
        WQ=cols(L0_xattn_W_Q), WK=cols(L0_xattn_W_K), WV=cols(L0_xattn_W_V), WO=np.asarray(L0_xattn_W_O).reshape(INNER, DIM),
        bQ=np.asarray(L0_xattn_b_Q).reshape(INNER), bK=np.asarray(L0_xattn_b_K).reshape(INNER),
        bV=np.asarray(L0_xattn_b_V).reshape(INNER), bO=L0_xattn_b_O,
        WgT=np.asarray(L0_ffn_Wg).T, W1T=np.asarray(L0_ffn_W1).transpose(0, 2, 1), b1=np.asarray(L0_ffn_b1).reshape(-1),
        W2T=np.asarray(L0_ffn_W2).transpose(0, 2, 1), b2=np.asarray(L0_ffn_b2).reshape(-1),
        W3T=np.asarray(L0_ffn_W3).transpose(0, 2, 1), b3=np.asarray(L0_ffn_b3).reshape(-1), consts=constants())
    arrays = {n: np.ascontiguousarray(arrays[n]) for n in _IN}
    nc = bacc.Bacc("TRN2", target_bir_lowering=False, num_devices=1)
    args = {n: nc.dram_tensor(f"in_{n}", a.shape, mybir.dt.from_np(a.dtype), kind="ExternalInput").ap() for n, a in arrays.items()}
    out = nc.dram_tensor("out_rows", (TOK, DIM), F32, kind="ExternalOutput").ap()
    decoder_kernel(nc, out=out, **args)
    r = run_bass_kernel_spmd(nc, [{f"in_{n}": a for n, a in arrays.items()}], core_ids=[0])
    return r.results[0]["out_rows"].reshape(x.shape)
```

```python
from contextlib import ExitStack

import numpy as np

import concourse.bass as bass
from concourse import mybir

F32 = mybir.dt.float32
F32R = mybir.dt.float32r
BF16 = mybir.dt.bfloat16
FP8 = mybir.dt.float8e4
U32 = mybir.dt.uint32
I32 = mybir.dt.int32
ALU = mybir.AluOpType
ACT = mybir.ActivationFunctionType
AX_X = mybir.AxisListType.X

P = 128
NB, SEQ, DIM = 8, 512, 256
TOK = NB * SEQ
TT = SEQ // P
DC = DIM // P
LIN_D = 16
HEADS, HD = 16, 64
PAIRS = HEADS // 2
INNER = HEADS * HD
UNITS = HEADS * TT
ORDER = (3, 0, 2, 1)
NE, FF, TOPK = 8, 512, 2
FC = FF // P
ROWTILES = TOK // P
MOE_TILES = TOK * TOPK // P + NE - 1
LIST_COLS = MOE_TILES + 2
HOT = 8
DUMP = TOK * TOPK
GT = 2
GROUPS = ROWTILES // GT
DEPTH = 4
EPS = 1e-5
FAR = 1e30

C_IDENT, C_CAUSAL, C_TRI, C_BLOCK, C_IOTA, C_LANE = 0, P, 2 * P, 3 * P, 4 * P, 5 * P
C_CODE = C_LANE + 8
C_COLS = C_CODE + ROWTILES


def constants():
    r, c = np.arange(P)[:, None], np.arange(P)[None, :]
    t = np.zeros((P, C_COLS), np.float32)
    t[:, C_IDENT:C_IDENT + P] = r == c
    t[:, C_CAUSAL:C_CAUSAL + P] = np.where(c > r, FAR, 0.0)
    t[:, C_TRI:C_TRI + P] = r < c
    t[:, C_BLOCK:C_BLOCK + P] = r // LIN_D == c // LIN_D
    t[:, C_IOTA:C_IOTA + P] = c
    t[:, C_LANE] = np.arange(P)
    t[:, C_LANE + 1] = DUMP + 1 + np.arange(P)
    t[:, C_LANE + 2] = 2 * np.arange(P) + 1
    t[:, C_LANE + 3] = 2 * np.arange(P) + 2
    t[:, C_CODE:C_CODE + ROWTILES] = np.arange(ROWTILES)
    t[:, C_LANE + 4] = -0.5
    t[:, C_LANE + 5] = -0.5
    t[:, C_LANE + 6] = -0.5
    t[:, C_LANE + 7] = -0.5
    return t


def unit(u):
    return u // (2 * TT), ORDER[u // 2 % TT], u % 2


def at(i, per, k):
    return i * per + k


TABLE_OWN = ([(2 * TT * p, "Q", p + 1) for p in range(PAIRS - 1)] + [(2 * TT * p + 2, "V", p + 1) for p in range(PAIRS - 1)]
             + [(2 * TT * p + 6, "K", p + 2) for p in range(PAIRS - 2)])
TABLE_TAIL = [(3, "wo", 0), (4, "wo", 1), (5, "wo", 2), (9, "wo", 3), (17, "x2T", 0), (20, "x2T", 1), (25, "gate", 0)]
TABLE_NEXT = [(12, "kv", 0), (13, "kv", 1), (21, "kv", 2), (28, "kv", 3), (29, "q", 0), (33, "q", 1), (36, "vTk", 0),
              (41, "vTkWp", 0), (44, "y", 0), (45, "y", 1), (52, "x1T", 0), (53, "x1T", 1),
              (54, "K", 0), (56, "Q", 0), (58, "V", 0), (62, "K", 1)]


class Round:

    def __init__(self, i, base, norms, own=True, tail=True, ahead=True):
        self.i, self.base = i, base
        self.own, self.tail, self.ahead = own, tail, ahead
        self.tail_norm, self.ahead_norm = norms, norms + (1 if tail else 0)
        self.table = sorted(TABLE_OWN * own + TABLE_TAIL * tail + TABLE_NEXT * ahead)

    def number(self, job, k=0):
        return self.base + [(j, n) for _, j, n in self.table].index((job, k))

    def slot(self, u):
        return [(job, k) for s, job, k in self.table if s == u]


PER_ROUND = len(TABLE_OWN + TABLE_TAIL + TABLE_NEXT)
BEFORE_0 = len(TABLE_NEXT) - len(TABLE_TAIL)


def prologue():
    return Round(-1, 0, 0, own=False, tail=False)


def first_round():
    return Round(0, len(TABLE_NEXT), 1, tail=False)


def middle_round(i):
    return Round(i, i * PER_ROUND + BEFORE_0, i * 2)


def last_round():
    return Round(NB - 1, (NB - 1) * PER_ROUND + BEFORE_0, 2 * NB - 2, ahead=False)


def epilogue():
    return Round(NB, NB * PER_ROUND - len(TABLE_TAIL), 2 * NB - 1, own=False, ahead=False)


PRODUCTS = NB * PER_ROUND


def decoder_kernel(nc, x, xT, cT, Wq, Wk, Wv, Wp, bq, bk, bv, bp, WQ, WK, WV, WO, bQ, bK, bV, bO,
                   WgT, W1T, b1, W2T, b2, W3T, b3, consts, out):
    x2_d = nc.dram_tensor("x2_rows", (TOK, DIM), F32, kind="Internal").ap()
    y_d = nc.dram_tensor("expert_rows", (DUMP + P, DIM), F32, kind="Internal").ap()

    with ExitStack() as ctx:
        def sb(name, shape, dt=F32):
            return ctx.enter_context(nc.sbuf_tensor(name, shape, dt))

        def sem(name):
            return ctx.enter_context(nc.semaphore(name))

        PS = ctx.enter_context(nc.psum_tensor("PS", [P, 8, 512], F32))

        cst = sb("cst", [P, C_COLS])
        ident = cst[:, C_IDENT:C_IDENT + P]
        ident_b = sb("ident_b", [P, P], BF16)
        causal_b = sb("causal_b", [P, P], BF16)
        tri_b = sb("tri_b", [P, P], BF16)
        ones_b = sb("ones_b", [P, P], BF16)
        logits = sb("logits", [P, ROWTILES, NE])
        gates = sb("gates", [P, TOPK, ROWTILES])
        w1_sb = sb("w1_sb", [P, NE * DC * FF])
        QH, QL, KH, KL = (sb(name, [P, 2, SEQ], F32R) for name in ("QH", "QL", "KH", "KL"))
        ARENA = 38 * 1024
        arena = sb("arena", [P, ARENA])
        used = [0, 0]

        def view(stage, *shape, dt=F32):
            n = int(np.prod(shape)) * (4 if dt in (F32, U32, I32) else 2 if dt == BF16 else 1) // 4
            a = used[stage]
            used[stage] += n
            assert used[stage] <= ARENA, used
            v = arena[:, a:a + n]
            if dt != F32:
                v = v.bitcast(dt)
            if len(shape) > 1:
                names = "abc"[:len(shape)]
                v = v.rearrange(f"p ({' '.join(names)}) -> p {' '.join(names)}",
                                **dict(zip(names[1:], shape[1:])))
            return v

        wq, wk, wv, wp = (view(0, DC, DIM) for _ in range(4))
        wQ, wK, wV = (view(0, DC, INNER, dt=BF16) for _ in range(3))
        bkv_b = view(0, 2 * DIM)
        bp_b = view(0, DIM)
        bV_b = view(0, INNER)
        xT_s, cT_s = view(0, DC, SEQ), view(0, DC, SEQ)
        xr_s = view(0, TT, DIM)
        kv_s = view(0, TT, 2 * DIM)
        ek_s, rk_s = view(0, DIM), view(0, DIM)
        rq_s = view(0, SEQ)
        qm_s = view(0, DC, SEQ)
        bd_s, m_s = view(0, DC, P), view(0, DC, DIM)
        cq_s, x1qT_s = view(0, DC, SEQ, dt=BF16), view(0, DC, SEQ, dt=BF16)
        EARLY = used[0]
        x1q_s = view(0, TT, DIM, dt=FP8)
        wO = view(0, PAIRS, DIM)
        wg = view(0, DC, NE)
        bq_c = view(0, DC)
        bQ_c, bK_c, nbQ = view(0, PAIRS), view(0, PAIRS), view(0, PAIRS)
        bO_b = view(0, DIM)
        q_s = view(0, DC, SEQ)
        x2T_s = q_s
        x1_s = view(0, TT, DIM)
        stats, mv, rstd = view(0, TT, 8), view(0, TT, 2), view(0, TT)
        stats1, mv1, rstd1 = view(0, TT, 8), view(0, TT, 2), view(0, TT)
        V_s = view(0, 2, TT, P)
        ZT = view(0, PAIRS, SEQ)
        prob, pnorm = view(0, 4, SEQ), view(0, 4, SEQ)
        smin, ssum, sinv = view(0, 4), view(0, 4), view(0, 4)
        PT = [view(0, TT, SEQ) for _ in range(4)]
        stage_w = [prob.rearrange("p a b -> p (a b)"), pnorm.rearrange("p a b -> p (a b)")]

        w2_sb = view(1, NE * DC * FF)
        w3_sb = view(1, NE * FC * DIM)
        W3_EARLY = (EARLY - NE * DC * FF) // (FC * DIM)
        b1_b, b2_b, b3_b = view(1, NE * FF), view(1, NE * FF), view(1, NE * DIM)
        mark = used[1]
        top = view(1, ROWTILES, NE)
        topi = view(1, ROWTILES, NE, dt=U32)
        choice = view(1, TOPK, ROWTILES)
        onehot = view(1, TOPK, ROWTILES * NE)
        both_b = view(1, ROWTILES * NE, dt=BF16)
        run_a, run_b = view(1, ROWTILES, NE), view(1, ROWTILES, NE)
        before = view(1, ROWTILES, NE)
        etiles, etiles_i = view(1, NE), view(1, NE, dt=I32)
        cum_a, cum_b = view(1, NE), view(1, NE)
        slot = view(1, TOPK, ROWTILES)
        slot_i, tile_i, lane_i = (view(1, TOPK * ROWTILES, dt=I32) for _ in range(3))
        tile_f, lane_f = view(1, TOPK * ROWTILES), view(1, TOPK * ROWTILES)
        lane_hot = view(1, 2, HOT, P, dt=BF16)
        tile_hot, code_hot = view(1, 2, HOT, LIST_COLS), view(1, 2, HOT, 2 * LIST_COLS, dt=BF16)
        hi_s, code, empty = view(1, LIST_COLS), view(1, LIST_COLS), view(1, LIST_COLS)
        past = view(1, LIST_COLS, NE)
        expert_f = view(1, LIST_COLS)
        expert = sb("expert", [P, LIST_COLS], I32)
        gather_l = sb("gather_l", [P, LIST_COLS], U32)
        scatter_l = sb("scatter_l", [P, LIST_COLS], U32)
        code_i = view(1, LIST_COLS, dt=I32)
        used[1] = mark
        xg = view(1, 2, DIM)
        g_idx, s_idx = sb("g_idx", [P, 2], U32), sb("s_idx", [P, 2], U32)
        xgT = view(1, 2, DIM)
        g_s, v_s = view(1, 2, FF), view(1, 2, FF)
        silu_s, h_s = view(1, 2, FF), view(1, 2, FF)
        hT_s = view(1, FF)
        yo = view(1, 2, DIM)
        used[1] = 0
        yy, xx = view(1, DEPTH, GT, TOPK * DIM), view(1, DEPTH, GT, DIM)
        zz, oo = view(1, DEPTH, GT, DIM), view(1, 2, GT, DIM)
        stats4, mv4, rstd4 = view(1, DEPTH, GT, 8), view(1, DEPTH, GT, 2), view(1, DEPTH, GT)

        s_const, s_wq, s_wlin, s_wo = sem("const_in"), sem("wq_in"), sem("lin_weights_in"), sem("wo_in")
        s_wraw = [sem(f"raw_weights_in{q}") for q in range(4)]
        s_w1, s_w23 = sem("w1_in"), sem("w23_in")
        s_cb, s_wexp, s_wmag, s_wadd, s_wcvt = sem("consts_bf16"), sem("w_exponents"), sem("w_magic"), sem("w_added"), sem("w_rounded")
        s_nbQ, s_wscaled = sem("scaled_bQ"), sem("scaled_WQ")
        s_xT, s_xr, s_cT, s_x2out = sem("xT_in"), sem("x_rows_in"), sem("ctx_in"), sem("x2_out")
        p7, x7 = sem("bank7_mm"), sem("bank7_read")
        p_s, p_t, p_z = sem("score_mm"), sem("probT_mm"), sem("z_mm")
        a_h, a_k, a_e, a_t = sem("KQ_rounded"), sem("k_exp_relu"), sem("exp_done"), sem("probT0_sb")
        d_kf, d_qf, d_ce, d_cm = sem("k_feat"), sem("q_feat"), sem("ctx_exponents"), sem("ctx_magic")
        d_st, d_mv, d_x1, d_xq, d_x2 = sem("ln_stats"), sem("ln_mean_var"), sem("x1_rows"), sem("x1q_rows"), sem("x2_rows_sb")
        d_min, d_inv, d_t, a_z = sem("row_min"), sem("row_inv"), sem("probT1_sb"), sem("Z_sb")
        g_ca, g_cq, g_res, g_ve, g_rs, g_n, g_res2 = sem("ctx_added"), sem("ctx_rounded"), sem("x_plus_bias"), sem("var_eps"), sem("rstd"), sem("prob_normed"), sem("x1_plus_bias")
        r_d, r_e, r_pre, r_hot, r_list, r_tab = sem("route_dve"), sem("route_exp"), sem("prefix_mm"), sem("hot_ready"), sem("list_mm"), sem("tables_ready")
        r_lane, r_tile, r_low, r_high = sem("lane_hot"), sem("tile_hot"), sem("code_low"), sem("code_high")
        m_gi, m_si = sem("gather_idx"), sem("scatter_idx")
        m_in, m_out = [sem(f"tokens_in{h}") for h in range(2)], [sem(f"rows_out{h}") for h in range(2)]
        c_in, s_out = [sem(f"mix_in{h}") for h in range(DEPTH)], [sem(f"out_stored{h}") for h in range(2)]
        m_xt, m_xs, m_g, m_v, m_ht, m_o = sem("xgT_mm"), sem("xgT_sb"), sem("g_mm"), sem("v_mm"), sem("hT_mm"), sem("o_mm")
        m_gb, m_vb, m_si_, m_h, m_hs, m_yo = sem("g_bias"), sem("v_bias"), sem("silu"), sem("h_sb"), sem("hT_sb"), sem("yo_sb")
        c_mix, c_sum, c_pre, c_st, c_mv, c_ve, c_rs, c_o = sem("mix_half"), sem("mix_plus_x2"), sem("mix_pre"), sem("mix_stats"), sem("mix_mv"), sem("mix_ve"), sem("mix_rstd"), sem("mix_out")

        s_passed = sem("waits_passed")

        def wait_alone(eng, semaphore, value):
            eng.wait_ge(semaphore, value)
            eng.sem_inc(s_passed, 1)

        def wait_past(eng, semaphore, i, per, k):
            if not (isinstance(i, int) and at(i, per, k) <= 0):
                eng.wait_ge(semaphore, at(i, per, k))

        def tile(u, k):
            return u * 2 + k, u + k // 2, k % 2

        block = ctx.enter_context(nc.Block())
        ds = bass.ds
        N_WRAW = 12
        raw_w = [(w, wt, k, n) for w, wt in ((WK, wK), (WQ, wQ), (WV, wV)) for k in range(DC) for n in range(2)]

        @block.sync
        def _(sp):
            sp.dma_start(cst[:, :], consts).then_inc(s_const, 16)

            def load_transposed(i):
                sp.dma_start(xT_s, xT[:, ds(i * SEQ, SEQ)].rearrange("(c p) t -> p c t", p=P)).then_inc(s_xT, 16)
                sp.dma_start(cT_s, cT[:, ds(i * SEQ, SEQ)].rearrange("(c p) t -> p c t", p=P)).then_inc(s_cT, 16)

            def load_rows(i):
                sp.dma_start(xr_s, x[ds(i * SEQ, SEQ), :].rearrange("(a p) d -> p a d", p=P)).then_inc(s_xr, 16)

            sp.dma_start(wq, Wq.rearrange("(c p) n -> p c n", p=P)).then_inc(s_wq, 16)
            sp.dma_start(bq_c, bq.rearrange("(c p) -> p c", p=P), allow_slow_non_contiguous=True).then_inc(s_wq, 16)
            load_transposed(0)
            for w, dst in ((Wk, wk), (Wv, wv), (Wp, wp)):
                sp.dma_start(dst, w.rearrange("(c p) n -> p c n", p=P)).then_inc(s_wlin, 16)
            sp.dma_start(bkv_b[:, 0:DIM], bk.partition_broadcast(P)).then_inc(s_wlin, 16)
            sp.dma_start(bkv_b[:, DIM:2 * DIM], bv.partition_broadcast(P)).then_inc(s_wlin, 16)
            sp.dma_start(bp_b, bp.partition_broadcast(P)).then_inc(s_wlin, 16)
            load_rows(0)
            for n, (w, _, k, c) in enumerate(raw_w):
                if n >= 4:
                    sp.wait_ge(s_wcvt, n - 3)
                sp.dma_start(stage_w[0][:, (n % 4) * 512:(n % 4) * 512 + 512],
                             w[k * P:(k + 1) * P, c * 512:(c + 1) * 512]).then_inc(s_wraw[n % 4], 16)
            sp.dma_start(wO, WO.rearrange("(c p) n -> p c n", p=P)).then_inc(s_wo, 16)
            sp.dma_start(wg, WgT.rearrange("(c p) n -> p c n", p=P)).then_inc(s_wo, 16)
            sp.dma_start(bQ_c, bQ.rearrange("(c p) -> p c", p=P), allow_slow_non_contiguous=True).then_inc(s_wo, 16)
            sp.dma_start(bK_c, bK.rearrange("(c p) -> p c", p=P), allow_slow_non_contiguous=True).then_inc(s_wo, 16)
            sp.dma_start(bV_b, bV.partition_broadcast(P)).then_inc(s_wo, 16)
            sp.dma_start(bO_b, bO.partition_broadcast(P)).then_inc(s_wo, 16)
            sp.dma_start(w1_sb[:, :].rearrange("p (e c f) -> p e c f", e=NE, c=DC),
                         W1T.rearrange("e (c p) f -> p e c f", p=P)).then_inc(s_w1, 16)

            def store_x2(i):
                sp.wait_ge(d_x2, at(i, TT, TT))
                sp.dma_start(x2_d[ds(i * SEQ, SEQ), :].rearrange("(a p) d -> p a d", p=P), x1_s).then_inc(s_x2out, 16)

            sp.wait_ge(g_cq, 1)
            load_transposed(1)
            sp.wait_ge(g_res2, 1)
            load_rows(1)
            with sp.Fori(2, NB) as i:
                sp.wait_ge(s_const, 16)
                sp.wait_ge(g_cq, i)
                load_transposed(i)
                store_x2(i - 2)
                sp.wait_ge(g_res2, i)
                load_rows(i)
            store_x2(NB - 2)

            sp.wait_ge(x7, last_round().number("V", PAIRS - 1) + 1)
            sp.dma_start(w2_sb.rearrange("p (e c f) -> p e c f", e=NE, c=DC),
                         W2T.rearrange("e (c p) f -> p e c f", p=P)).then_inc(s_w23, 16)

            def load_w3(a, b):
                sp.dma_start(w3_sb[:, a * FC * DIM:b * FC * DIM].rearrange("p (e c f) -> p e c f", e=b - a, c=FC),
                             W3T[a:b].rearrange("e (c p) f -> p e c f", p=P)).then_inc(s_w23, 16)

            load_w3(0, W3_EARLY)
            store_x2(NB - 1)
            sp.wait_ge(x7, PRODUCTS)
            sp.wait_ge(s_x2out, 16 * NB)
            load_w3(W3_EARLY, NE)
            sp.dma_start(b1_b, b1.partition_broadcast(P)).then_inc(s_w23, 16)
            sp.dma_start(b2_b, b2.partition_broadcast(P)).then_inc(s_w23, 16)
            sp.dma_start(b3_b, b3.partition_broadcast(P)).then_inc(s_w23, 16)

            sp.wait_ge(m_out[0], 16 * ((MOE_TILES + 1) // 2))
            sp.wait_ge(m_out[1], 16 * (MOE_TILES // 2))

            def load_mix(i):
                a, n, h = i * GT * P, GT * P, i % DEPTH
                sp.dma_start(yy[:, h], y_d[a * TOPK:(a + n) * TOPK, :]
                             .rearrange("(a p j) d -> p a (j d)", p=P, j=TOPK)).then_inc(c_in[h], 16)
                sp.dma_start(xx[:, h], x2_d[a:a + n, :].rearrange("(a p) d -> p a d", p=P)).then_inc(c_in[h], 16)

            for i in range(DEPTH):
                load_mix(i)
            for i in range(GROUPS):
                if i + DEPTH < GROUPS:
                    sp.wait_ge(c_pre, GT * (i + 1))
                    load_mix(i + DEPTH)
                sp.wait_ge(c_o, GT * (i + 1))
                sp.dma_start(out[i * GT * P:(i + 1) * GT * P, :].rearrange("(a p) d -> p a d", p=P), oo[:, i % 2]).then_inc(s_out[i % 2], 16)
            sp.wait_ge(s_out[0], 16 * GROUPS // 2)
            sp.wait_ge(s_out[1], 16 * GROUPS // 2)

        @block.tensor
        def _(pe):
            mm = nc.tensor.matmul

            B7 = PS[:, 7, :]

            def q_features(r, m):
                pe.wait_ge(s_xT, at(r.i, 16, 32))
                for k in range(DC):
                    last = mm(B7, wq[:, k, m * P:(m + 1) * P], xT_s[:, k, :], start=k == 0, stop=k == DC - 1)
                return last

            def kv_rows(r, t):
                pe.wait_ge(s_xT, at(r.i, 16, 32))
                for n, w in enumerate((wk, wv)):
                    for k in range(DC):
                        last = mm(B7[:, n * DIM:(n + 1) * DIM], xT_s[:, k, t * P:(t + 1) * P], w[:, k, :],
                                  start=k == 0, stop=k == DC - 1)
                return last

            def vTk(r):
                pe.wait_ge(d_kf, at(r.i, TT, 2 * TT))
                for g in range(DC):
                    for t in range(TT):
                        last = mm(B7[:, g * P:(g + 1) * P], kv_s[:, t, DIM + g * P:DIM + (g + 1) * P],
                                  kv_s[:, t, g * P:(g + 1) * P], start=t == 0, stop=t == TT - 1)
                return last

            def vTkWp(r):
                for g in range(DC):
                    last = mm(B7[:, g * DIM:(g + 1) * DIM], bd_s[:, g, :], wp[:, g, :], start=True, stop=True)
                return last

            def lin_rows(r, n):
                pe.wait_ge(d_qf, at(r.i, DC, 2 * DC))
                for t in (2 * n, 2 * n + 1):
                    for g in range(DC):
                        last = mm(B7[:, (t % 2) * DIM:(t % 2 + 1) * DIM], q_s[:, g, t * P:(t + 1) * P],
                                  m_s[:, g, :], start=g == 0, stop=g == DC - 1)
                return last

            def x1T(r, k):
                wait_alone(pe, d_xq, at(r.i, TT, 2 * TT))
                for t in range(TT):
                    last = mm(B7[:, t * P:(t + 1) * P], x1q_s[:, t, k * P:(k + 1) * P], ident_b[:, :], start=True, stop=True)
                return last

            def proj_k(r, p):
                if p == 0:
                    pe.wait_ge(g_cq, at(r.i, 1, 2))
                for k in range(DC):
                    last = mm(B7, wK[:, k, p * P:(p + 1) * P], cq_s[:, k, :], start=k == 0, stop=k == DC - 1)
                return last

            def proj_q(r, p):
                for k in range(DC):
                    last = mm(B7, wQ[:, k, p * P:(p + 1) * P], x1qT_s[:, k, :], start=k == 0, stop=k == DC - 1)
                return last

            def proj_v(r, p):
                for t in range(TT):
                    for k in range(DC):
                        last = mm(B7[:, t * P:(t + 1) * P], cq_s[:, k, t * P:(t + 1) * P], wV[:, k, p * P:(p + 1) * P],
                                  start=k == 0, stop=k == DC - 1)
                return last

            def out_rows(r, t):
                pe.wait_ge(a_z, at(r.i, PAIRS, 0))
                for p in range(PAIRS):
                    last = mm(B7[:, 0:DIM], ZT[:, p, t * P:(t + 1) * P], wO[:, p, :], start=p == 0, stop=p == PAIRS - 1)
                return last

            def x2T(r, k):
                pe.wait_ge(d_x2, at(r.i, TT, 0))
                for t in range(TT):
                    last = nc.tensor.transpose(B7[:, t * P:(t + 1) * P], x1_s[:, t, k * P:(k + 1) * P], ident)
                return last

            def gate(r):
                for t in range(TT):
                    for k in range(DC):
                        last = mm(B7[:, t * NE:(t + 1) * NE], x2T_s[:, k, t * P:(t + 1) * P], wg[:, k, :],
                                  start=k == 0, stop=k == DC - 1)
                return last

            def product(r, job, k):
                if r.tail or r.number(job, k) > 0:
                    pe.wait_ge(x7, r.number(job, k))
                if job == "K":
                    last = proj_k(r, k)
                elif job == "Q":
                    last = proj_q(r, k)
                elif job == "V":
                    last = proj_v(r, k)
                elif job == "wo":
                    last = out_rows(r, k)
                elif job == "x2T":
                    last = x2T(r, k)
                elif job == "gate":
                    last = gate(r)
                elif job == "q":
                    last = q_features(r, k)
                elif job == "kv":
                    last = kv_rows(r, k)
                elif job == "vTk":
                    last = vTk(r)
                elif job == "vTkWp":
                    last = vTkWp(r)
                elif job == "y":
                    last = lin_rows(r, k)
                else:
                    last = x1T(r, k)
                last.then_inc(p7, 1)

            def scores(r, u):
                p, t, e = unit(u)
                n = (t + 1) * P
                if u % (2 * TT) == 0:
                    pe.wait_ge(x7, r.number("Q", p % PAIRS) + 1)
                wait_past(pe, a_e, r.i, UNITS, u - 3)
                bank = u % 4
                for n_part, (q_part, k_part) in enumerate(((QH, KH), (QH, KL), (QL, KH))):
                    mm(PS[:, bank, 0:n], q_part[e * HD:(e + 1) * HD, p % 2, t * P:(t + 1) * P],
                       k_part[e * HD:(e + 1) * HD, p % 2, 0:n], start=n_part == 0, stop=False)
                mm(PS[:, bank, n - P:n], ident_b[:, :], causal_b[:, :], start=False, stop=True).then_inc(p_s, 1)

            def transposes(r, u):
                p, t, e = unit(u)
                pe.wait_ge(g_n, at(r.i, UNITS, u + 1))
                wait_past(pe, (a_t, d_t)[e], r.i, UNITS // 2, u // 2)
                for j in range(t + 1):
                    last = nc.tensor.transpose(PS[:, 4 + e, j * P:(j + 1) * P], pnorm[:, u % 4, j * P:(j + 1) * P], ident)
                last.then_inc(p_t, 1)

            def weighted(r, p):
                pe.wait_ge(a_t, at(r.i, UNITS // 2, TT * (p + 1)))
                pe.wait_ge(d_t, at(r.i, UNITS // 2, TT * (p + 1)))
                pe.wait_ge(x7, r.number("V", p) + 1 if p >= 1 else r.base)
                wait_past(pe, a_z, r.i, PAIRS, p)
                for j in range(TT):
                    for e in range(2):
                        last = mm(PS[e * HD:(e + 1) * HD, 6, j * P:SEQ], V_s[:, p % 2, j, e * HD:(e + 1) * HD],
                                  PT[2 * (p % 2) + e][:, j, j * P:SEQ], start=j == 0, stop=j == TT - 1)
                last.then_inc(p_z, 1)

            def run(r):
                for u in range(UNITS):
                    p, n = divmod(u, 2 * TT)
                    if u + 4 < UNITS or r.ahead:
                        scores(r, u + 4)
                    transposes(r, u)
                    if n == 1 and (p >= 1 or r.tail):
                        weighted(r, p - 1)
                    for job, k in r.slot(u):
                        product(r, job, k)

            pe.wait_ge(s_wq, 16 * 2)
            for _, job, k in prologue().table:
                if (job, k) == ("kv", 0):
                    pe.wait_ge(s_wlin, 16 * 6)
                elif (job, k) == ("x1T", 0):
                    pe.wait_ge(s_cb, 3)
                elif (job, k) == ("K", 0):
                    pe.wait_ge(s_wo, 16 * 6)
                    pe.wait_ge(s_const, 16)
                    pe.wait_ge(s_wscaled, 1)
                    pe.wait_ge(s_wcvt, N_WRAW)
                product(prologue(), job, k)
            for u in range(4):
                scores(prologue(), UNITS + u)
            run(first_round())
            with pe.Fori(1, NB - 1) as i:
                run(middle_round(i))
            run(last_round())
            weighted(epilogue(), -1)
            for _, job, k in epilogue().table:
                product(epilogue(), job, k)

            pe.wait_ge(r_hot, 1)
            mm(PS[:, 0, 0:ROWTILES * NE], tri_b[:, :], both_b, start=True, stop=True)
            mm(PS[:, 1, 0:ROWTILES * NE], ones_b[:, :], both_b, start=True, stop=True).then_inc(r_pre, 1)
            for c in range(ROWTILES * TOPK // HOT):
                pe.wait_ge(r_lane, c + 1)
                pe.wait_ge(r_low, c + 1)
                pe.wait_ge(r_high, c + 1)
                for m in range(HOT):
                    last = mm(PS[:, 2, 0:2 * LIST_COLS], lane_hot[:, c % 2, m, :], code_hot[:, c % 2, m, :],
                              start=c == 0 and m == 0, stop=(c + 1) * HOT + m == ROWTILES * TOPK + HOT - 1)
                last.then_inc(r_list, 1)

            def expert_of(s):
                return pe.value_load(expert[0:1, ds(s, 1)], min_val=0, max_val=NE - 1)

            def tokensT(s, nth, h):
                pe.wait_ge(m_in[h], at(nth, 16, 16))
                for k in range(DC):
                    last = nc.tensor.transpose(PS[:, 0, k * P:(k + 1) * P], xg[:, h, k * P:(k + 1) * P], ident)
                last.then_inc(m_xt, 1)

            def up(s, h, bank, w, done):
                e = expert_of(s)
                for k in range(DC):
                    last = mm(PS[:, bank + h, :], xgT[:, h, k * P:(k + 1) * P], w[:, ds(e * (DC * FF) + k * FF, FF)],
                              start=k == 0, stop=k == DC - 1)
                last.then_inc(done, 1)

            def up_g(s, nth, h):
                pe.wait_ge(m_xs, at(s, 1, 1))
                up(s, h, 1, w1_sb, m_g)

            def up_v(s, nth, h):
                up(s, h, 3, w2_sb, m_v)

            def hiddenT(s, nth, h):
                pe.wait_ge(m_h, at(s, 1, 1))
                for f in range(FC):
                    last = nc.tensor.transpose(PS[:, 5, f * P:(f + 1) * P], h_s[:, h, f * P:(f + 1) * P], ident)
                last.then_inc(m_ht, 1)

            def down(s, nth, h, bank_read, value):
                e = expert_of(s)
                pe.wait_ge(bank_read, value)
                pe.wait_ge(m_hs, at(s, 1, 1))
                for f in range(FC):
                    last = mm(PS[:, 6, 0:DIM], hT_s[:, f * P:(f + 1) * P], w3_sb[:, ds(e * (FC * DIM) + f * DIM, DIM)],
                              start=f == 0, stop=f == FC - 1)
                last.then_inc(m_o, 1)

            pe.wait_ge(r_tab, 1)
            pe.wait_ge(s_w1, 16)
            pe.wait_ge(s_w23, 16 * 6)
            tokensT(*tile(0, 0))
            up_g(*tile(0, 0))
            tokensT(*tile(0, 1))
            up_v(*tile(0, 0))
            with pe.Fori(0, (MOE_TILES - 1) // 2) as u:
                for k in (1, 2):
                    up_g(*tile(u, k))
                    hiddenT(*tile(u, k - 1))
                    tokensT(*tile(u, k + 1))
                    up_v(*tile(u, k))
                    down(*tile(u, k - 1), m_xs, at(tile(u, k + 1)[0], 1, 1))
            hiddenT(*tile(0, MOE_TILES - 1))
            down(*tile(0, MOE_TILES - 1), m_yo, MOE_TILES - 1)

        @block.scalar
        def _(act):
            A = nc.scalar.activation

            B7 = PS[:, 7, :]

            def read(r, job, k):
                if job not in ("K", "Q", "x1T", "x2T", "q", "vTkWp"):
                    return
                if job == "q" and k > 0:
                    act.wait_ge(d_qf, at(r.i, DC, DC + k))
                act.wait_ge(p7, r.number(job, k) + 1)
                if job == "K":
                    A(KH[:, k % 2, :], B7, ACT.Identity, bias=bK_c[:, k:k + 1]).then_inc(a_h, 1)
                elif job == "Q":
                    A(QH[:, k % 2, :], B7, ACT.Identity, bias=nbQ[:, k:k + 1]).then_inc(a_h, 1)
                elif job == "x1T":
                    A(x1qT_s[:, k, :], B7, ACT.Copy).then_inc(x7, 1)
                elif job == "x2T":
                    A(x2T_s[:, k, :], B7, ACT.Copy).then_inc(x7, 1)
                elif job == "vTkWp":
                    A(m_s.rearrange("p a b -> p (a b)"), B7, ACT.Copy).then_inc(x7, 1)
                else:
                    A(q_s[:, k, :], B7, ACT.Exp, bias=bq_c[:, k:k + 1])
                    A(rq_s, B7, ACT.Relu, bias=bq_c[:, k:k + 1]).then_inc(x7, 1)

            def k_exp_relu(r, t):
                act.wait_ge(x7, r.number("kv", t) + 1)
                wait_past(act, d_kf, r.i, TT, TT + t)
                A(ek_s, kv_s[:, t, 0:DIM], ACT.Exp)
                A(rk_s, kv_s[:, t, 0:DIM], ACT.Relu).then_inc(a_k, 1)

            def exps(r, u):
                n = (unit(u)[1] + 1) * P
                wait_past(act, g_n, r.i, UNITS, u - 3)
                act.wait_ge(d_min, at(r.i, UNITS, u + 1))
                A(prob[:, u % 4, 0:n], PS[:, u % 4, 0:n], ACT.Exp, bias=smin[:, u % 4:u % 4 + 1], scale=-1.0,
                  accum_out=ssum[:, u % 4:u % 4 + 1]).then_inc(a_e, 1)

            def z_rows(r, p):
                act.wait_ge(p_z, at(r.i, PAIRS, p + 1))
                if p == 0 and r.tail:
                    act.wait_ge(p7, r.number("wo", TT - 1) + 1)
                A(ZT[:, p % PAIRS, :], PS[:, 6, :], ACT.Copy).then_inc(a_z, 1)

            def run(r):
                for u in range(UNITS):
                    p, t, e = unit(u)
                    for job, k in r.slot(u - 1):
                        read(r, job, k)
                    if e == 0:
                        act.wait_ge(p_t, at(r.i, UNITS, u + 1))
                        A(PT[2 * (p % 2)][:, 0:t + 1, t * P:(t + 1) * P],
                          PS[:, 4, 0:(t + 1) * P].rearrange("p (a b) -> p a b", b=P), ACT.Copy).then_inc(a_t, 1)
                    if u + 4 < UNITS or r.ahead:
                        exps(r, u + 4)
                    if u % (2 * TT) == 2 and (p >= 1 or r.tail):
                        z_rows(r, p - 1)
                    for job, k in r.slot(u - 2):
                        if job == "kv":
                            k_exp_relu(r, k)

            act.wait_ge(s_wq, 16 * 2)
            for _, job, k in prologue().table:
                if (job, k) == ("K", 0):
                    act.wait_ge(s_wo, 16 * 6)
                    A(nbQ, bQ_c, ACT.Copy, scale=-1.0 / HD ** 0.5).then_inc(s_nbQ, 1)
                    act.wait_ge(s_nbQ, 1)
                read(prologue(), job, k)
                if job == "kv":
                    k_exp_relu(prologue(), k)
            for u in range(4):
                exps(prologue(), UNITS + u)
            run(first_round())
            with act.Fori(1, NB - 1) as i:
                run(middle_round(i))
            run(last_round())
            z_rows(epilogue(), -1)
            for _, job, k in epilogue().table:
                read(epilogue(), job, k)

            act.wait_ge(r_d, 3)
            A(gates[:, 1, :], choice[:, 0, :], ACT.Exp).then_inc(r_e, 1)

            for c in range(ROWTILES * TOPK // HOT):
                low = C_LANE + 2 + c * HOT // ROWTILES
                if c >= 2:
                    act.wait_ge(r_list, c - 1)
                act.wait_ge(r_tile, c + 1)
                A(code_hot[:, c % 2, :, 0:LIST_COLS], tile_hot[:, c % 2], ACT.Copy, scale=cst[:, low:low + 1]).then_inc(r_low, 1)

            def silu(s, nth, h):
                act.wait_ge(m_gb, at(s, 1, 1))
                A(silu_s[:, h, :], g_s[:, h, :], ACT.Silu).then_inc(m_si_, 1)

            def hidden(s, nth, h):
                act.wait_ge(m_ht, at(s, 1, 1))
                A(hT_s, PS[:, 5, :], ACT.Copy).then_inc(m_hs, 1)

            silu(*tile(0, 0))
            with act.Fori(0, (MOE_TILES - 1) // 2) as u:
                for k in (1, 2):
                    hidden(*tile(u, k - 1))
                    silu(*tile(u, k))
            hidden(*tile(0, MOE_TILES - 1))

            for i in range(GROUPS):
                act.wait_ge(c_in[i % DEPTH], 32 * (i // DEPTH + 1))
                if i >= DEPTH:
                    act.wait_ge(c_o, GT * (i - DEPTH + 1))
                for t in range(GT):
                    A(zz[:, i % DEPTH, t, :], yy[:, i % DEPTH, t, 0:DIM], ACT.Copy,
                      scale=gates[:, 0, i * GT + t:i * GT + t + 1]).then_inc(c_mix, 1)

        @block.vector
        def _(ve):
            V = nc.vector

            def row_stats(t, pre, st, pre_done, value, done_st):
                ve.wait_ge(pre_done, value)
                V.bn_stats(st[:, t, 0:6], pre[:, t, :]).then_inc(done_st, 1)

            def mean_var(t, st, mvt, done_st, value, done_mv):
                wait_alone(ve, done_st, value)
                V.bn_aggr(mvt[:, t, :], st[:, t, 0:6]).then_inc(done_mv, 1)

            B7 = PS[:, 7, :]

            def read(r, job, k):
                if job not in ("K", "Q", "V", "wo", "gate", "kv", "vTk", "y"):
                    return
                if job in ("K", "Q"):
                    high, low, bias = (KH, KL, bK_c) if job == "K" else (QH, QL, nbQ)
                    done = 2 * k + (job == "Q") + 1 + (2 * PAIRS if k == 0 or (job, k) == ("K", 1) else 0)
                    ve.wait_ge(a_h, at(r.i, 2 * PAIRS, done))
                    V.scalar_tensor_tensor(low[:, k % 2, :], B7, bias[:, k:k + 1], high[:, k % 2, :].bitcast(F32),
                                           ALU.add, ALU.subtract).then_inc(x7, 1)
                    return
                if job == "wo":
                    ve.wait_ge(g_res2, at(r.i, 1, 0))
                if job == "y":
                    ve.wait_ge(g_res, at(r.i, 1, 2))
                ve.wait_ge(p7, r.number(job, k) + 1)
                if job == "V":
                    V.tensor_tensor(V_s[:, k % 2], B7.rearrange("p (a b) -> p a b", b=P),
                                    bV_b[:, k * P:(k + 1) * P].unsqueeze(1).to_broadcast([P, TT, P]), ALU.add).then_inc(x7, 1)
                elif job == "wo":
                    V.tensor_tensor(x1_s[:, k, :], B7[:, 0:DIM], x1_s[:, k, :], ALU.add).then_inc(x7, 1)
                elif job == "gate":
                    V.tensor_copy(logits[:, ds(r.i * TT - TT, TT), :], B7[:, 0:TT * NE].rearrange("p (a b) -> p a b", b=NE))\
                     .then_inc(x7, 1)
                elif job == "kv":
                    V.tensor_tensor(kv_s[:, k, :], B7, bkv_b, ALU.add).then_inc(x7, 1)
                elif job == "vTk":
                    V.tensor_tensor(bd_s, B7[:, 0:DIM].rearrange("p (a b) -> p a b", b=P),
                                    cst[:, C_BLOCK:C_BLOCK + P].unsqueeze(1).to_broadcast([P, DC, P]), ALU.mult).then_inc(x7, 1)
                else:
                    V.tensor_tensor(xr_s[:, 2 * k:2 * k + 2, :], B7.rearrange("p (a b) -> p a b", b=DIM),
                                    xr_s[:, 2 * k:2 * k + 2, :], ALU.add).then_inc(x7, 1)

            def q_feature(r, m):
                ve.wait_ge(x7, r.number("q", m) + 1)
                V.scalar_tensor_tensor(q_s[:, m, :], q_s[:, m, :], 1.0, rq_s, ALU.min, ALU.add).then_inc(d_qf, 1)

            def k_feature(r, t):
                ve.wait_ge(a_k, at(r.i, TT, TT + t + 1))
                V.scalar_tensor_tensor(kv_s[:, t, 0:DIM], ek_s, 1.0, rk_s, ALU.min, ALU.add).then_inc(d_kf, 1)

            def context_magic(r):
                ve.wait_ge(s_cT, at(r.i, 16, 32))
                wait_past(ve, g_cq, r.i, 1, 1)
                V.tensor_scalar(qm_s.bitcast(U32), cT_s.bitcast(U32), 0x7F800000, None, ALU.bitwise_and).then_inc(d_ce, 1)
                ve.wait_ge(d_ce, at(r.i, 1, 2))
                V.tensor_scalar(qm_s, qm_s, 2.0 ** -6, 1.5 * 2.0 ** 20, ALU.max, ALU.mult).then_inc(d_cm, 1)

            def lin_stats(r, t):
                row_stats(t, xr_s, stats1, x7, r.number("y", t // 2) + 1, d_st)

            def lin_mean_var(r):
                for t in range(TT):
                    mean_var(t, stats1, mv1, d_st, at(r.ahead_norm, TT, t + 1), d_mv)

            def x1q_rows(r, half):
                if half == 0:
                    wait_alone(ve, g_rs, at(r.ahead_norm, 1, 1))
                for t in (2 * half, 2 * half + 1):
                    V.tensor_scalar(x1q_s[:, t, :], xr_s[:, t, :], mv1[:, t, 0:1], rstd1[:, t:t + 1], ALU.subtract, ALU.mult,
                                    saturate=False).then_inc(d_xq, 1)

            def out_stats(r, t):
                row_stats(t, x1_s, stats, x7, r.number("wo", t) + 1, d_st)

            def out_mean_var(r):
                for t in range(TT):
                    mean_var(t, stats, mv, d_st, at(r.tail_norm, TT, t + 1), d_mv)

            def x2_rows(r, half):
                if half == 0:
                    ve.wait_ge(g_rs, at(r.tail_norm, 1, 1))
                for t in (2 * half, 2 * half + 1):
                    V.tensor_scalar(x1_s[:, t, :], x1_s[:, t, :], mv[:, t, 0:1], rstd[:, t:t + 1], ALU.subtract, ALU.mult)\
                     .then_inc(d_x2, 1)

            def x1_rows(r, half):
                if r.tail and half == 0:
                    wait_alone(ve, s_x2out, at(r.i, 16, 0))
                for t in (2 * half, 2 * half + 1):
                    V.tensor_scalar(x1_s[:, t, :], xr_s[:, t, :], mv1[:, t, 0:1], rstd1[:, t:t + 1], ALU.subtract, ALU.mult)\
                     .then_inc(d_x1, 1)

            def row_min(r, u):
                n = (unit(u)[1] + 1) * P
                ve.wait_ge(p_s, at(r.i, UNITS, u + 1))
                V.tensor_reduce(smin[:, u % 4:u % 4 + 1], PS[:, u % 4, 0:n], AX_X, ALU.min).then_inc(d_min, 1)

            def row_inv(r, u):
                ve.wait_ge(a_e, at(r.i, UNITS, u + 1))
                V.reciprocal(sinv[:, u % 4:u % 4 + 1], ssum[:, u % 4:u % 4 + 1]).then_inc(d_inv, 1)

            def run(r):
                for u in range(UNITS):
                    p, t, e = unit(u)
                    if u + 2 < UNITS or r.ahead:
                        row_inv(r, u + 2)
                    for job, k in r.slot(u - 1):
                        if job not in ("K", "Q"):
                            read(r, job, k)
                    if u + 4 < UNITS or r.ahead:
                        row_min(r, u + 4)
                    if e == 1:
                        ve.wait_ge(p_t, at(r.i, UNITS, u + 1))
                        V.tensor_copy(PT[2 * (p % 2) + 1][:, 0:t + 1, t * P:(t + 1) * P],
                                      PS[:, 5, 0:(t + 1) * P].rearrange("p (a b) -> p a b", b=P)).then_inc(d_t, 1)
                    for job, k in r.slot(u - 1):
                        if job in ("K", "Q"):
                            read(r, job, k)
                    for job, k in r.slot(u - 2):
                        if job == "wo":
                            out_stats(r, k)
                        elif job == "q":
                            q_feature(r, k)
                        elif job == "y":
                            lin_stats(r, 2 * k)
                            lin_stats(r, 2 * k + 1)
                    for job, k in r.slot(u - 3):
                        if job == "kv":
                            k_feature(r, k)
                    if r.tail and u == 12:
                        out_mean_var(r)
                    if r.tail and u in (14, 15):
                        x2_rows(r, u - 14)
                    if r.ahead and u == 33:
                        context_magic(r)
                    if r.ahead and u == 47:
                        lin_mean_var(r)
                    if r.ahead and u in (49, 50):
                        x1q_rows(r, u - 49)
                    if u in (22, 23):
                        x1_rows(r, u - 22)

            ve.wait_ge(s_const, 16)
            V.tensor_copy(ident_b[:, :], ident)
            V.tensor_copy(causal_b[:, :], cst[:, C_CAUSAL:C_CAUSAL + P]).then_inc(s_cb, 1)
            V.memset(ones_b[:, :], 1.0).then_inc(s_cb, 1)
            V.tensor_copy(tri_b[:, :], cst[:, C_TRI:C_TRI + P]).then_inc(s_cb, 1)
            raw_bits, magic = stage_w[0], stage_w[1]

            def round_weights(n):
                _, wt, k, c = raw_w[n]
                q = (n % 4) * 512
                m = (n % 2) * 1024
                ve.wait_ge(s_wraw[n % 4], 16 * (n // 4 + 1))
                V.tensor_scalar(magic[:, m:m + 512].bitcast(U32), raw_bits[:, q:q + 512].bitcast(U32), 0x7F800000, None,
                                ALU.bitwise_and).then_inc(s_wexp, 1)
                ve.wait_ge(s_wexp, n + 1)
                V.tensor_scalar(magic[:, m + 512:m + 1024], magic[:, m:m + 512], 2.0 ** -6, 1.5 * 2.0 ** 20, ALU.max, ALU.mult)\
                 .then_inc(s_wmag, 1)
                ve.wait_ge(s_wmag, n + 1)
                V.tensor_tensor(magic[:, m:m + 512], raw_bits[:, q:q + 512], magic[:, m + 512:m + 1024], ALU.add).then_inc(s_wadd, 1)
                ve.wait_ge(s_wadd, n + 1)
                V.tensor_tensor(wt[:, k, c * 512:(c + 1) * 512], magic[:, m:m + 512], magic[:, m + 512:m + 1024], ALU.subtract)\
                 .then_inc(s_wcvt, 1)

            ve.wait_ge(s_wlin, 16 * 6)
            r = prologue()
            context_magic(r)
            for n, (_, job, k) in enumerate(r.table):
                if (job, k) == ("K", 0):
                    ve.wait_ge(s_wo, 16 * 6)
                elif job == "Q":
                    ve.wait_ge(s_nbQ, 1)
                read(r, job, k)
                if job == "q":
                    q_feature(r, k)
                if job == "kv" and k > 0:
                    k_feature(r, k - 1)
                    if k == TT - 1:
                        k_feature(r, k)
                if job == "y":
                    lin_stats(r, 2 * k)
                    lin_stats(r, 2 * k + 1)
                    if k == 1:
                        lin_mean_var(r)
                        x1q_rows(r, 0)
                        x1q_rows(r, 1)
                if n < N_WRAW:
                    round_weights(n)
                if n == 2 * N_WRAW // 3:
                    ve.wait_ge(s_wcvt, n)
                    V.tensor_scalar(wQ, wQ, -1.0 / HD ** 0.5, None, ALU.mult).then_inc(s_wscaled, 1)
            for u in range(4):
                row_min(r, UNITS + u)
            for u in range(2):
                row_inv(r, UNITS + u)
            run(first_round())
            with ve.Fori(1, NB - 1) as i:
                run(middle_round(i))
            run(last_round())
            r = epilogue()
            for _, job, k in r.table:
                read(r, job, k)
                if job == "wo":
                    out_stats(r, k)
                    if k == TT - 1:
                        out_mean_var(r)
                        x2_rows(r, 0)
                        x2_rows(r, 1)

            step = [0]

            def done(ins):
                ins.then_inc(r_d, 1)
                step[0] += 1
                ve.wait_ge(r_d, step[0])

            ve.wait_ge(x7, PRODUCTS)
            for t in range(ROWTILES):
                last = V.max(top[:, t, :], logits[:, t, :])
            done(last)
            for t in range(ROWTILES):
                last = V.max_index(topi[:, t, :], top[:, t, :], logits[:, t, :])
            done(last)
            done(V.tensor_tensor(choice[:, 0, :], top[:, :, 1], top[:, :, 0], ALU.subtract))
            ve.wait_ge(r_e, 1)
            done(V.tensor_scalar(gates[:, 0, :], gates[:, 1, :], 1.0, None, ALU.add))
            done(V.reciprocal(slot[:, 0, :], gates[:, 0, :]))
            done(V.tensor_copy(gates[:, 0, :], slot[:, 0, :]))
            done(V.tensor_tensor(slot[:, 1, :], gates[:, 1, :], slot[:, 0, :], ALU.mult))
            done(V.tensor_copy(gates[:, 1, :], slot[:, 1, :]))
            done(V.tensor_copy(choice, topi[:, :, 0:TOPK].rearrange("p t j -> p j t")))
            iota_e = cst[:, C_IOTA:C_IOTA + NE].unsqueeze(1).to_broadcast([P, ROWTILES, NE])
            hot = [onehot[:, j, :].rearrange("p (t e) -> p t e", e=NE) for j in range(TOPK)]
            for j in range(TOPK):
                done(V.tensor_tensor(hot[j], iota_e, choice[:, j, :].unsqueeze(2).to_broadcast([P, ROWTILES, NE]), ALU.is_equal))
            V.tensor_tensor(both_b, onehot[:, 0, :], onehot[:, 1, :], ALU.add).then_inc(r_hot, 1)
            ve.wait_ge(r_pre, 1)
            done(V.tensor_copy(run_a, PS[:, 1, 0:ROWTILES * NE].rearrange("p (t e) -> p t e", e=NE)))
            a, b = run_a, run_b
            d = 1
            while d < ROWTILES:
                V.tensor_copy(b[:, 0:d, :], a[:, 0:d, :])
                done(V.tensor_tensor(b[:, d:, :], a[:, d:, :], a[:, 0:ROWTILES - d, :], ALU.add))
                a, b = b, a
                d *= 2
            done(V.tensor_scalar(etiles, a[:, ROWTILES - 1, :], float(P - 1), None, ALU.add))
            done(V.tensor_copy(etiles_i, etiles))
            done(V.tensor_scalar(etiles_i, etiles_i, 7, None, ALU.logical_shift_right))
            done(V.tensor_copy(etiles, etiles_i))
            done(V.tensor_copy(cum_a, etiles))
            ca, cb = cum_a, cum_b
            d = 1
            while d < NE:
                V.tensor_copy(cb[:, 0:d], ca[:, 0:d])
                done(V.tensor_tensor(cb[:, d:], ca[:, d:], ca[:, 0:NE - d], ALU.add))
                ca, cb = cb, ca
                d *= 2
            done(V.tensor_tensor(past, cst[:, C_IOTA:C_IOTA + LIST_COLS].unsqueeze(2).to_broadcast([P, LIST_COLS, NE]),
                                 ca.unsqueeze(1).to_broadcast([P, LIST_COLS, NE]), ALU.is_ge))
            done(V.tensor_reduce(expert_f, past, AX_X, ALU.add))
            done(V.tensor_scalar(expert_f, expert_f, float(NE - 1), None, ALU.min))
            done(V.tensor_copy(expert[:, :], expert_f))
            done(V.tensor_tensor(cb, ca, etiles, ALU.subtract))
            done(V.tensor_scalar(cb, cb, float(P), None, ALU.mult))
            done(V.tensor_tensor(before, a, PS[:, 1, 0:ROWTILES * NE].rearrange("p (t e) -> p t e", e=NE), ALU.subtract))
            done(V.tensor_tensor(before, before, PS[:, 0, 0:ROWTILES * NE].rearrange("p (t e) -> p t e", e=NE), ALU.add))
            done(V.tensor_tensor(before, before, cb.unsqueeze(1).to_broadcast([P, ROWTILES, NE]), ALU.add))
            for j in range(TOPK):
                done(V.tensor_tensor(hot[j], hot[j], before, ALU.mult))
                done(V.tensor_reduce(slot[:, j, :], hot[j], AX_X, ALU.add))
            flat = slot.rearrange("p j t -> p (j t)")
            done(V.tensor_copy(slot_i, flat))
            done(V.tensor_scalar(tile_i, slot_i, 7, None, ALU.logical_shift_right))
            done(V.tensor_scalar(lane_i, slot_i, P - 1, None, ALU.bitwise_and))
            done(V.tensor_copy(tile_f, tile_i))
            done(V.tensor_copy(lane_f, lane_i))
            for c in range(ROWTILES * TOPK // HOT):
                cols = slice(c * HOT, (c + 1) * HOT)
                if c >= 2:
                    ve.wait_ge(r_list, c - 1)
                V.tensor_tensor(tile_hot[:, c % 2], cst[:, C_IOTA:C_IOTA + LIST_COLS].unsqueeze(1).to_broadcast([P, HOT, LIST_COLS]),
                                tile_f[:, cols].unsqueeze(2).to_broadcast([P, HOT, LIST_COLS]), ALU.is_equal).then_inc(r_tile, 1)
                V.tensor_tensor(lane_hot[:, c % 2], cst[:, C_IOTA:C_IOTA + P].unsqueeze(1).to_broadcast([P, HOT, P]),
                                lane_f[:, cols].unsqueeze(2).to_broadcast([P, HOT, P]), ALU.is_equal).then_inc(r_lane, 1)
            ve.wait_ge(r_list, ROWTILES * TOPK // HOT)
            done(V.tensor_copy(hi_s, PS[:, 2, LIST_COLS:2 * LIST_COLS]))
            done(V.scalar_tensor_tensor(code, hi_s, float(TOPK * P), PS[:, 2, 0:LIST_COLS], ALU.mult, ALU.add))
            done(V.tensor_scalar(empty, code, 0.0, cst[:, C_LANE + 1:C_LANE + 2], ALU.is_equal, ALU.mult))
            done(V.tensor_scalar(hi_s, code, -1.0, 0.0, ALU.add, ALU.max))
            done(V.tensor_tensor(empty, empty, code, ALU.add))
            done(V.tensor_scalar(empty, empty, -1.0, None, ALU.add))
            done(V.tensor_copy(scatter_l[:, :], empty))
            done(V.tensor_copy(code_i, hi_s))
            done(V.tensor_scalar(gather_l[:, :].bitcast(I32), code_i, 1, None, ALU.logical_shift_right))
            V.tensor_copy(hi_s, expert_f).then_inc(r_tab, 1)

            def expert_of(s):
                return ve.value_load(expert[0:1, ds(s, 1)], min_val=0, max_val=NE - 1)

            def tokensT(s, nth, h):
                ve.wait_ge(m_xt, at(s, 1, 1))
                V.tensor_copy(xgT[:, h, :], PS[:, 0, 0:DIM]).then_inc(m_xs, 1)

            def gate_bias(s, nth, h):
                e = expert_of(s)
                ve.wait_ge(m_g, at(s, 1, 1))
                V.tensor_tensor(g_s[:, h, :], PS[:, 1 + h, :], b1_b[:, ds(e * FF, FF)], ALU.add).then_inc(m_gb, 1)

            def gated(s, nth, h):
                e = expert_of(s)
                ve.wait_ge(m_v, at(s, 1, 1))
                V.tensor_tensor(v_s[:, h, :], PS[:, 3 + h, :], b2_b[:, ds(e * FF, FF)], ALU.add).then_inc(m_vb, 1)
                ve.wait_ge(m_si_, at(s, 1, 1))
                ve.wait_ge(m_vb, at(s, 1, 1))
                V.tensor_tensor(h_s[:, h, :], silu_s[:, h, :], v_s[:, h, :], ALU.mult).then_inc(m_h, 1)

            def rows_out(s, nth, h, wait=True):
                e = expert_of(s)
                ve.wait_ge(m_o, at(s, 1, 1))
                if wait:
                    ve.wait_ge(m_out[h], nth * 16)
                V.tensor_tensor(yo[:, h, :], PS[:, 6, 0:DIM], b3_b[:, ds(e * DIM, DIM)], ALU.add).then_inc(m_yo, 1)

            ve.wait_ge(s_w23, 16 * 6)
            tokensT(*tile(0, 0))
            gate_bias(*tile(0, 0))
            tokensT(*tile(0, 1))
            gated(*tile(0, 0))
            for k in (1, 2):
                gate_bias(*tile(0, k))
                tokensT(*tile(0, k + 1))
                gated(*tile(0, k))
                rows_out(*tile(0, k - 1), wait=False)
            with ve.Fori(1, (MOE_TILES - 1) // 2) as u:
                for k in (1, 2):
                    gate_bias(*tile(u, k))
                    tokensT(*tile(u, k + 1))
                    gated(*tile(u, k))
                    rows_out(*tile(u, k - 1))
            rows_out(*tile(0, MOE_TILES - 1))

            def mix(i):
                h = i % DEPTH
                ve.wait_ge(c_sum, i + 1)
                for t in range(GT):
                    V.scalar_tensor_tensor(zz[:, h, t, :], yy[:, h, t, DIM:2 * DIM], gates[:, 1, i * GT + t:i * GT + t + 1],
                                           zz[:, h, t, :], ALU.mult, ALU.add).then_inc(c_pre, 1)
                for t in range(GT):
                    row_stats(t, zz[:, h], stats4[:, h], c_pre, i * GT + t + 1, c_st)
                for t in range(GT):
                    mean_var(t, stats4[:, h], mv4[:, h], c_st, i * GT + t + 1, c_mv)

            mix(0)
            for i in range(GROUPS):
                h = i % DEPTH
                if i + 1 < GROUPS:
                    mix(i + 1)
                ve.wait_ge(c_rs, i + 1)
                if i >= 2:
                    ve.wait_ge(s_out[i % 2], 16 * (i // 2))
                for t in range(GT):
                    V.tensor_scalar(oo[:, i % 2, t, :], zz[:, h, t, :], mv4[:, h, t, 0:1], rstd4[:, h, t:t + 1], ALU.subtract, ALU.mult)\
                     .then_inc(c_o, 1)

        @block.gpsimd
        def _(po):
            G = nc.gpsimd
            half = cst[:, C_LANE + 4:C_LANE + 8]

            def rsqrt(out_, mvt, ve_sem, n, done):
                G.tensor_scalar(out_, mvt[:, :, 1], EPS, 1.0, ALU.add, ALU.mult).then_inc(ve_sem, 1)
                wait_alone(po, ve_sem, n)
                G.tensor_tensor(out_, out_, half[:, 0:mvt.shape[1]], ALU.pow).then_inc(done, 1)

            po.wait_ge(s_const, 16)
            po.wait_ge(s_wlin, 16 * 6)

            def signal(last, piece, semaphore):
                if piece == TT - 1:
                    last.then_inc(semaphore, 1)

            def quarter(v, n):
                half = SEQ * DC // TT
                return v[:, n * half // SEQ, n * half % SEQ:n * half % SEQ + half]

            def x_plus_bias(r, n):
                if n == 0:
                    po.wait_ge(s_xr, at(r.i, 16, 32))
                signal(G.tensor_tensor(xr_s[:, n, :], xr_s[:, n, :], bp_b, ALU.add), n, g_res)

            def context_add(r, n):
                if n == 0:
                    po.wait_ge(d_cm, at(r.i, 1, 2))
                signal(G.tensor_tensor(quarter(cT_s, n), quarter(cT_s, n), quarter(qm_s, n), ALU.add), n, g_ca)

            def context_subtract(r, n):
                if n == 0:
                    po.wait_ge(g_ca, at(r.i, 1, 2))
                    if r.own:
                        po.wait_ge(p7, r.number("V", PAIRS - 1) + 1)
                signal(G.tensor_tensor(quarter(cq_s, n), quarter(cT_s, n), quarter(qm_s, n), ALU.subtract), n, g_cq)

            def x1_plus_bias(r, n):
                if n == 0:
                    if not r.tail:
                        po.wait_ge(s_wo, 16 * 6)
                    po.wait_ge(d_x1, at(r.i, TT, TT))
                signal(G.tensor_tensor(x1_s[:, n, :], x1_s[:, n, :], bO_b, ALU.add), n, g_res2)

            def lin_rstd(r):
                wait_alone(po, d_mv, at(r.ahead_norm, TT, TT))
                rsqrt(rstd1, mv1, g_ve, at(r.ahead_norm, 1, 1), g_rs)

            def out_rstd(r):
                wait_alone(po, d_mv, at(r.tail_norm, TT, TT))
                rsqrt(rstd, mv, g_ve, at(r.tail_norm, 1, 1), g_rs)

            def run(r):
                for u in range(UNITS):
                    n = (unit(u)[1] + 1) * P
                    wait_alone(po, d_inv, at(r.i, UNITS, u + 1))
                    G.tensor_scalar(pnorm[:, u % 4, 0:n], prob[:, u % 4, 0:n], sinv[:, u % 4:u % 4 + 1], 1.0,
                                    ALU.mult, ALU.mult).then_inc(g_n, 1)
                    if r.tail and u == 13:
                        out_rstd(r)
                    if u in range(24, 28):
                        x1_plus_bias(r, u - 24)
                    if r.ahead and u in range(35, 39):
                        context_add(r, u - 35)
                    if r.ahead and u in range(39, 43):
                        x_plus_bias(r, u - 39)
                    if r.ahead and u == 48:
                        lin_rstd(r)
                    if r.ahead and u == 51:
                        context_subtract(r, 0)
                        context_subtract(r, 1)
                    if r.ahead and u in (52, 53):
                        context_subtract(r, u - 50)

            for n in range(TT):
                x_plus_bias(prologue(), n)
            for n in range(TT):
                context_add(prologue(), n)
            lin_rstd(prologue())
            for n in range(TT):
                context_subtract(prologue(), n)
            run(first_round())
            with po.Fori(1, NB - 1) as i:
                run(middle_round(i))
            run(last_round())
            out_rstd(epilogue())

            def gather(s, nth, h):
                G.tensor_copy(g_idx[:, h:h + 1], gather_l[:, ds(s, 1)]).then_inc(m_gi, 1)
                wait_alone(po, m_gi, at(s, 1, 1))
                G.indirect_dma_start(out=xg[:, h, :], out_offset=None, in_=x2_d,
                                     in_offset=bass.IndirectOffsetOnAxis(ap=g_idx[:, h:h + 1], axis=0)).then_inc(m_in[h], 16)

            def scatter(s, nth, h, first=False, second=False):
                if not (first or second):
                    po.wait_ge(m_out[h], nth * 16)
                G.tensor_copy(s_idx[:, h:h + 1], scatter_l[:, ds(s, 1)]).then_inc(m_si, 1)
                po.wait_ge(m_si, at(s, 1, 1))
                if not first:
                    po.wait_ge(m_out[1 - h], (nth + h) * 16)
                wait_alone(po, m_yo, at(s, 1, 1))
                G.indirect_dma_start(out=y_d, out_offset=bass.IndirectOffsetOnAxis(ap=s_idx[:, h:h + 1], axis=0),
                                     in_=yo[:, h, :], in_offset=None).then_inc(m_out[h], 16)

            def transposed(s, nth, h):
                po.wait_ge(m_xt, at(s, 1, 1))

            for c in range(ROWTILES * TOPK // HOT):
                first = C_CODE + c * HOT % ROWTILES
                if c >= 2:
                    po.wait_ge(r_list, c - 1)
                po.wait_ge(r_tile, c + 1)
                G.tensor_tensor(code_hot[:, c % 2, :, LIST_COLS:], tile_hot[:, c % 2],
                                cst[:, first:first + HOT].unsqueeze(2).to_broadcast([P, HOT, LIST_COLS]),
                                ALU.mult).then_inc(r_high, 1)

            po.wait_ge(r_tab, 1)
            po.wait_ge(s_x2out, 16 * NB)
            gather(*tile(0, 0))
            gather(*tile(0, 1))
            transposed(*tile(0, 0))
            gather(*tile(0, 2))
            for k in (1, 2):
                transposed(*tile(0, k))
                gather(*tile(0, k + 2))
                scatter(*tile(0, k - 1), first=k == 1, second=k == 2)
            with po.Fori(1, (MOE_TILES - 1) // 2) as u:
                for k in (1, 2):
                    transposed(*tile(u, k))
                    gather(*tile(u, k + 2))
                    scatter(*tile(u, k - 1))
            scatter(*tile(0, MOE_TILES - 1))
            po.wait_ge(m_in[0], 16 * ((LIST_COLS + 1) // 2))
            po.wait_ge(m_in[1], 16 * (LIST_COLS // 2))

            def add_x2(i):
                po.wait_ge(c_mix, GT * (i + 1))
                G.tensor_tensor(zz[:, i % DEPTH], zz[:, i % DEPTH], xx[:, i % DEPTH], ALU.add).then_inc(c_sum, 1)

            add_x2(0)
            add_x2(1)
            for i in range(GROUPS):
                if i + 2 < GROUPS:
                    add_x2(i + 2)
                po.wait_ge(c_mv, GT * (i + 1))
                rsqrt(rstd4[:, i % DEPTH], mv4[:, i % DEPTH], c_ve, i + 1, c_rs)


_IN = ["x", "xT", "cT", "Wq", "Wk", "Wv", "Wp", "bq", "bk", "bv", "bp", "WQ", "WK", "WV", "WO", "bQ", "bK", "bV", "bO",
       "WgT", "W1T", "b1", "W2T", "b2", "W3T", "b3", "consts"]


def kernel(x, ctx_1024, L0_attn_Wq, L0_attn_bq, L0_attn_Wk, L0_attn_bk, L0_attn_Wv, L0_attn_bv, L0_attn_Wp, L0_attn_bp,
           L0_xattn_W_Q, L0_xattn_W_K, L0_xattn_W_V, L0_xattn_W_O, L0_xattn_b_Q, L0_xattn_b_K, L0_xattn_b_V, L0_xattn_b_O,
           L0_ffn_Wg, L0_ffn_W1, L0_ffn_b1, L0_ffn_W2, L0_ffn_b2, L0_ffn_W3, L0_ffn_b3):
    import concourse.bacc as bacc
    from concourse.bass_utils import run_bass_kernel_spmd

    x = np.asarray(x)
    ctx_1024 = np.asarray(ctx_1024)

    def cols(w):
        return np.asarray(w).transpose(1, 0, 2).reshape(DIM, INNER)

    arrays = dict(
        x=x.reshape(TOK, DIM), xT=x.reshape(TOK, DIM).T, cT=ctx_1024.reshape(TOK, DIM).T,
        Wq=L0_attn_Wq, Wk=L0_attn_Wk, Wv=L0_attn_Wv, Wp=L0_attn_Wp, bq=L0_attn_bq, bk=L0_attn_bk, bv=L0_attn_bv, bp=L0_attn_bp,
        WQ=cols(L0_xattn_W_Q), WK=cols(L0_xattn_W_K), WV=cols(L0_xattn_W_V), WO=np.asarray(L0_xattn_W_O).reshape(INNER, DIM),
        bQ=np.asarray(L0_xattn_b_Q).reshape(INNER), bK=np.asarray(L0_xattn_b_K).reshape(INNER),
        bV=np.asarray(L0_xattn_b_V).reshape(INNER), bO=L0_xattn_b_O,
        WgT=np.asarray(L0_ffn_Wg).T, W1T=np.asarray(L0_ffn_W1).transpose(0, 2, 1), b1=np.asarray(L0_ffn_b1).reshape(-1),
        W2T=np.asarray(L0_ffn_W2).transpose(0, 2, 1), b2=np.asarray(L0_ffn_b2).reshape(-1),
        W3T=np.asarray(L0_ffn_W3).transpose(0, 2, 1), b3=np.asarray(L0_ffn_b3).reshape(-1), consts=constants())
    arrays = {n: np.ascontiguousarray(arrays[n]) for n in _IN}
    nc = bacc.Bacc("TRN2", target_bir_lowering=False, num_devices=1)
    args = {n: nc.dram_tensor(f"in_{n}", a.shape, mybir.dt.from_np(a.dtype), kind="ExternalInput").ap() for n, a in arrays.items()}
    out = nc.dram_tensor("out_rows", (TOK, DIM), F32, kind="ExternalOutput").ap()
    decoder_kernel(nc, out=out, **args)
    r = run_bass_kernel_spmd(nc, [{f"in_{n}": a for n, a in arrays.items()}], core_ids=[0])
    return r.results[0]["out_rows"].reshape(x.shape)
```

```python
from contextlib import ExitStack

import numpy as np

import concourse.bass as bass
from concourse import mybir

F32 = mybir.dt.float32
F32R = mybir.dt.float32r
BF16 = mybir.dt.bfloat16
FP8 = mybir.dt.float8e4
U32 = mybir.dt.uint32
I32 = mybir.dt.int32
ALU = mybir.AluOpType
ACT = mybir.ActivationFunctionType
AX_X = mybir.AxisListType.X

P = 128
NB, SEQ, DIM = 8, 512, 256
TOK = NB * SEQ
TT = SEQ // P
DC = DIM // P
LIN_D = 16
HEADS, HD = 16, 64
PAIRS = HEADS // 2
INNER = HEADS * HD
UNITS = HEADS * TT
ORDER = (3, 0, 2, 1)
NE, FF, TOPK = 8, 512, 2
FC = FF // P
ROWTILES = TOK // P
MOE_TILES = TOK * TOPK // P + NE - 1
LIST_COLS = MOE_TILES + 2
HOT = 8
DUMP = TOK * TOPK
GT = 2
GROUPS = ROWTILES // GT
DEPTH = 4
EPS = 1e-5
FAR = 1e30

C_IDENT, C_CAUSAL, C_TRI, C_BLOCK, C_IOTA, C_LANE = 0, P, 2 * P, 3 * P, 4 * P, 5 * P
C_CODE = C_LANE + 8
C_COLS = C_CODE + ROWTILES


def constants():
    r, c = np.arange(P)[:, None], np.arange(P)[None, :]
    t = np.zeros((P, C_COLS), np.float32)
    t[:, C_IDENT:C_IDENT + P] = r == c
    t[:, C_CAUSAL:C_CAUSAL + P] = np.where(c > r, FAR, 0.0)
    t[:, C_TRI:C_TRI + P] = r < c
    t[:, C_BLOCK:C_BLOCK + P] = r // LIN_D == c // LIN_D
    t[:, C_IOTA:C_IOTA + P] = c
    t[:, C_LANE] = np.arange(P)
    t[:, C_LANE + 1] = DUMP + 1 + np.arange(P)
    t[:, C_LANE + 2] = 2 * np.arange(P) + 1
    t[:, C_LANE + 3] = 2 * np.arange(P) + 2
    t[:, C_CODE:C_CODE + ROWTILES] = np.arange(ROWTILES)
    t[:, C_LANE + 4] = -0.5
    t[:, C_LANE + 5] = -0.5
    t[:, C_LANE + 6] = -0.5
    t[:, C_LANE + 7] = -0.5
    return t


def unit(u):
    return u // (2 * TT), ORDER[u // 2 % TT], u % 2


def at(i, per, k):
    return i * per + k


TABLE_OWN = ([(2 * TT * p + 1, "V", p + 1) for p in range(PAIRS - 1)]
             + [(2 * TT * p + n, job, p + 2) for p in range(PAIRS - 2) for n, job in ((3, "K"), (6, "Q"))])
TABLE_TAIL = [(3, "wo", 0), (4, "wo", 1), (6, "wo", 2), (8, "wo", 3), (15, "x2T", 0), (18, "x2T", 1), (21, "gate", 0)]
TABLE_NEXT = [(12, "kv", 0), (13, "kv", 1), (19, "kv", 2), (20, "kv", 3), (23, "q", 0), (26, "q", 1), (28, "vTk", 0),
              (31, "vTkWp", 0), (38, "y", 0), (39, "y", 1), (51, "x1T", 0), (53, "x1T", 1),
              (52, "K", 0), (54, "Q", 0), (57, "V", 0), (59, "K", 1), (62, "Q", 1)]


class Round:

    def __init__(self, i, base, norms, own=True, tail=True, ahead=True):
        self.i, self.base = i, base
        self.own, self.tail, self.ahead = own, tail, ahead
        self.tail_norm, self.ahead_norm = norms, norms + (1 if tail else 0)
        self.table = sorted(TABLE_OWN * own + TABLE_TAIL * tail + TABLE_NEXT * ahead)

    def number(self, job, k=0):
        return self.base + [(j, n) for _, j, n in self.table if j not in "KQ"].index((job, k))

    def slot(self, u):
        return [(job, k) for s, job, k in self.table if s == u]


def in_bank7(table):
    return sum(job not in "KQ" for _, job, _ in table)


PER_ROUND = in_bank7(TABLE_OWN + TABLE_TAIL + TABLE_NEXT)
BEFORE_0 = in_bank7(TABLE_NEXT) - in_bank7(TABLE_TAIL)


def kq_events(job, k):
    return 2 * k + (1 if job == "K" else 2) + (2 * PAIRS if k < 2 else 0)


def prologue():
    return Round(-1, 0, 0, own=False, tail=False)


def first_round():
    return Round(0, in_bank7(TABLE_NEXT), 1, tail=False)


def middle_round(i):
    return Round(i, i * PER_ROUND + BEFORE_0, i * 2)


def last_round():
    return Round(NB - 1, (NB - 1) * PER_ROUND + BEFORE_0, 2 * NB - 2, ahead=False)


def epilogue():
    return Round(NB, NB * PER_ROUND - in_bank7(TABLE_TAIL), 2 * NB - 1, own=False, ahead=False)


PRODUCTS = NB * PER_ROUND


def decoder_kernel(nc, x, xT, cT, Wq, Wk, Wv, Wp, bq, bk, bv, bp, WQ, WK, WV, WO, bQ, bK, bV, bO,
                   WgT, W1T, b1, W2T, b2, W3T, b3, consts, out):
    x2_d = nc.dram_tensor("x2_rows", (TOK, DIM), F32, kind="Internal").ap()
    y_d = nc.dram_tensor("expert_rows", (DUMP + P, DIM), F32, kind="Internal").ap()

    with ExitStack() as ctx:
        def sb(name, shape, dt=F32):
            return ctx.enter_context(nc.sbuf_tensor(name, shape, dt))

        def sem(name):
            return ctx.enter_context(nc.semaphore(name))

        PS = ctx.enter_context(nc.psum_tensor("PS", [P, 8, 512], F32))

        cst = sb("cst", [P, C_COLS])
        ident = cst[:, C_IDENT:C_IDENT + P]
        ident_b = sb("ident_b", [P, P], BF16)
        causal_b = sb("causal_b", [P, P], BF16)
        tri_b = sb("tri_b", [P, P], BF16)
        ones_b = sb("ones_b", [P, P], BF16)
        logits = sb("logits", [P, ROWTILES, NE])
        gates = sb("gates", [P, TOPK, ROWTILES])
        w3H, w3L = (sb(name, [P, NE * FC * DIM], F32R) for name in ("w3H", "w3L"))
        ZH, ZL = (w3H[:, n * PAIRS * SEQ:(n + 1) * PAIRS * SEQ].rearrange("p (a b) -> p a b", b=SEQ) for n in range(2))
        QH, QL, KH, KL = (w3L[:, n * 2 * SEQ:(n + 1) * 2 * SEQ].rearrange("p (a b) -> p a b", b=SEQ) for n in range(4))
        wOH, wOL = (w3L[:, 8 * SEQ + n * PAIRS * DIM:8 * SEQ + (n + 1) * PAIRS * DIM].rearrange("p (a b) -> p a b", b=DIM)
                    for n in range(2))
        hTH, hTL = (sb(name, [P, FF], F32R) for name in ("hTH", "hTL"))
        ARENA = 32 * 1024
        arena = sb("arena", [P, ARENA])
        used = [0, 0]

        def view(stage, *shape, dt=F32):
            n = int(np.prod(shape)) * (4 if dt in (F32, U32, I32) else 2 if dt == BF16 else 1) // 4
            a = used[stage]
            used[stage] += n
            assert used[stage] <= ARENA, used
            v = arena[:, a:a + n]
            if dt != F32:
                v = v.bitcast(dt)
            if len(shape) > 1:
                names = "abc"[:len(shape)]
                v = v.rearrange(f"p ({' '.join(names)}) -> p {' '.join(names)}",
                                **dict(zip(names[1:], shape[1:])))
            return v

        wq, wk, wv, wp = (view(0, DC, DIM) for _ in range(4))
        wQ, wK, wV = (view(0, DC, INNER, dt=BF16) for _ in range(3))
        bkv_b = view(0, 2 * DIM)
        bp_b = view(0, DIM)
        bV_b = view(0, INNER)
        xT_s, cT_s = view(0, DC, SEQ), view(0, DC, SEQ)
        xr_s = view(0, TT, DIM)
        kv_s = view(0, TT, 2 * DIM)
        ek_s, rk_s = view(0, DIM), view(0, DIM)
        rq_s = view(0, SEQ)
        qm_s = view(0, DC, SEQ)
        bd_s, m_s = view(0, DC, P), view(0, DC, DIM)
        cq_s, x1qT_s = view(0, DC, SEQ, dt=BF16), view(0, DC, SEQ, dt=BF16)
        EARLY = used[0]
        x1q_s = view(0, TT, DIM, dt=FP8)
        wg = view(0, DC, NE)
        bq_c = view(0, DC)
        bQ_c, bK_c, nbQ = view(0, PAIRS), view(0, PAIRS), view(0, PAIRS)
        bO_b = view(0, DIM)
        q_s = view(0, DC, SEQ)
        x2T_s = q_s
        x1_s = view(0, TT, DIM)
        stats, mv, rstd = view(0, TT, 8), view(0, TT, 2), view(0, TT)
        stats1, mv1, rstd1 = view(0, TT, 8), view(0, TT, 2), view(0, TT)
        V_s = view(0, 2, TT, P)
        prob, pnorm = view(0, 4, SEQ), view(0, 4, SEQ)
        smin, ssum, sinv = view(0, 4), view(0, 4), view(0, 4)
        PT = [view(0, TT, SEQ) for _ in range(4)]
        wO_raw = PT[0].rearrange("p a b -> p (a b)").rearrange("p (a b) -> p a b", b=DIM)
        stage_w = [prob.rearrange("p a b -> p (a b)"), pnorm.rearrange("p a b -> p (a b)")]

        w1_sb, w2_sb = view(1, NE * DC * FF), view(1, NE * DC * FF)
        w3_raw = w1_sb
        W2_EARLY = (EARLY - NE * DC * FF) // (DC * FF)
        b1_b, b2_b, b3_b = view(1, NE * FF), view(1, NE * FF), view(1, NE * DIM)
        mark = used[1]
        top = view(1, ROWTILES, NE)
        topi = view(1, ROWTILES, NE, dt=U32)
        choice = view(1, TOPK, ROWTILES)
        lane_hot = view(1, 2, HOT, P, dt=BF16)
        used[1] -= 2 * HOT * P // 2
        onehot = view(1, TOPK, ROWTILES * NE)
        run_a, run_b = view(1, ROWTILES, NE), view(1, ROWTILES, NE)
        both_b = view(1, ROWTILES * NE, dt=BF16)
        before = view(1, ROWTILES, NE)
        etiles, etiles_i = view(1, NE), view(1, NE, dt=I32)
        cum_a, cum_b = view(1, NE), view(1, NE)
        slot = view(1, TOPK, ROWTILES)
        slot_i, tile_i, lane_i = (view(1, TOPK * ROWTILES, dt=I32) for _ in range(3))
        tile_f, lane_f = view(1, TOPK * ROWTILES), view(1, TOPK * ROWTILES)
        past = view(1, LIST_COLS, NE)
        used[1] -= LIST_COLS * NE
        tile_hot, code_hot = view(1, 2, HOT, LIST_COLS), view(1, 2, HOT, 2 * LIST_COLS, dt=BF16)
        hi_s, code, empty = view(1, LIST_COLS), view(1, LIST_COLS), view(1, LIST_COLS)
        expert_f = view(1, LIST_COLS)
        expert = sb("expert", [P, LIST_COLS], I32)
        gather_l = sb("gather_l", [P, LIST_COLS], U32)
        scatter_l = sb("scatter_l", [P, LIST_COLS], U32)
        code_i = view(1, LIST_COLS, dt=I32)
        used[1] = mark
        xg = view(1, 2, DIM)
        g_idx, s_idx = sb("g_idx", [P, 2], U32), sb("s_idx", [P, 2], U32)
        xgT = view(1, 2, DIM)
        g_s, v_s = view(1, 2, FF), view(1, 2, FF)
        silu_s, h_s = view(1, 2, FF), view(1, 2, FF)
        yo = view(1, 2, DIM)
        used[1] = 0
        yy, xx = view(1, DEPTH, GT, TOPK * DIM), view(1, DEPTH, GT, DIM)
        zz, oo = view(1, DEPTH, GT, DIM), view(1, 2, GT, DIM)
        stats4, mv4, rstd4 = view(1, DEPTH, GT, 8), view(1, DEPTH, GT, 2), view(1, DEPTH, GT)

        s_const, s_wq, s_wlin, s_wo = sem("const_in"), sem("wq_in"), sem("lin_weights_in"), sem("wo_in")
        s_wraw = [sem(f"raw_weights_in{q}") for q in range(4)]
        s_w3, s_w12 = sem("w3_in"), sem("w12_in")
        s_wOH, s_wOL, r_w3h, r_w3l = sem("wO_rounded"), sem("wO_rest"), sem("w3_rounded"), sem("w3_rest")
        s_cb, s_wexp, s_wmag, s_wadd, s_wcvt = sem("consts_bf16"), sem("w_exponents"), sem("w_magic"), sem("w_added"), sem("w_rounded")
        s_nbQ, s_wscaled = sem("scaled_bQ"), sem("scaled_WQ")
        s_xT, s_xr, s_cT, s_x2out = sem("xT_in"), sem("x_rows_in"), sem("ctx_in"), sem("x2_out")
        p7, x7 = sem("bank7_mm"), sem("bank7_read")
        d_z = sem("Z_rest")
        p_kq, a_h, d_l = sem("KQ_mm"), sem("KQ_rounded"), sem("KQ_rest")
        p_s, p_t, p_z = sem("score_mm"), sem("probT_mm"), sem("z_mm")
        a_k, a_e, a_t = sem("k_exp_relu"), sem("exp_done"), sem("probT0_sb")
        d_kf, d_qf, d_ce, d_cm = sem("k_feat"), sem("q_feat"), sem("ctx_exponents"), sem("ctx_magic")
        d_st, d_mv, d_x1, d_xq, d_x2 = sem("ln_stats"), sem("ln_mean_var"), sem("x1_rows"), sem("x1q_rows"), sem("x2_rows_sb")
        d_min, d_inv, d_t, a_z = sem("row_min"), sem("row_inv"), sem("probT1_sb"), sem("Z_rounded")
        g_ca, g_cq, g_res, g_ve, g_rs, g_n, g_res2 = sem("ctx_added"), sem("ctx_rounded"), sem("x_plus_bias"), sem("var_eps"), sem("rstd"), sem("prob_normed"), sem("x1_plus_bias")
        r_d, r_e, r_pre, r_hot, r_list, r_tab = sem("route_dve"), sem("route_exp"), sem("prefix_mm"), sem("hot_ready"), sem("list_mm"), sem("tables_ready")
        r_gap = sem("logit_gap")
        r_lane, r_tile, r_low, r_high = sem("lane_hot"), sem("tile_hot"), sem("code_low"), sem("code_high")
        m_gi, m_si = sem("gather_idx"), sem("scatter_idx")
        m_in, m_out = [sem(f"tokens_in{h}") for h in range(2)], [sem(f"rows_out{h}") for h in range(2)]
        c_in, s_out = [sem(f"mix_in{h}") for h in range(DEPTH)], [sem(f"out_stored{h}") for h in range(2)]
        m_xt, m_xs, m_g, m_v, m_ht, m_o = sem("xgT_mm"), sem("xgT_sb"), sem("g_mm"), sem("v_mm"), sem("hT_mm"), sem("o_mm")
        m_hl, m_gb, m_vb, m_si_, m_h, m_hs, m_yo = sem("hT_rest"), sem("g_bias"), sem("v_bias"), sem("silu"), sem("h_sb"), sem("hT_sb"), sem("yo_sb")
        c_mix, c_sum, c_pre, c_st, c_mv, c_ve, c_rs, c_o = sem("mix_half"), sem("mix_plus_x2"), sem("mix_pre"), sem("mix_stats"), sem("mix_mv"), sem("mix_ve"), sem("mix_rstd"), sem("mix_out")

        s_passed = sem("waits_passed")

        def wait_alone(eng, semaphore, value):
            eng.wait_ge(semaphore, value)
            eng.sem_inc(s_passed, 1)

        def wait_past(eng, semaphore, i, per, k):
            if not (isinstance(i, int) and at(i, per, k) <= 0):
                eng.wait_ge(semaphore, at(i, per, k))

        def tile(u, k):
            return u * 2 + k, u + k // 2, k % 2

        block = ctx.enter_context(nc.Block())
        ds = bass.ds
        N_WRAW = 12
        raw_w = [(w, wt, k, n) for w, wt in ((WK, wK), (WQ, wQ), (WV, wV)) for k in range(DC) for n in range(2)]

        @block.sync
        def _(sp):
            sp.dma_start(cst[:, :], consts).then_inc(s_const, 16)

            def load_transposed(i):
                sp.dma_start(xT_s, xT[:, ds(i * SEQ, SEQ)].rearrange("(c p) t -> p c t", p=P)).then_inc(s_xT, 16)
                sp.dma_start(cT_s, cT[:, ds(i * SEQ, SEQ)].rearrange("(c p) t -> p c t", p=P)).then_inc(s_cT, 16)

            def load_rows(i):
                sp.dma_start(xr_s, x[ds(i * SEQ, SEQ), :].rearrange("(a p) d -> p a d", p=P)).then_inc(s_xr, 16)

            sp.dma_start(wq, Wq.rearrange("(c p) n -> p c n", p=P)).then_inc(s_wq, 16)
            sp.dma_start(bq_c, bq.rearrange("(c p) -> p c", p=P), allow_slow_non_contiguous=True).then_inc(s_wq, 16)
            load_transposed(0)
            for w, dst in ((Wk, wk), (Wv, wv), (Wp, wp)):
                sp.dma_start(dst, w.rearrange("(c p) n -> p c n", p=P)).then_inc(s_wlin, 16)
            sp.dma_start(bkv_b[:, 0:DIM], bk.partition_broadcast(P)).then_inc(s_wlin, 16)
            sp.dma_start(bkv_b[:, DIM:2 * DIM], bv.partition_broadcast(P)).then_inc(s_wlin, 16)
            sp.dma_start(bp_b, bp.partition_broadcast(P)).then_inc(s_wlin, 16)
            load_rows(0)
            for n, (w, _, k, c) in enumerate(raw_w):
                if n >= 4:
                    sp.wait_ge(s_wcvt, n - 3)
                sp.dma_start(stage_w[0][:, (n % 4) * 512:(n % 4) * 512 + 512],
                             w[k * P:(k + 1) * P, c * 512:(c + 1) * 512]).then_inc(s_wraw[n % 4], 16)
            sp.dma_start(wO_raw, WO.rearrange("(c p) n -> p c n", p=P)).then_inc(s_wo, 16)
            sp.dma_start(wg, WgT.rearrange("(c p) n -> p c n", p=P)).then_inc(s_wo, 16)
            sp.dma_start(bQ_c, bQ.rearrange("(c p) -> p c", p=P), allow_slow_non_contiguous=True).then_inc(s_wo, 16)
            sp.dma_start(bK_c, bK.rearrange("(c p) -> p c", p=P), allow_slow_non_contiguous=True).then_inc(s_wo, 16)
            sp.dma_start(bV_b, bV.partition_broadcast(P)).then_inc(s_wo, 16)
            sp.dma_start(bO_b, bO.partition_broadcast(P)).then_inc(s_wo, 16)

            def store_x2(i):
                sp.wait_ge(d_x2, at(i, TT, TT))
                sp.dma_start(x2_d[ds(i * SEQ, SEQ), :].rearrange("(a p) d -> p a d", p=P), x1_s).then_inc(s_x2out, 16)

            sp.wait_ge(g_cq, 1)
            load_transposed(1)
            sp.wait_ge(g_res2, 1)
            load_rows(1)
            with sp.Fori(2, NB) as i:
                sp.wait_ge(s_const, 16)
                sp.wait_ge(g_cq, i)
                load_transposed(i)
                store_x2(i - 2)
                sp.wait_ge(g_res2, i)
                load_rows(i)
            store_x2(NB - 2)

            sp.wait_ge(x7, last_round().number("V", PAIRS - 1) + 1)
            sp.dma_start(w3_raw.rearrange("p (e c f) -> p e c f", e=NE, c=FC),
                         W3T.rearrange("e (c p) f -> p e c f", p=P)).then_inc(s_w3, 16)

            def load_w2(a, b):
                sp.dma_start(w2_sb[:, a * DC * FF:b * DC * FF].rearrange("p (e c f) -> p e c f", e=b - a, c=DC),
                             W2T[a:b].rearrange("e (c p) f -> p e c f", p=P)).then_inc(s_w12, 16)

            load_w2(0, W2_EARLY)
            store_x2(NB - 1)
            def load_w1(a, b):
                sp.dma_start(w1_sb[:, a * DC * FF:b * DC * FF].rearrange("p (e c f) -> p e c f", e=b - a, c=DC),
                             W1T[a:b].rearrange("e (c p) f -> p e c f", p=P)).then_inc(s_w12, 16)

            sp.wait_ge(r_w3l, NE // 4)
            load_w1(0, NE // 4)
            sp.wait_ge(x7, PRODUCTS)
            sp.wait_ge(s_x2out, 16 * NB)
            load_w2(W2_EARLY, NE)
            sp.dma_start(b1_b, b1.partition_broadcast(P)).then_inc(s_w12, 16)
            sp.dma_start(b2_b, b2.partition_broadcast(P)).then_inc(s_w12, 16)
            sp.dma_start(b3_b, b3.partition_broadcast(P)).then_inc(s_w12, 16)
            for q in range(1, 4):
                sp.wait_ge(r_w3l, (q + 1) * NE // 4)
                load_w1(q * NE // 4, (q + 1) * NE // 4)

            sp.wait_ge(m_out[0], 16 * ((MOE_TILES + 1) // 2))
            sp.wait_ge(m_out[1], 16 * (MOE_TILES // 2))

            def load_mix(i):
                a, n, h = i * GT * P, GT * P, i % DEPTH
                sp.dma_start(yy[:, h], y_d[a * TOPK:(a + n) * TOPK, :]
                             .rearrange("(a p j) d -> p a (j d)", p=P, j=TOPK)).then_inc(c_in[h], 16)
                sp.dma_start(xx[:, h], x2_d[a:a + n, :].rearrange("(a p) d -> p a d", p=P)).then_inc(c_in[h], 16)

            for i in range(DEPTH):
                load_mix(i)
            for i in range(GROUPS):
                if i + DEPTH < GROUPS:
                    sp.wait_ge(c_pre, GT * (i + 1))
                    load_mix(i + DEPTH)
                sp.wait_ge(c_o, GT * (i + 1))
                sp.dma_start(out[i * GT * P:(i + 1) * GT * P, :].rearrange("(a p) d -> p a d", p=P), oo[:, i % 2]).then_inc(s_out[i % 2], 16)
            sp.wait_ge(s_out[0], 16 * GROUPS // 2)
            sp.wait_ge(s_out[1], 16 * GROUPS // 2)

        @block.tensor
        def _(pe):
            mm = nc.tensor.matmul

            B6, B7 = PS[:, 6, :], PS[:, 7, :]

            def q_features(r, m):
                pe.wait_ge(s_xT, at(r.i, 16, 32))
                for k in range(DC):
                    last = mm(B7, wq[:, k, m * P:(m + 1) * P], xT_s[:, k, :], start=k == 0, stop=k == DC - 1)
                return last

            def kv_rows(r, t):
                pe.wait_ge(s_xT, at(r.i, 16, 32))
                for n, w in enumerate((wk, wv)):
                    for k in range(DC):
                        last = mm(B7[:, n * DIM:(n + 1) * DIM], xT_s[:, k, t * P:(t + 1) * P], w[:, k, :],
                                  start=k == 0, stop=k == DC - 1)
                return last

            def vTk(r):
                pe.wait_ge(d_kf, at(r.i, TT, 2 * TT))
                for g in range(DC):
                    for t in range(TT):
                        last = mm(B7[:, g * P:(g + 1) * P], kv_s[:, t, DIM + g * P:DIM + (g + 1) * P],
                                  kv_s[:, t, g * P:(g + 1) * P], start=t == 0, stop=t == TT - 1)
                return last

            def vTkWp(r):
                for g in range(DC):
                    last = mm(B7[:, g * DIM:(g + 1) * DIM], bd_s[:, g, :], wp[:, g, :], start=True, stop=True)
                return last

            def lin_rows(r, n):
                pe.wait_ge(d_qf, at(r.i, DC, 2 * DC))
                for t in (2 * n, 2 * n + 1):
                    for g in range(DC):
                        last = mm(B7[:, (t % 2) * DIM:(t % 2 + 1) * DIM], q_s[:, g, t * P:(t + 1) * P],
                                  m_s[:, g, :], start=g == 0, stop=g == DC - 1)
                return last

            def x1T(r, k):
                wait_alone(pe, d_xq, at(r.i, TT, 2 * TT))
                for t in range(TT):
                    last = mm(B7[:, t * P:(t + 1) * P], x1q_s[:, t, k * P:(k + 1) * P], ident_b[:, :], start=True, stop=True)
                return last

            def proj_k(r, p):
                if p == 0:
                    pe.wait_ge(g_cq, at(r.i, 1, 2))
                for k in range(DC):
                    last = mm(B6, wK[:, k, p * P:(p + 1) * P], cq_s[:, k, :], start=k == 0, stop=k == DC - 1)
                return last

            def proj_q(r, p):
                if p == 0:
                    pe.wait_ge(x7, r.number("x1T", 1) + 1)
                for k in range(DC):
                    last = mm(B6, wQ[:, k, p * P:(p + 1) * P], x1qT_s[:, k, :], start=k == 0, stop=k == DC - 1)
                return last

            def proj_v(r, p):
                for t in range(TT):
                    for k in range(DC):
                        last = mm(B7[:, t * P:(t + 1) * P], cq_s[:, k, t * P:(t + 1) * P], wV[:, k, p * P:(p + 1) * P],
                                  start=k == 0, stop=k == DC - 1)
                return last

            def out_rows(r, t):
                pe.wait_ge(d_z, at(r.i, PAIRS, 0))
                pe.wait_ge(s_wOL, 1)
                for p in range(PAIRS):
                    for n, (z_part, w_part) in enumerate(((ZH, wOH), (ZH, wOL), (ZL, wOH))):
                        last = mm(B7[:, 0:DIM], z_part[:, p, t * P:(t + 1) * P], w_part[:, p, :], start=p == 0 and n == 0,
                                  stop=p == PAIRS - 1 and n == 2)
                return last

            def x2T(r, k):
                pe.wait_ge(d_x2, at(r.i, TT, 0))
                for t in range(TT):
                    last = nc.tensor.transpose(B7[:, t * P:(t + 1) * P], x1_s[:, t, k * P:(k + 1) * P], ident)
                return last

            def gate(r):
                for t in range(TT):
                    for k in range(DC):
                        last = mm(B7[:, t * NE:(t + 1) * NE], x2T_s[:, k, t * P:(t + 1) * P], wg[:, k, :],
                                  start=k == 0, stop=k == DC - 1)
                return last

            def product(r, job, k):
                if job in ("K", "Q"):
                    wait_past(pe, d_z, r.i, PAIRS, k - 2 + (PAIRS if k < 2 else 0))
                    wait_past(pe, d_l, r.i, 2 * PAIRS, kq_events(job, k) - 1)
                    (proj_k if job == "K" else proj_q)(r, k).then_inc(p_kq, 1)
                    return
                if r.tail or r.number(job, k) > 0:
                    pe.wait_ge(x7, r.number(job, k))
                if job == "V":
                    last = proj_v(r, k)
                elif job == "wo":
                    last = out_rows(r, k)
                elif job == "x2T":
                    last = x2T(r, k)
                elif job == "gate":
                    last = gate(r)
                elif job == "q":
                    last = q_features(r, k)
                elif job == "kv":
                    last = kv_rows(r, k)
                elif job == "vTk":
                    last = vTk(r)
                elif job == "vTkWp":
                    last = vTkWp(r)
                elif job == "y":
                    last = lin_rows(r, k)
                else:
                    last = x1T(r, k)
                last.then_inc(p7, 1)

            def scores(r, u):
                p, t, e = unit(u)
                n = (t + 1) * P
                if u % (2 * TT) == 0:
                    pe.wait_ge(d_l, at(r.i, 2 * PAIRS, 2 * p + 2))
                wait_past(pe, a_e, r.i, UNITS, u - 3)
                bank = u % 4
                for n_part, (q_part, k_part) in enumerate(((QH, KH), (QH, KL), (QL, KH))):
                    mm(PS[:, bank, 0:n], q_part[e * HD:(e + 1) * HD, p % 2, t * P:(t + 1) * P],
                       k_part[e * HD:(e + 1) * HD, p % 2, 0:n], start=n_part == 0, stop=False)
                mm(PS[:, bank, n - P:n], ident_b[:, :], causal_b[:, :], start=False, stop=True).then_inc(p_s, 1)

            def transposes(r, u):
                p, t, e = unit(u)
                pe.wait_ge(g_n, at(r.i, UNITS, u + 1))
                wait_past(pe, (a_t, d_t)[e], r.i, UNITS // 2, u // 2)
                for j in range(t + 1):
                    last = nc.tensor.transpose(PS[:, 4 + e, j * P:(j + 1) * P], pnorm[:, u % 4, j * P:(j + 1) * P], ident)
                last.then_inc(p_t, 1)

            def weighted(r, p):
                pe.wait_ge(a_t, at(r.i, UNITS // 2, TT * (p + 1)))
                pe.wait_ge(d_t, at(r.i, UNITS // 2, TT * (p + 1)))
                pe.wait_ge(x7, r.number("V", p) + 1 if p >= 1 else r.base)
                wait_past(pe, d_z, r.i, PAIRS, p)
                pe.wait_ge(d_l, at(r.i, 2 * PAIRS, 2 * p + 6 if r.ahead else min(2 * p + 6, 2 * PAIRS) if r.own else 0))
                for j in range(TT):
                    for e in range(2):
                        last = mm(PS[e * HD:(e + 1) * HD, 6, j * P:SEQ], V_s[:, p % 2, j, e * HD:(e + 1) * HD],
                                  PT[2 * (p % 2) + e][:, j, j * P:SEQ], start=j == 0, stop=j == TT - 1)
                last.then_inc(p_z, 1)

            def run(r):
                for u in range(UNITS):
                    p, n = divmod(u, 2 * TT)
                    if u + 4 < UNITS or r.ahead:
                        scores(r, u + 4)
                    transposes(r, u)
                    if n == 1 and (p >= 1 or r.tail):
                        weighted(r, p - 1)
                    for job, k in r.slot(u):
                        product(r, job, k)

            pe.wait_ge(s_wq, 16 * 2)
            for _, job, k in prologue().table:
                if (job, k) == ("kv", 0):
                    pe.wait_ge(s_wlin, 16 * 6)
                elif (job, k) == ("x1T", 0):
                    pe.wait_ge(s_cb, 3)
                elif (job, k) == ("K", 0):
                    pe.wait_ge(s_wo, 16 * 6)
                    pe.wait_ge(s_const, 16)
                    pe.wait_ge(s_wscaled, 1)
                    pe.wait_ge(s_wcvt, N_WRAW)
                product(prologue(), job, k)
            for u in range(4):
                scores(prologue(), UNITS + u)
            run(first_round())
            with pe.Fori(1, NB - 1) as i:
                run(middle_round(i))
            run(last_round())
            weighted(epilogue(), -1)
            for _, job, k in epilogue().table:
                product(epilogue(), job, k)

            pe.wait_ge(r_hot, 1)
            mm(PS[:, 0, 0:ROWTILES * NE], tri_b[:, :], both_b, start=True, stop=True)
            mm(PS[:, 1, 0:ROWTILES * NE], ones_b[:, :], both_b, start=True, stop=True).then_inc(r_pre, 1)
            for c in range(ROWTILES * TOPK // HOT):
                pe.wait_ge(r_lane, c + 1)
                pe.wait_ge(r_low, c + 1)
                pe.wait_ge(r_high, c + 1)
                for m in range(HOT):
                    last = mm(PS[:, 2, 0:2 * LIST_COLS], lane_hot[:, c % 2, m, :], code_hot[:, c % 2, m, :],
                              start=c == 0 and m == 0, stop=(c + 1) * HOT + m == ROWTILES * TOPK + HOT - 1)
                last.then_inc(r_list, 1)

            def expert_of(s):
                return pe.value_load(expert[0:1, ds(s, 1)], min_val=0, max_val=NE - 1)

            def tokensT(s, nth, h):
                pe.wait_ge(m_in[h], at(nth, 16, 16))
                for k in range(DC):
                    last = nc.tensor.transpose(PS[:, 0, k * P:(k + 1) * P], xg[:, h, k * P:(k + 1) * P], ident)
                last.then_inc(m_xt, 1)

            def up(e, h, bank, w, done):
                w_e = w[:, ds(e * (DC * FF), DC * FF)]
                for k in range(DC):
                    last = mm(PS[:, bank + h, :], xgT[:, h, k * P:(k + 1) * P], w_e[:, k * FF:(k + 1) * FF],
                              start=k == 0, stop=k == DC - 1)
                last.then_inc(done, 1)

            def up_g(e, s, nth, h):
                pe.wait_ge(m_xs, at(s, 1, 1))
                up(e, h, 1, w1_sb, m_g)

            def up_v(e, s, nth, h):
                up(e, h, 3, w2_sb, m_v)

            def hiddenT(s, nth, h):
                pe.wait_ge(m_h, at(s, 1, 1))
                for f in range(FC):
                    last = nc.tensor.transpose(PS[:, 5, f * P:(f + 1) * P], h_s[:, h, f * P:(f + 1) * P], ident)
                last.then_inc(m_ht, 1)

            def down(e, s, nth, h, bank_read, value):
                pe.wait_ge(bank_read, value)
                pe.wait_ge(m_hl, at(s, 1, 1))
                wH, wL = (w[:, ds(e * (FC * DIM), FC * DIM)] for w in (w3H, w3L))
                for f in range(FC):
                    for n, (h_part, w_part) in enumerate(((hTH, wH), (hTH, wL), (hTL, wH))):
                        last = mm(PS[:, 6, 0:DIM], h_part[:, f * P:(f + 1) * P], w_part[:, f * DIM:(f + 1) * DIM],
                                  start=f == 0 and n == 0, stop=f == FC - 1 and n == 2)
                last.then_inc(m_o, 1)

            pe.wait_ge(r_tab, 1)
            pe.wait_ge(s_w12, 16 * 9)
            tokensT(*tile(0, 0))
            e = expert_of(0)
            up_g(e, *tile(0, 0))
            tokensT(*tile(0, 1))
            up_v(e, *tile(0, 0))
            up_g(expert_of(1), *tile(0, 1))
            with pe.Fori(0, (MOE_TILES - 1) // 2) as u:
                e = {1: expert_of(tile(u, 1)[0])}
                for k in (1, 2):
                    hiddenT(*tile(u, k - 1))
                    tokensT(*tile(u, k + 1))
                    up_v(e[k], *tile(u, k))
                    for n in {1: (0, 2), 2: (3,)}[k]:
                        e[n] = expert_of(tile(u, n)[0])
                    down(e[k - 1], *tile(u, k - 1), m_xs, at(tile(u, k + 1)[0], 1, 1))
                    up_g(e[k + 1], *tile(u, k + 1))
            hiddenT(*tile(0, MOE_TILES - 1))
            down(expert_of(MOE_TILES - 1), *tile(0, MOE_TILES - 1), m_yo, MOE_TILES - 1)

        @block.scalar
        def _(act):
            A = nc.scalar.activation

            B6, B7 = PS[:, 6, :], PS[:, 7, :]

            def read(r, job, k):
                if job not in ("K", "Q", "x1T", "x2T", "q", "vTkWp"):
                    return
                if job == "q" and k > 0:
                    act.wait_ge(d_qf, at(r.i, DC, DC + k))
                if job in ("K", "Q"):
                    high, bias = (KH, bK_c) if job == "K" else (QH, nbQ)
                    act.wait_ge(p_kq, at(r.i, 2 * PAIRS, kq_events(job, k)))
                    A(high[:, k % 2, :], B6, ACT.Identity, bias=bias[:, k:k + 1]).then_inc(a_h, 1)
                    return
                act.wait_ge(p7, r.number(job, k) + 1)
                if job == "x1T":
                    A(x1qT_s[:, k, :], B7, ACT.Copy).then_inc(x7, 1)
                elif job == "x2T":
                    A(x2T_s[:, k, :], B7, ACT.Copy).then_inc(x7, 1)
                elif job == "vTkWp":
                    A(m_s.rearrange("p a b -> p (a b)"), B7, ACT.Copy).then_inc(x7, 1)
                else:
                    A(q_s[:, k, :], B7, ACT.Exp, bias=bq_c[:, k:k + 1])
                    A(rq_s, B7, ACT.Relu, bias=bq_c[:, k:k + 1]).then_inc(x7, 1)

            def k_exp_relu(r, t):
                act.wait_ge(x7, r.number("kv", t) + 1)
                wait_past(act, d_kf, r.i, TT, TT + t)
                A(ek_s, kv_s[:, t, 0:DIM], ACT.Exp)
                A(rk_s, kv_s[:, t, 0:DIM], ACT.Relu).then_inc(a_k, 1)

            def exps(r, u):
                n = (unit(u)[1] + 1) * P
                wait_past(act, g_n, r.i, UNITS, u - 3)
                act.wait_ge(d_min, at(r.i, UNITS, u + 1))
                A(prob[:, u % 4, 0:n], PS[:, u % 4, 0:n], ACT.Exp, bias=smin[:, u % 4:u % 4 + 1], scale=-1.0,
                  accum_out=ssum[:, u % 4:u % 4 + 1]).then_inc(a_e, 1)

            def z_rows(r, p):
                act.wait_ge(p_z, at(r.i, PAIRS, p + 1))
                if p == 0 and r.tail:
                    act.wait_ge(p7, r.number("wo", TT - 1) + 1)
                A(ZH[:, p % PAIRS, :], B6, ACT.Copy).then_inc(a_z, 1)

            def run(r):
                for u in range(UNITS):
                    p, t, e = unit(u)
                    if u % (2 * TT) == 2 and (p >= 1 or r.tail):
                        z_rows(r, p - 1)
                    for job, k in r.slot(u - 1):
                        read(r, job, k)
                    if e == 0:
                        act.wait_ge(p_t, at(r.i, UNITS, u + 1))
                        A(PT[2 * (p % 2)][:, 0:t + 1, t * P:(t + 1) * P],
                          PS[:, 4, 0:(t + 1) * P].rearrange("p (a b) -> p a b", b=P), ACT.Copy).then_inc(a_t, 1)
                    if u + 4 < UNITS or r.ahead:
                        exps(r, u + 4)
                    for job, k in r.slot(u - 2):
                        if job == "kv":
                            k_exp_relu(r, k)

            act.wait_ge(s_wq, 16 * 2)
            for _, job, k in prologue().table:
                if (job, k) == ("K", 0):
                    act.wait_ge(s_wo, 16 * 6)
                    A(wOH, wO_raw, ACT.Copy).then_inc(s_wOH, 1)
                    A(nbQ, bQ_c, ACT.Copy, scale=-1.0 / HD ** 0.5).then_inc(s_nbQ, 1)
                    act.wait_ge(s_nbQ, 1)
                read(prologue(), job, k)
                if job == "kv":
                    k_exp_relu(prologue(), k)
            for u in range(4):
                exps(prologue(), UNITS + u)
            run(first_round())
            with act.Fori(1, NB - 1) as i:
                run(middle_round(i))
            run(last_round())
            z_rows(epilogue(), -1)
            act.wait_ge(s_w3, 16)
            act.wait_ge(p7, epilogue().number("wo", TT - 1) + 1)
            def round_w3(e):
                part = slice(e * FC * DIM, (e + 1) * FC * DIM)
                A(w3H[:, part], w3_raw[:, part], ACT.Copy).then_inc(r_w3h, 1)

            for e in range(NE // 2):
                round_w3(e)
            for _, job, k in epilogue().table:
                read(epilogue(), job, k)
            for e in range(NE // 2, NE):
                round_w3(e)


            for c in range(ROWTILES * TOPK // HOT):
                low = C_LANE + 2 + c * HOT // ROWTILES
                if c >= 2:
                    act.wait_ge(r_list, c - 1)
                act.wait_ge(r_tile, c + 1)
                A(code_hot[:, c % 2, :, 0:LIST_COLS], tile_hot[:, c % 2], ACT.Copy, scale=cst[:, low:low + 1]).then_inc(r_low, 1)

            act.wait_ge(r_gap, 1)
            A(gates[:, 1, :], choice[:, 0, :], ACT.Exp).then_inc(r_e, 1)

            def silu(s, nth, h):
                act.wait_ge(m_gb, at(s, 1, 1))
                A(silu_s[:, h, :], g_s[:, h, :], ACT.Silu).then_inc(m_si_, 1)

            def hidden(s, nth, h):
                act.wait_ge(m_ht, at(s, 1, 1))
                A(hTH[:, :], PS[:, 5, :], ACT.Copy).then_inc(m_hs, 1)

            silu(*tile(0, 0))
            with act.Fori(0, (MOE_TILES - 1) // 2) as u:
                for k in (1, 2):
                    hidden(*tile(u, k - 1))
                    silu(*tile(u, k))
            hidden(*tile(0, MOE_TILES - 1))

            for i in range(GROUPS):
                act.wait_ge(c_in[i % DEPTH], 32 * (i // DEPTH + 1))
                if i >= DEPTH:
                    act.wait_ge(c_o, GT * (i - DEPTH + 1))
                for t in range(GT):
                    A(zz[:, i % DEPTH, t, :], yy[:, i % DEPTH, t, 0:DIM], ACT.Copy,
                      scale=gates[:, 0, i * GT + t:i * GT + t + 1]).then_inc(c_mix, 1)

        @block.vector
        def _(ve):
            V = nc.vector

            def row_stats(t, pre, st, pre_done, value, done_st):
                ve.wait_ge(pre_done, value)
                V.bn_stats(st[:, t, 0:6], pre[:, t, :]).then_inc(done_st, 1)

            def mean_var(t, st, mvt, done_st, value, done_mv):
                wait_alone(ve, done_st, value)
                V.bn_aggr(mvt[:, t, :], st[:, t, 0:6]).then_inc(done_mv, 1)

            B6, B7 = PS[:, 6, :], PS[:, 7, :]

            def read(r, job, k):
                if job not in ("K", "Q", "V", "wo", "gate", "kv", "vTk", "y"):
                    return
                if job in ("K", "Q"):
                    high, low, bias = (KH, KL, bK_c) if job == "K" else (QH, QL, nbQ)
                    ve.wait_ge(a_h, at(r.i, 2 * PAIRS, kq_events(job, k)))
                    V.scalar_tensor_tensor(low[:, k % 2, :], B6, bias[:, k:k + 1], high[:, k % 2, :].bitcast(F32),
                                           ALU.add, ALU.subtract).then_inc(d_l, 1)
                    return
                if job == "wo":
                    ve.wait_ge(g_res2, at(r.i, 1, 0))
                if job == "y":
                    ve.wait_ge(g_res, at(r.i, 1, 2))
                ve.wait_ge(p7, r.number(job, k) + 1)
                if job == "V":
                    V.tensor_tensor(V_s[:, k % 2], B7.rearrange("p (a b) -> p a b", b=P),
                                    bV_b[:, k * P:(k + 1) * P].unsqueeze(1).to_broadcast([P, TT, P]), ALU.add).then_inc(x7, 1)
                elif job == "wo":
                    V.tensor_tensor(x1_s[:, k, :], B7[:, 0:DIM], x1_s[:, k, :], ALU.add).then_inc(x7, 1)
                elif job == "gate":
                    V.tensor_copy(logits[:, ds(r.i * TT - TT, TT), :], B7[:, 0:TT * NE].rearrange("p (a b) -> p a b", b=NE))\
                     .then_inc(x7, 1)
                elif job == "kv":
                    V.tensor_tensor(kv_s[:, k, :], B7, bkv_b, ALU.add).then_inc(x7, 1)
                elif job == "vTk":
                    V.tensor_tensor(bd_s, B7[:, 0:DIM].rearrange("p (a b) -> p a b", b=P),
                                    cst[:, C_BLOCK:C_BLOCK + P].unsqueeze(1).to_broadcast([P, DC, P]), ALU.mult).then_inc(x7, 1)
                else:
                    V.tensor_tensor(xr_s[:, 2 * k:2 * k + 2, :], B7.rearrange("p (a b) -> p a b", b=DIM),
                                    xr_s[:, 2 * k:2 * k + 2, :], ALU.add).then_inc(x7, 1)

            def q_feature(r, m):
                ve.wait_ge(x7, r.number("q", m) + 1)
                V.scalar_tensor_tensor(q_s[:, m, :], q_s[:, m, :], 1.0, rq_s, ALU.min, ALU.add).then_inc(d_qf, 1)

            def k_feature(r, t):
                ve.wait_ge(a_k, at(r.i, TT, TT + t + 1))
                V.scalar_tensor_tensor(kv_s[:, t, 0:DIM], ek_s, 1.0, rk_s, ALU.min, ALU.add).then_inc(d_kf, 1)

            def context_magic(r):
                ve.wait_ge(s_cT, at(r.i, 16, 32))
                wait_past(ve, g_cq, r.i, 1, 1)
                V.tensor_scalar(qm_s.bitcast(U32), cT_s.bitcast(U32), 0x7F800000, None, ALU.bitwise_and).then_inc(d_ce, 1)
                ve.wait_ge(d_ce, at(r.i, 1, 2))
                V.tensor_scalar(qm_s, qm_s, 2.0 ** -6, 1.5 * 2.0 ** 20, ALU.max, ALU.mult).then_inc(d_cm, 1)

            def lin_stats(r, t):
                row_stats(t, xr_s, stats1, x7, r.number("y", t // 2) + 1, d_st)

            def lin_mean_var(r):
                for t in range(TT):
                    mean_var(t, stats1, mv1, d_st, at(r.ahead_norm, TT, t + 1), d_mv)

            def x1q_rows(r, half):
                if half == 0:
                    wait_alone(ve, g_rs, at(r.ahead_norm, 1, 1))
                for t in (2 * half, 2 * half + 1):
                    V.tensor_scalar(x1q_s[:, t, :], xr_s[:, t, :], mv1[:, t, 0:1], rstd1[:, t:t + 1], ALU.subtract, ALU.mult,
                                    saturate=False).then_inc(d_xq, 1)

            def out_stats(r, t):
                row_stats(t, x1_s, stats, x7, r.number("wo", t) + 1, d_st)

            def out_mean_var(r):
                for t in range(TT):
                    mean_var(t, stats, mv, d_st, at(r.tail_norm, TT, t + 1), d_mv)

            def x2_rows(r, half):
                if half == 0:
                    ve.wait_ge(g_rs, at(r.tail_norm, 1, 1))
                for t in (2 * half, 2 * half + 1):
                    V.tensor_scalar(x1_s[:, t, :], x1_s[:, t, :], mv[:, t, 0:1], rstd[:, t:t + 1], ALU.subtract, ALU.mult)\
                     .then_inc(d_x2, 1)

            def x1_rows(r, half):
                if r.tail and half == 0:
                    wait_alone(ve, s_x2out, at(r.i, 16, 0))
                for t in (2 * half, 2 * half + 1):
                    V.tensor_scalar(x1_s[:, t, :], xr_s[:, t, :], mv1[:, t, 0:1], rstd1[:, t:t + 1], ALU.subtract, ALU.mult)\
                     .then_inc(d_x1, 1)

            def row_min(r, u):
                n = (unit(u)[1] + 1) * P
                ve.wait_ge(p_s, at(r.i, UNITS, u + 1))
                V.tensor_reduce(smin[:, u % 4:u % 4 + 1], PS[:, u % 4, 0:n], AX_X, ALU.min).then_inc(d_min, 1)

            def row_inv(r, u):
                ve.wait_ge(a_e, at(r.i, UNITS, u + 1))
                V.reciprocal(sinv[:, u % 4:u % 4 + 1], ssum[:, u % 4:u % 4 + 1]).then_inc(d_inv, 1)

            def z_rest(r, p):
                ve.wait_ge(a_z, at(r.i, PAIRS, p + 1))
                V.tensor_tensor(ZL[:, p % PAIRS, :], B6, ZH[:, p % PAIRS, :].bitcast(F32), ALU.subtract).then_inc(d_z, 1)

            def run(r):
                for u in range(UNITS):
                    p, t, e = unit(u)
                    if u + 2 < UNITS or r.ahead:
                        row_inv(r, u + 2)
                    for job, k in r.slot(u - 1):
                        if job not in ("K", "Q"):
                            read(r, job, k)
                    if u % (2 * TT) == 2 and (p >= 1 or r.tail):
                        z_rest(r, p - 1)
                    if u + 4 < UNITS or r.ahead:
                        row_min(r, u + 4)
                    if e == 1:
                        ve.wait_ge(p_t, at(r.i, UNITS, u + 1))
                        V.tensor_copy(PT[2 * (p % 2) + 1][:, 0:t + 1, t * P:(t + 1) * P],
                                      PS[:, 5, 0:(t + 1) * P].rearrange("p (a b) -> p a b", b=P)).then_inc(d_t, 1)
                    for job, k in r.slot(u - 1):
                        if job in ("K", "Q"):
                            read(r, job, k)
                    for job, k in r.slot(u - 2):
                        if job == "wo":
                            out_stats(r, k)
                        elif job == "q":
                            q_feature(r, k)
                        elif job == "y":
                            lin_stats(r, 2 * k)
                            lin_stats(r, 2 * k + 1)
                    for job, k in r.slot(u - 3):
                        if job == "kv":
                            k_feature(r, k)
                    if r.tail and u == 11:
                        out_mean_var(r)
                    if r.tail and u in (13, 14):
                        x2_rows(r, u - 13)
                    if r.ahead and u == 33:
                        context_magic(r)
                    if r.ahead and u == 42:
                        lin_mean_var(r)
                    if r.ahead and u in (45, 46):
                        x1q_rows(r, u - 45)
                    if u in (22, 23):
                        x1_rows(r, u - 22)

            ve.wait_ge(s_const, 16)
            V.tensor_copy(ident_b[:, :], ident)
            V.tensor_copy(causal_b[:, :], cst[:, C_CAUSAL:C_CAUSAL + P]).then_inc(s_cb, 1)
            V.memset(ones_b[:, :], 1.0).then_inc(s_cb, 1)
            V.tensor_copy(tri_b[:, :], cst[:, C_TRI:C_TRI + P]).then_inc(s_cb, 1)
            raw_bits, magic = stage_w[0], stage_w[1]

            def round_weights(n):
                _, wt, k, c = raw_w[n]
                q = (n % 4) * 512
                m = (n % 2) * 1024
                ve.wait_ge(s_wraw[n % 4], 16 * (n // 4 + 1))
                V.tensor_scalar(magic[:, m:m + 512].bitcast(U32), raw_bits[:, q:q + 512].bitcast(U32), 0x7F800000, None,
                                ALU.bitwise_and).then_inc(s_wexp, 1)
                ve.wait_ge(s_wexp, n + 1)
                V.tensor_scalar(magic[:, m + 512:m + 1024], magic[:, m:m + 512], 2.0 ** -6, 1.5 * 2.0 ** 20, ALU.max, ALU.mult)\
                 .then_inc(s_wmag, 1)
                ve.wait_ge(s_wmag, n + 1)
                V.tensor_tensor(magic[:, m:m + 512], raw_bits[:, q:q + 512], magic[:, m + 512:m + 1024], ALU.add).then_inc(s_wadd, 1)
                ve.wait_ge(s_wadd, n + 1)
                V.tensor_tensor(wt[:, k, c * 512:(c + 1) * 512], magic[:, m:m + 512], magic[:, m + 512:m + 1024], ALU.subtract)\
                 .then_inc(s_wcvt, 1)

            ve.wait_ge(s_wlin, 16 * 6)
            r = prologue()
            context_magic(r)
            round_weights(0)
            for n, (_, job, k) in enumerate(r.table):
                if (job, k) == ("K", 0):
                    ve.wait_ge(s_wo, 16 * 6)
                    ve.wait_ge(s_wOH, 1)
                    V.tensor_tensor(wOL, wO_raw, wOH.bitcast(F32), ALU.subtract).then_inc(s_wOL, 1)
                elif (job, k) == ("Q", 0):
                    ve.wait_ge(s_nbQ, 1)
                read(r, job, k)
                if job == "q":
                    q_feature(r, k)
                if job == "kv" and k > 0:
                    k_feature(r, k - 1)
                    if k == TT - 1:
                        k_feature(r, k)
                if job == "y":
                    lin_stats(r, 2 * k)
                    lin_stats(r, 2 * k + 1)
                    if k == 1:
                        lin_mean_var(r)
                        x1q_rows(r, 0)
                        x1q_rows(r, 1)
                if n + 1 < N_WRAW:
                    round_weights(n + 1)
                if n + 1 == 2 * N_WRAW // 3:
                    ve.wait_ge(s_wcvt, n + 1)
                    V.tensor_scalar(wQ, wQ, -1.0 / HD ** 0.5, None, ALU.mult).then_inc(s_wscaled, 1)
            for u in range(4):
                row_min(r, UNITS + u)
            for u in range(2):
                row_inv(r, UNITS + u)
            run(first_round())
            with ve.Fori(1, NB - 1) as i:
                run(middle_round(i))
            run(last_round())
            step = [0]

            def done(ins):
                ins.then_inc(r_d, 1)
                step[0] += 1
                ve.wait_ge(r_d, step[0])

            def best_two(a, b):
                for t in range(a, b):
                    last = V.max(top[:, t, :], logits[:, t, :])
                done(last)
                for t in range(a, b):
                    last = V.max_index(topi[:, t, :], top[:, t, :], logits[:, t, :])
                done(last)

            r = epilogue()
            z_rest(r, -1)
            for _, job, k in r.table:
                read(r, job, k)
                if job == "wo":
                    out_stats(r, k)
                    if k < TT - 1:
                        n = (ROWTILES - TT) // (TT - 1) + 1
                        best_two(k * n, min((k + 1) * n, ROWTILES - TT))
                    if k == TT - 1:
                        out_mean_var(r)
                        x2_rows(r, 0)
                        x2_rows(r, 1)

            ve.wait_ge(x7, PRODUCTS)
            best_two(ROWTILES - TT, ROWTILES)
            done(V.tensor_copy(choice, topi[:, :, 0:TOPK].rearrange("p t j -> p j t")))
            iota_e = cst[:, C_IOTA:C_IOTA + NE].unsqueeze(1).to_broadcast([P, ROWTILES, NE])
            hot = [onehot[:, j, :].rearrange("p (t e) -> p t e", e=NE) for j in range(TOPK)]
            for j in range(TOPK):
                done(V.tensor_tensor(hot[j], iota_e, choice[:, j, :].unsqueeze(2).to_broadcast([P, ROWTILES, NE]), ALU.is_equal))
            V.tensor_tensor(both_b, onehot[:, 0, :], onehot[:, 1, :], ALU.add).then_inc(r_hot, 1)
            ve.wait_ge(r_pre, 1)
            done(V.tensor_copy(run_a, PS[:, 1, 0:ROWTILES * NE].rearrange("p (t e) -> p t e", e=NE)))
            a, b = run_a, run_b
            d = 1
            while d < ROWTILES:
                V.tensor_copy(b[:, 0:d, :], a[:, 0:d, :])
                done(V.tensor_tensor(b[:, d:, :], a[:, d:, :], a[:, 0:ROWTILES - d, :], ALU.add))
                a, b = b, a
                d *= 2
            done(V.tensor_scalar(etiles, a[:, ROWTILES - 1, :], float(P - 1), None, ALU.add))
            done(V.tensor_copy(etiles_i, etiles))
            done(V.tensor_scalar(etiles_i, etiles_i, 7, None, ALU.logical_shift_right))
            done(V.tensor_copy(etiles, etiles_i))
            done(V.tensor_copy(cum_a, etiles))
            ca, cb = cum_a, cum_b
            d = 1
            while d < NE:
                V.tensor_copy(cb[:, 0:d], ca[:, 0:d])
                done(V.tensor_tensor(cb[:, d:], ca[:, d:], ca[:, 0:NE - d], ALU.add))
                ca, cb = cb, ca
                d *= 2
            done(V.tensor_tensor(past, cst[:, C_IOTA:C_IOTA + LIST_COLS].unsqueeze(2).to_broadcast([P, LIST_COLS, NE]),
                                 ca.unsqueeze(1).to_broadcast([P, LIST_COLS, NE]), ALU.is_ge))
            done(V.tensor_reduce(expert_f, past, AX_X, ALU.add))
            done(V.tensor_scalar(expert_f, expert_f, float(NE - 1), None, ALU.min))
            done(V.tensor_copy(expert[:, :], expert_f))
            done(V.tensor_tensor(cb, ca, etiles, ALU.subtract))
            done(V.tensor_scalar(cb, cb, float(P), None, ALU.mult))
            done(V.tensor_tensor(before, a, PS[:, 1, 0:ROWTILES * NE].rearrange("p (t e) -> p t e", e=NE), ALU.subtract))
            done(V.tensor_tensor(before, before, PS[:, 0, 0:ROWTILES * NE].rearrange("p (t e) -> p t e", e=NE), ALU.add))
            done(V.tensor_tensor(before, before, cb.unsqueeze(1).to_broadcast([P, ROWTILES, NE]), ALU.add))
            for j in range(TOPK):
                done(V.tensor_tensor(hot[j], hot[j], before, ALU.mult))
                done(V.tensor_reduce(slot[:, j, :], hot[j], AX_X, ALU.add))
            flat = slot.rearrange("p j t -> p (j t)")
            done(V.tensor_copy(slot_i, flat))
            done(V.tensor_scalar(tile_i, slot_i, 7, None, ALU.logical_shift_right))
            done(V.tensor_scalar(lane_i, slot_i, P - 1, None, ALU.bitwise_and))
            done(V.tensor_copy(tile_f, tile_i))
            done(V.tensor_copy(lane_f, lane_i))
            for c in range(ROWTILES * TOPK // HOT):
                cols = slice(c * HOT, (c + 1) * HOT)
                if c >= 2:
                    ve.wait_ge(r_list, c - 1)
                V.tensor_tensor(tile_hot[:, c % 2], cst[:, C_IOTA:C_IOTA + LIST_COLS].unsqueeze(1).to_broadcast([P, HOT, LIST_COLS]),
                                tile_f[:, cols].unsqueeze(2).to_broadcast([P, HOT, LIST_COLS]), ALU.is_equal).then_inc(r_tile, 1)
                V.tensor_tensor(lane_hot[:, c % 2], cst[:, C_IOTA:C_IOTA + P].unsqueeze(1).to_broadcast([P, HOT, P]),
                                lane_f[:, cols].unsqueeze(2).to_broadcast([P, HOT, P]), ALU.is_equal).then_inc(r_lane, 1)
            V.tensor_tensor(choice[:, 0, :], top[:, :, 1], top[:, :, 0], ALU.subtract).then_inc(r_gap, 1)
            ve.wait_ge(r_e, 1)
            done(V.tensor_scalar(gates[:, 0, :], gates[:, 1, :], 1.0, None, ALU.add))
            done(V.reciprocal(slot[:, 0, :], gates[:, 0, :]))
            done(V.tensor_copy(gates[:, 0, :], slot[:, 0, :]))
            done(V.tensor_tensor(slot[:, 1, :], gates[:, 1, :], slot[:, 0, :], ALU.mult))
            done(V.tensor_copy(gates[:, 1, :], slot[:, 1, :]))
            ve.wait_ge(r_list, ROWTILES * TOPK // HOT)
            done(V.tensor_copy(hi_s, PS[:, 2, LIST_COLS:2 * LIST_COLS]))
            done(V.scalar_tensor_tensor(code, hi_s, float(TOPK * P), PS[:, 2, 0:LIST_COLS], ALU.mult, ALU.add))
            done(V.tensor_scalar(empty, code, 0.0, cst[:, C_LANE + 1:C_LANE + 2], ALU.is_equal, ALU.mult))
            done(V.tensor_scalar(hi_s, code, -1.0, 0.0, ALU.add, ALU.max))
            done(V.tensor_tensor(empty, empty, code, ALU.add))
            done(V.tensor_scalar(empty, empty, -1.0, None, ALU.add))
            done(V.tensor_copy(scatter_l[:, :], empty))
            done(V.tensor_copy(code_i, hi_s))
            done(V.tensor_scalar(gather_l[:, :].bitcast(I32), code_i, 1, None, ALU.logical_shift_right))
            V.tensor_copy(hi_s, expert_f).then_inc(r_tab, 1)

            def expert_of(s):
                return ve.value_load(expert[0:1, ds(s, 1)], min_val=0, max_val=NE - 1)

            def tokensT(s, nth, h):
                ve.wait_ge(m_xt, at(s, 1, 1))
                V.tensor_copy(xgT[:, h, :], PS[:, 0, 0:DIM]).then_inc(m_xs, 1)

            def gate_bias(s, nth, h):
                e = expert_of(s)
                ve.wait_ge(m_g, at(s, 1, 1))
                V.tensor_tensor(g_s[:, h, :], PS[:, 1 + h, :], b1_b[:, ds(e * FF, FF)], ALU.add).then_inc(m_gb, 1)

            def hidden_rest(s, nth, h):
                ve.wait_ge(m_hs, at(s, 1, 1))
                V.tensor_tensor(hTL[:, :], PS[:, 5, :], hTH[:, :].bitcast(F32), ALU.subtract).then_inc(m_hl, 1)

            def gated(s, nth, h):
                e = expert_of(s)
                ve.wait_ge(m_v, at(s, 1, 1))
                V.tensor_tensor(v_s[:, h, :], PS[:, 3 + h, :], b2_b[:, ds(e * FF, FF)], ALU.add).then_inc(m_vb, 1)
                ve.wait_ge(m_si_, at(s, 1, 1))
                ve.wait_ge(m_vb, at(s, 1, 1))
                V.tensor_tensor(h_s[:, h, :], silu_s[:, h, :], v_s[:, h, :], ALU.mult).then_inc(m_h, 1)

            def rows_out(s, nth, h, wait=True):
                e = expert_of(s)
                ve.wait_ge(m_o, at(s, 1, 1))
                if wait:
                    ve.wait_ge(m_out[h], nth * 16)
                V.tensor_tensor(yo[:, h, :], PS[:, 6, 0:DIM], b3_b[:, ds(e * DIM, DIM)], ALU.add).then_inc(m_yo, 1)

            ve.wait_ge(s_w12, 16 * 9)
            tokensT(*tile(0, 0))
            gate_bias(*tile(0, 0))
            tokensT(*tile(0, 1))
            gated(*tile(0, 0))
            for k in (1, 2):
                gate_bias(*tile(0, k))
                hidden_rest(*tile(0, k - 1))
                tokensT(*tile(0, k + 1))
                gated(*tile(0, k))
                rows_out(*tile(0, k - 1), wait=False)
            with ve.Fori(1, (MOE_TILES - 1) // 2) as u:
                for k in (1, 2):
                    gate_bias(*tile(u, k))
                    hidden_rest(*tile(u, k - 1))
                    tokensT(*tile(u, k + 1))
                    gated(*tile(u, k))
                    rows_out(*tile(u, k - 1))
            hidden_rest(*tile(0, MOE_TILES - 1))
            rows_out(*tile(0, MOE_TILES - 1))

            def mix(i):
                h = i % DEPTH
                ve.wait_ge(c_sum, i + 1)
                for t in range(GT):
                    V.scalar_tensor_tensor(zz[:, h, t, :], yy[:, h, t, DIM:2 * DIM], gates[:, 1, i * GT + t:i * GT + t + 1],
                                           zz[:, h, t, :], ALU.mult, ALU.add).then_inc(c_pre, 1)
                for t in range(GT):
                    row_stats(t, zz[:, h], stats4[:, h], c_pre, i * GT + t + 1, c_st)
                for t in range(GT):
                    mean_var(t, stats4[:, h], mv4[:, h], c_st, i * GT + t + 1, c_mv)

            mix(0)
            for i in range(GROUPS):
                h = i % DEPTH
                if i + 1 < GROUPS:
                    mix(i + 1)
                ve.wait_ge(c_rs, i + 1)
                if i >= 2:
                    ve.wait_ge(s_out[i % 2], 16 * (i // 2))
                for t in range(GT):
                    V.tensor_scalar(oo[:, i % 2, t, :], zz[:, h, t, :], mv4[:, h, t, 0:1], rstd4[:, h, t:t + 1], ALU.subtract, ALU.mult)\
                     .then_inc(c_o, 1)

        @block.gpsimd
        def _(po):
            G = nc.gpsimd
            half = cst[:, C_LANE + 4:C_LANE + 8]

            def rsqrt(out_, mvt, ve_sem, n, done):
                G.tensor_scalar(out_, mvt[:, :, 1], EPS, 1.0, ALU.add, ALU.mult).then_inc(ve_sem, 1)
                wait_alone(po, ve_sem, n)
                G.tensor_tensor(out_, out_, half[:, 0:mvt.shape[1]], ALU.pow).then_inc(done, 1)

            po.wait_ge(s_const, 16)
            po.wait_ge(s_wlin, 16 * 6)

            def signal(last, piece, semaphore):
                if piece == TT - 1:
                    last.then_inc(semaphore, 1)

            def quarter(v, n):
                half = SEQ * DC // TT
                return v[:, n * half // SEQ, n * half % SEQ:n * half % SEQ + half]

            def x_plus_bias(r, n):
                if n == 0:
                    po.wait_ge(s_xr, at(r.i, 16, 32))
                signal(G.tensor_tensor(xr_s[:, n, :], xr_s[:, n, :], bp_b, ALU.add), n, g_res)

            def context_add(r, n):
                if n == 0:
                    po.wait_ge(d_cm, at(r.i, 1, 2))
                signal(G.tensor_tensor(quarter(cT_s, n), quarter(cT_s, n), quarter(qm_s, n), ALU.add), n, g_ca)

            def context_subtract(r, n):
                if n == 0:
                    po.wait_ge(g_ca, at(r.i, 1, 2))
                    if r.own:
                        po.wait_ge(p7, r.number("V", PAIRS - 1) + 1)
                signal(G.tensor_tensor(quarter(cq_s, n), quarter(cT_s, n), quarter(qm_s, n), ALU.subtract), n, g_cq)

            def x1_plus_bias(r, n):
                if n == 0:
                    if not r.tail:
                        po.wait_ge(s_wo, 16 * 6)
                    po.wait_ge(d_x1, at(r.i, TT, TT))
                signal(G.tensor_tensor(x1_s[:, n, :], x1_s[:, n, :], bO_b, ALU.add), n, g_res2)

            def lin_rstd(r):
                wait_alone(po, d_mv, at(r.ahead_norm, TT, TT))
                rsqrt(rstd1, mv1, g_ve, at(r.ahead_norm, 1, 1), g_rs)

            def out_rstd(r):
                wait_alone(po, d_mv, at(r.tail_norm, TT, TT))
                rsqrt(rstd, mv, g_ve, at(r.tail_norm, 1, 1), g_rs)

            def run(r):
                for u in range(UNITS):
                    n = (unit(u)[1] + 1) * P
                    wait_alone(po, d_inv, at(r.i, UNITS, u + 1))
                    G.tensor_scalar(pnorm[:, u % 4, 0:n], prob[:, u % 4, 0:n], sinv[:, u % 4:u % 4 + 1], 1.0,
                                    ALU.mult, ALU.mult).then_inc(g_n, 1)
                    if r.tail and u == 12:
                        out_rstd(r)
                    if u in range(24, 28):
                        x1_plus_bias(r, u - 24)
                    if r.ahead and u in range(34, 38):
                        x_plus_bias(r, u - 34)
                    if r.ahead and u in range(38, 42):
                        context_add(r, u - 38)
                    if r.ahead and u == 43:
                        lin_rstd(r)
                    if r.ahead and u in (50, 51):
                        context_subtract(r, 2 * u - 100)
                        context_subtract(r, 2 * u - 99)

            for n in range(TT):
                x_plus_bias(prologue(), n)
            for n in range(TT):
                context_add(prologue(), n)
            lin_rstd(prologue())
            for n in range(TT):
                context_subtract(prologue(), n)
            run(first_round())
            with po.Fori(1, NB - 1) as i:
                run(middle_round(i))
            run(last_round())
            out_rstd(epilogue())
            for e in range(NE):
                part = slice(e * FC * DIM, (e + 1) * FC * DIM)
                po.wait_ge(r_w3h, e + 1)
                G.tensor_tensor(w3L[:, part], w3_raw[:, part], w3H[:, part].bitcast(F32), ALU.subtract).then_inc(r_w3l, 1)

            def gather(s, nth, h):
                G.tensor_copy(g_idx[:, h:h + 1], gather_l[:, ds(s, 1)]).then_inc(m_gi, 1)
                wait_alone(po, m_gi, at(s, 1, 1))
                G.indirect_dma_start(out=xg[:, h, :], out_offset=None, in_=x2_d,
                                     in_offset=bass.IndirectOffsetOnAxis(ap=g_idx[:, h:h + 1], axis=0)).then_inc(m_in[h], 16)

            def scatter(s, nth, h, first=False, second=False):
                if not (first or second):
                    po.wait_ge(m_out[h], nth * 16)
                G.tensor_copy(s_idx[:, h:h + 1], scatter_l[:, ds(s, 1)]).then_inc(m_si, 1)
                po.wait_ge(m_si, at(s, 1, 1))
                if not first:
                    po.wait_ge(m_out[1 - h], (nth + h) * 16)
                wait_alone(po, m_yo, at(s, 1, 1))
                G.indirect_dma_start(out=y_d, out_offset=bass.IndirectOffsetOnAxis(ap=s_idx[:, h:h + 1], axis=0),
                                     in_=yo[:, h, :], in_offset=None).then_inc(m_out[h], 16)

            def transposed(s, nth, h):
                po.wait_ge(m_xt, at(s, 1, 1))

            for c in range(ROWTILES * TOPK // HOT):
                first = C_CODE + c * HOT % ROWTILES
                if c >= 2:
                    po.wait_ge(r_list, c - 1)
                po.wait_ge(r_tile, c + 1)
                G.tensor_tensor(code_hot[:, c % 2, :, LIST_COLS:], tile_hot[:, c % 2],
                                cst[:, first:first + HOT].unsqueeze(2).to_broadcast([P, HOT, LIST_COLS]),
                                ALU.mult).then_inc(r_high, 1)

            po.wait_ge(r_tab, 1)
            po.wait_ge(s_x2out, 16 * NB)
            gather(*tile(0, 0))
            gather(*tile(0, 1))
            transposed(*tile(0, 0))
            gather(*tile(0, 2))
            for k in (1, 2):
                transposed(*tile(0, k))
                gather(*tile(0, k + 2))
                scatter(*tile(0, k - 1), first=k == 1, second=k == 2)
            with po.Fori(1, (MOE_TILES - 1) // 2) as u:
                for k in (1, 2):
                    transposed(*tile(u, k))
                    gather(*tile(u, k + 2))
                    scatter(*tile(u, k - 1))
            scatter(*tile(0, MOE_TILES - 1))
            po.wait_ge(m_in[0], 16 * ((LIST_COLS + 1) // 2))
            po.wait_ge(m_in[1], 16 * (LIST_COLS // 2))

            def add_x2(i):
                po.wait_ge(c_mix, GT * (i + 1))
                G.tensor_tensor(zz[:, i % DEPTH], zz[:, i % DEPTH], xx[:, i % DEPTH], ALU.add).then_inc(c_sum, 1)

            add_x2(0)
            add_x2(1)
            for i in range(GROUPS):
                if i + 2 < GROUPS:
                    add_x2(i + 2)
                po.wait_ge(c_mv, GT * (i + 1))
                rsqrt(rstd4[:, i % DEPTH], mv4[:, i % DEPTH], c_ve, i + 1, c_rs)


_IN = ["x", "xT", "cT", "Wq", "Wk", "Wv", "Wp", "bq", "bk", "bv", "bp", "WQ", "WK", "WV", "WO", "bQ", "bK", "bV", "bO",
       "WgT", "W1T", "b1", "W2T", "b2", "W3T", "b3", "consts"]


def kernel(x, ctx_1024, L0_attn_Wq, L0_attn_bq, L0_attn_Wk, L0_attn_bk, L0_attn_Wv, L0_attn_bv, L0_attn_Wp, L0_attn_bp,
           L0_xattn_W_Q, L0_xattn_W_K, L0_xattn_W_V, L0_xattn_W_O, L0_xattn_b_Q, L0_xattn_b_K, L0_xattn_b_V, L0_xattn_b_O,
           L0_ffn_Wg, L0_ffn_W1, L0_ffn_b1, L0_ffn_W2, L0_ffn_b2, L0_ffn_W3, L0_ffn_b3):
    import concourse.bacc as bacc
    from concourse.bass_utils import run_bass_kernel_spmd

    x = np.asarray(x)
    ctx_1024 = np.asarray(ctx_1024)

    def cols(w):
        return np.asarray(w).transpose(1, 0, 2).reshape(DIM, INNER)

    arrays = dict(
        x=x.reshape(TOK, DIM), xT=x.reshape(TOK, DIM).T, cT=ctx_1024.reshape(TOK, DIM).T,
        Wq=L0_attn_Wq, Wk=L0_attn_Wk, Wv=L0_attn_Wv, Wp=L0_attn_Wp, bq=L0_attn_bq, bk=L0_attn_bk, bv=L0_attn_bv, bp=L0_attn_bp,
        WQ=cols(L0_xattn_W_Q), WK=cols(L0_xattn_W_K), WV=cols(L0_xattn_W_V), WO=np.asarray(L0_xattn_W_O).reshape(INNER, DIM),
        bQ=np.asarray(L0_xattn_b_Q).reshape(INNER), bK=np.asarray(L0_xattn_b_K).reshape(INNER),
        bV=np.asarray(L0_xattn_b_V).reshape(INNER), bO=L0_xattn_b_O,
        WgT=np.asarray(L0_ffn_Wg).T, W1T=np.asarray(L0_ffn_W1).transpose(0, 2, 1), b1=np.asarray(L0_ffn_b1).reshape(-1),
        W2T=np.asarray(L0_ffn_W2).transpose(0, 2, 1), b2=np.asarray(L0_ffn_b2).reshape(-1),
        W3T=np.asarray(L0_ffn_W3).transpose(0, 2, 1), b3=np.asarray(L0_ffn_b3).reshape(-1), consts=constants())
    arrays = {n: np.ascontiguousarray(arrays[n]) for n in _IN}
    nc = bacc.Bacc("TRN2", target_bir_lowering=False, num_devices=1)
    args = {n: nc.dram_tensor(f"in_{n}", a.shape, mybir.dt.from_np(a.dtype), kind="ExternalInput").ap() for n, a in arrays.items()}
    out = nc.dram_tensor("out_rows", (TOK, DIM), F32, kind="ExternalOutput").ap()
    decoder_kernel(nc, out=out, **args)
    r = run_bass_kernel_spmd(nc, [{f"in_{n}": a for n, a in arrays.items()}], core_ids=[0])
    return r.results[0]["out_rows"].reshape(x.shape)
```
